# Optimizing a Trainium2 kernel written in Bass

```python
import numpy as np
import jax
import jax.numpy as jnp

def _softmax(x, axis=-1):
    return jax.nn.softmax(x, axis=axis)

def _gelu(x):
    return jax.nn.gelu(x, approximate=True)

def _silu(x):
    return jax.nn.silu(x)

def _sigmoid(x):
    return jax.nn.sigmoid(x)

def _layernorm(x, axis=-1, eps=1e-05):
    m = jnp.mean(x, axis=axis, keepdims=True)
    v = jnp.var(x, axis=axis, keepdims=True)
    return (x - m) / jnp.sqrt(v + eps)

def _scatter_add(tgt, idx, src, axis=0):
    return tgt.at[idx].add(src)

def _segment_sum(src, seg, n):
    return jax.ops.segment_sum(src, seg, n)
kernel_name = 'mk_flamingo_gated_d2_seqx_r8_7da77b'

def setup_inputs(seed: int=0):
    np.random.seed(seed)
    _w = jnp.asarray

    def _rec_inputs():
        import jax
        import jax.numpy as jnp
        _rk = jax.random.key(seed)
        x = 7.22e-05 + 1 * jax.random.normal(jax.random.fold_in(_rk, 1), (32, 64, 256), jnp.float32)
        _lenS = 64 - jax.random.randint(jax.random.fold_in(_rk, 7), (32,), 0, max(1, 64 // 4) + 1, jnp.int32)
        _lenS2 = 64 - jax.random.randint(jax.random.fold_in(_rk, 8), (32,), 0, max(1, 64 // 4) + 1, jnp.int32)
        _ctx_512P = jax.random.normal(jax.random.fold_in(_rk, 11), (32, 16, 64), jnp.float32)
        _ctx_512c = jax.random.dirichlet(jax.random.fold_in(_rk, 511), 0.3 * jnp.ones((16,), jnp.float32), (32, 64))
        _ctx_512t = jnp.einsum('bsk,bkd->bsd', _ctx_512c, _ctx_512P)
        _ctx_512t = _ctx_512t * jax.lax.rsqrt(jnp.mean(jnp.square(_ctx_512t)) + 1e-12) * 0.953939
        ctx_512 = -0.000514642 + 1.00011 * (_ctx_512t + 0.3 * jax.random.normal(jax.random.fold_in(_rk, 611), (32, 64, 64), jnp.float32))
        _g = jax.random.normal(jax.random.fold_in(_rk, 9001), (2, 2), jnp.float32)
        _g = jnp.sign(_g) * jnp.maximum(jnp.abs(_g), 1.0) + (_g == 0) * 1.0
        g_xattn = _g[0]
        g_ffn = _g[1]
        return (x, ctx_512, g_xattn, g_ffn)
    x, ctx_512, g_xattn, g_ffn = _rec_inputs()

    def _L0_xattn_setup():
        import jax, jax.numpy as jnp
        import numpy as np
        B, S, E = (2, 256, 256)
        QH, KVH = (32, 8)
        D = E // QH
        G = QH // KVH
        DROPOUT = 1.0
        key = jax.random.key(seed)
        k1, k2, k3 = jax.random.split(key, 3)
        q = jax.random.normal(k1, (B, S, E), dtype=jnp.float32)
        k = jax.random.normal(k2, (B, S, E // G), dtype=jnp.float32)
        v = jax.random.normal(k3, (B, S, E // G), dtype=jnp.float32)
        return {'q': q, 'k': k, 'v': v}
    _L0_xattn_all = _L0_xattn_setup()
    _L0_xattn_in = {k: v for k, v in _L0_xattn_all.items() if k in ()}
    del _L0_xattn_all

    def _L0_ffn_setup():
        import jax, jax.numpy as jnp
        import numpy as np
        D_MODEL = 256
        D_EXPERT = 1024
        EPS = 1e-08

        def ternary_quant(w):
            scale = jnp.mean(jnp.abs(w)) + EPS
            q = jnp.clip(jnp.round(w / scale), -1.0, 1.0) * scale
            return w + jax.lax.stop_gradient(q - w)
        key = jax.random.key(seed)
        k_x, k_up, k_gate, k_down = jax.random.split(key, 4)
        std_in = 1.0 / np.sqrt(D_MODEL)
        std_exp = 1.0 / np.sqrt(D_EXPERT)
        return {'x': jax.random.normal(k_x, (4, 256, D_MODEL), dtype=jnp.float32), 'W_up': jax.random.normal(k_up, (D_EXPERT, D_MODEL), dtype=jnp.float32) * std_in, 'W_gate': jax.random.normal(k_gate, (D_EXPERT, D_MODEL), dtype=jnp.float32) * std_in, 'W_down': jax.random.normal(k_down, (D_MODEL, D_EXPERT), dtype=jnp.float32) * std_exp}
    _L0_ffn_all = _L0_ffn_setup()
    _L0_ffn_in = {k: v for k, v in _L0_ffn_all.items() if k in ('W_up', 'W_gate', 'W_down')}
    del _L0_ffn_all

    def _L1_xattn_setup():
        import jax, jax.numpy as jnp
        import numpy as np
        B, S, L = (2, 128, 128)
        DIM_Q, H, K, D_C, D_CQ, R = (256, 16, 128, 64, 192, 64)

        def _rope_tables(length, dim):
            inv = 1.0 / 10000.0 ** (jnp.arange(0, dim, 2, dtype=jnp.float32) / dim)
            f = jnp.arange(length, dtype=jnp.float32)[:, None] * inv[None, :]
            sin = jnp.repeat(jnp.sin(f), 2, axis=-1)
            cos = jnp.repeat(jnp.cos(f), 2, axis=-1)
            return (sin, cos)

        def _rotate_half(x):
            half = x.shape[-1] // 2
            return jnp.concatenate([-x[..., half:], x[..., :half]], axis=-1)

        def _apply_rope(x, sin, cos):
            return x * cos + _rotate_half(x) * sin
        key = jax.random.key(seed)
        ks = jax.random.split(key, 8)
        return {'hidden_q': jax.random.normal(ks[0], (B, S, DIM_Q), jnp.float32), 'kv_c': jax.random.normal(ks[1], (B, L, D_C), jnp.float32), 'Wq': jax.random.normal(ks[2], (H * K, DIM_Q), jnp.float32) / np.sqrt(DIM_Q).astype(np.float32), 'w_kc_q': jax.random.normal(ks[3], (H, K, D_CQ), jnp.float32) / np.sqrt(K).astype(np.float32), 'w_kc_kv': jax.random.normal(ks[4], (H, K, D_C), jnp.float32) / np.sqrt(K).astype(np.float32), 'W_qr': jax.random.normal(ks[5], (H, D_CQ, R), jnp.float32) / np.float32(np.sqrt(D_CQ) * np.sqrt(R)), 'W_kr': jax.random.normal(ks[6], (H, D_C, R), jnp.float32) / np.sqrt(D_C).astype(np.float32), 'Wo': jax.random.normal(ks[7], (DIM_Q, H * K), jnp.float32) / np.sqrt(H * K).astype(np.float32)}
    _L1_xattn_all = _L1_xattn_setup()
    _L1_xattn_in = {k: v for k, v in _L1_xattn_all.items() if k in ('Wq', 'w_kc_q', 'w_kc_kv', 'W_qr', 'W_kr', 'Wo')}
    del _L1_xattn_all

    def _L1_ffn_setup():
        import jax, jax.numpy as jnp
        import numpy as np
        from jax import lax
        E = 64
        H = 256
        I = 88
        G = 8
        TOPK_GROUP = 4
        K = 8
        B, S = (2, 256)
        N = B * S
        CAP = 2 * N * K // E
        SCALE = 2.5

        def _route(x, router_weight, e_bias):
            logits = x.astype(jnp.float32) @ router_weight.astype(jnp.float32).T
            scores = jax.nn.sigmoid(logits)
            sc = scores + e_bias
            n = x.shape[0]
            group_scores = lax.top_k(sc.reshape(n, G, E // G), 2)[0].sum(-1)
            grp_idx = lax.top_k(group_scores, TOPK_GROUP)[1]
            group_mask = jnp.zeros((n, G), jnp.float32).at[jnp.arange(n)[:, None], grp_idx].set(1.0)
            score_mask = jnp.repeat(group_mask, E // G, axis=1)
            masked = jnp.where(score_mask > 0, sc, 0.0)
            topk_idx = lax.top_k(masked, K)[1]
            topk_w = jnp.take_along_axis(scores, topk_idx, axis=1)
            topk_w = topk_w / (topk_w.sum(-1, keepdims=True) + 1e-20)
            return (topk_idx, topk_w * SCALE)

        def _moe_experts(x, topk_idx, topk_w, w_gate, w_up, w_down):
            n = x.shape[0]
            flat_e = topk_idx.reshape(-1)
            rows = jnp.repeat(jnp.arange(n), K)
            oh = jax.nn.one_hot(flat_e, E, dtype=jnp.int32)
            pos = jnp.cumsum(oh, axis=0) - oh
            pos = jnp.take_along_axis(pos, flat_e[:, None], axis=1)[:, 0]
            valid = (pos < CAP).astype(x.dtype)
            p = jnp.minimum(pos, CAP - 1)
            buf = jnp.zeros((E, CAP, H), x.dtype).at[flat_e, p].add(x[rows] * valid[:, None])
            g = jnp.einsum('ech,ehi->eci', buf, w_gate)
            u = jnp.einsum('ech,ehi->eci', buf, w_up)
            y = jnp.einsum('eci,eih->ech', jax.nn.silu(g) * u, w_down)
            y_tok = y[flat_e, p] * (topk_w.reshape(-1) * valid)[:, None]
            return jnp.zeros((n, H), x.dtype).at[rows].add(y_tok)

        def _shared_mlp(x, sh_gate, sh_up, sh_down):
            return jax.nn.silu(x @ sh_gate) * (x @ sh_up) @ sh_down
        key = jax.random.key(seed)
        ks = jax.random.split(key, 9)
        f32 = jnp.float32
        return {'hidden_states': jax.random.normal(ks[0], (B, S, H), f32), 'router_weight': jax.random.normal(ks[1], (E, H), f32) * (2.0 / H) ** 0.5, 'e_bias': jnp.zeros((E,), f32), 'w_gate': jax.random.normal(ks[2], (E, H, I), f32) * (1.0 / H) ** 0.5, 'w_up': jax.random.normal(ks[3], (E, H, I), f32) * (1.0 / H) ** 0.5, 'w_down': jax.random.normal(ks[4], (E, I, H), f32) * (1.0 / I) ** 0.5, 'sh_gate': jax.random.normal(ks[5], (H, I), f32) * (1.0 / H) ** 0.5, 'sh_up': jax.random.normal(ks[6], (H, I), f32) * (1.0 / H) ** 0.5, 'sh_down': jax.random.normal(ks[7], (I, H), f32) * (1.0 / I) ** 0.5}
    _L1_ffn_all = _L1_ffn_setup()
    _L1_ffn_in = {k: v for k, v in _L1_ffn_all.items() if k in ('router_weight', 'e_bias', 'w_gate', 'w_up', 'w_down', 'sh_gate', 'sh_up', 'sh_down')}
    del _L1_ffn_all
    return {'x': x, 'ctx_512': ctx_512, 'g_xattn': g_xattn, 'g_ffn': g_ffn, 'L0_ffn_W_up': _L0_ffn_in['W_up'], 'L0_ffn_W_gate': _L0_ffn_in['W_gate'], 'L0_ffn_W_down': _L0_ffn_in['W_down'], 'L1_xattn_Wq': _L1_xattn_in['Wq'], 'L1_xattn_w_kc_q': _L1_xattn_in['w_kc_q'], 'L1_xattn_w_kc_kv': _L1_xattn_in['w_kc_kv'], 'L1_xattn_W_qr': _L1_xattn_in['W_qr'], 'L1_xattn_W_kr': _L1_xattn_in['W_kr'], 'L1_xattn_Wo': _L1_xattn_in['Wo'], 'L1_ffn_router_weight': _L1_ffn_in['router_weight'], 'L1_ffn_e_bias': _L1_ffn_in['e_bias'], 'L1_ffn_w_gate': _L1_ffn_in['w_gate'], 'L1_ffn_w_up': _L1_ffn_in['w_up'], 'L1_ffn_w_down': _L1_ffn_in['w_down'], 'L1_ffn_sh_gate': _L1_ffn_in['sh_gate'], 'L1_ffn_sh_up': _L1_ffn_in['sh_up'], 'L1_ffn_sh_down': _L1_ffn_in['sh_down']}

def reference(x, ctx_512, g_xattn, g_ffn, L0_ffn_W_up, L0_ffn_W_gate, L0_ffn_W_down, L1_xattn_Wq, L1_xattn_w_kc_q, L1_xattn_w_kc_kv, L1_xattn_W_qr, L1_xattn_W_kr, L1_xattn_Wo, L1_ffn_router_weight, L1_ffn_e_bias, L1_ffn_w_gate, L1_ffn_w_up, L1_ffn_w_down, L1_ffn_sh_gate, L1_ffn_sh_up, L1_ffn_sh_down):
    import jax
    import jax.numpy as jnp

    def _L0_xattn_ref(q, k, v):
        import jax, jax.numpy as jnp
        import numpy as np
        B, S, E = (2, 256, 256)
        QH, KVH = (32, 8)
        D = E // QH
        G = QH // KVH
        DROPOUT = 1.0
        b, s, _ = q.shape
        qh = q.reshape(b, s, KVH, G, D).transpose(0, 2, 3, 1, 4)
        kh = k.reshape(b, s, KVH, D).transpose(0, 2, 1, 3)
        vh = v.reshape(b, s, KVH, D).transpose(0, 2, 1, 3)
        scale = 1.0 / jnp.sqrt(jnp.float32(D))
        scores = jnp.einsum('bkgsd,bktd->bkgst', qh, kh) * scale
        attn = jax.nn.softmax(scores, axis=-1) / DROPOUT
        out = jnp.einsum('bkgst,bktd->bkgsd', attn, vh)
        return out.transpose(0, 3, 1, 2, 4).reshape(b, s, E)

    def _L0_ffn_ref(x, W_up, W_gate, W_down):
        import jax, jax.numpy as jnp
        import numpy as np
        D_MODEL = 256
        D_EXPERT = 1024
        EPS = 1e-08

        def ternary_quant(w):
            scale = jnp.mean(jnp.abs(w)) + EPS
            q = jnp.clip(jnp.round(w / scale), -1.0, 1.0) * scale
            return w + jax.lax.stop_gradient(q - w)
        wu = ternary_quant(W_up)
        wg = ternary_quant(W_gate)
        wd = ternary_quant(W_down)
        up = jnp.einsum('bsd,ed->bse', x, wu)
        gate = jnp.einsum('bsd,ed->bse', x, wg)
        hidden = jax.nn.silu(up) * gate
        return jnp.einsum('bse,de->bsd', hidden, wd)

    def _L1_xattn_ref(hidden_q, kv_c, Wq, w_kc_q, w_kc_kv, W_qr, W_kr, Wo):
        import jax, jax.numpy as jnp
        import numpy as np
        B, S, L = (2, 128, 128)
        DIM_Q, H, K, D_C, D_CQ, R = (256, 16, 128, 64, 192, 64)

        def _rope_tables(length, dim):
            inv = 1.0 / 10000.0 ** (jnp.arange(0, dim, 2, dtype=jnp.float32) / dim)
            f = jnp.arange(length, dtype=jnp.float32)[:, None] * inv[None, :]
            sin = jnp.repeat(jnp.sin(f), 2, axis=-1)
            cos = jnp.repeat(jnp.cos(f), 2, axis=-1)
            return (sin, cos)

        def _rotate_half(x):
            half = x.shape[-1] // 2
            return jnp.concatenate([-x[..., half:], x[..., :half]], axis=-1)

        def _apply_rope(x, sin, cos):
            return x * cos + _rotate_half(x) * sin
        Bv, Sv, _ = hidden_q.shape
        _, Lv, _ = kv_c.shape
        q_hk = (hidden_q @ Wq.T).reshape(Bv, Sv, H, K)
        q_big = jnp.einsum('bshk,hkq->bshq', q_hk, w_kc_q)
        sin_q, cos_q = _rope_tables(Sv, D_CQ)
        q_big = _apply_rope(q_big, sin_q[None, :, None, :], cos_q[None, :, None, :])
        sin_k, cos_k = _rope_tables(Lv, D_C)
        kv_r = _apply_rope(kv_c, sin_k[None], cos_k[None])
        q_r = jnp.einsum('bshq,hqr->bhsr', q_big, W_qr)
        k_r = jnp.einsum('bld,hdr->bhlr', kv_r, W_kr)
        scores = jnp.einsum('bhsr,bhlr->bhsl', q_r, k_r)
        attn = jax.nn.softmax(scores, axis=-1)
        ctx_c = jnp.einsum('bhsl,bld->bhsd', attn, kv_r)
        ctx_lat = jnp.einsum('bhsd,hkd->bhsk', ctx_c, w_kc_kv)
        ctx = ctx_lat.transpose(0, 2, 1, 3).reshape(Bv, Sv, H * K)
        return ctx @ Wo.T

    def _L1_ffn_ref(hidden_states, router_weight, e_bias, w_gate, w_up, w_down, sh_gate, sh_up, sh_down):
        import jax, jax.numpy as jnp
        import numpy as np
        from jax import lax
        E = 64
        H = 256
        I = 88
        G = 8
        TOPK_GROUP = 4
        K = 8
        B, S = (2, 256)
        N = B * S
        CAP = 2 * N * K // E
        SCALE = 2.5

        def _route(x, router_weight, e_bias):
            logits = x.astype(jnp.float32) @ router_weight.astype(jnp.float32).T
            scores = jax.nn.sigmoid(logits)
            sc = scores + e_bias
            n = x.shape[0]
            group_scores = lax.top_k(sc.reshape(n, G, E // G), 2)[0].sum(-1)
            grp_idx = lax.top_k(group_scores, TOPK_GROUP)[1]
            group_mask = jnp.zeros((n, G), jnp.float32).at[jnp.arange(n)[:, None], grp_idx].set(1.0)
            score_mask = jnp.repeat(group_mask, E // G, axis=1)
            masked = jnp.where(score_mask > 0, sc, 0.0)
            topk_idx = lax.top_k(masked, K)[1]
            topk_w = jnp.take_along_axis(scores, topk_idx, axis=1)
            topk_w = topk_w / (topk_w.sum(-1, keepdims=True) + 1e-20)
            return (topk_idx, topk_w * SCALE)

        def _moe_experts(x, topk_idx, topk_w, w_gate, w_up, w_down):
            n = x.shape[0]
            flat_e = topk_idx.reshape(-1)
            rows = jnp.repeat(jnp.arange(n), K)
            oh = jax.nn.one_hot(flat_e, E, dtype=jnp.int32)
            pos = jnp.cumsum(oh, axis=0) - oh
            pos = jnp.take_along_axis(pos, flat_e[:, None], axis=1)[:, 0]
            valid = (pos < CAP).astype(x.dtype)
            p = jnp.minimum(pos, CAP - 1)
            buf = jnp.zeros((E, CAP, H), x.dtype).at[flat_e, p].add(x[rows] * valid[:, None])
            g = jnp.einsum('ech,ehi->eci', buf, w_gate)
            u = jnp.einsum('ech,ehi->eci', buf, w_up)
            y = jnp.einsum('eci,eih->ech', jax.nn.silu(g) * u, w_down)
            y_tok = y[flat_e, p] * (topk_w.reshape(-1) * valid)[:, None]
            return jnp.zeros((n, H), x.dtype).at[rows].add(y_tok)

        def _shared_mlp(x, sh_gate, sh_up, sh_down):
            return jax.nn.silu(x @ sh_gate) * (x @ sh_up) @ sh_down
        orig_shape = hidden_states.shape
        x = hidden_states.reshape(-1, H)
        topk_idx, topk_w = _route(x, router_weight, e_bias)
        moe_out = _moe_experts(x, topk_idx, topk_w.astype(x.dtype), w_gate, w_up, w_down)
        out = moe_out + _shared_mlp(x, sh_gate, sh_up, sh_down)
        return out.reshape(orig_shape)
    x = x + jnp.tanh(g_xattn[0]) * _L0_xattn_ref(_layernorm(x, axis=-1), ctx_512, ctx_512)
    x = x + jnp.tanh(g_ffn[0]) * _L0_ffn_ref(_layernorm(x, axis=-1), L0_ffn_W_up, L0_ffn_W_gate, L0_ffn_W_down)
    x = x + jnp.tanh(g_xattn[1]) * _L1_xattn_ref(_layernorm(x, axis=-1), ctx_512, L1_xattn_Wq, L1_xattn_w_kc_q, L1_xattn_w_kc_kv, L1_xattn_W_qr, L1_xattn_W_kr, L1_xattn_Wo)
    x = x + jnp.tanh(g_ffn[1]) * _L1_ffn_ref(_layernorm(x, axis=-1), L1_ffn_router_weight, L1_ffn_e_bias, L1_ffn_w_gate, L1_ffn_w_up, L1_ffn_w_down, L1_ffn_sh_gate, L1_ffn_sh_up, L1_ffn_sh_down)
    return x

_drawn_inputs = setup_inputs


def setup_inputs(seed=0):
    import zlib

    import numpy as np

    out = dict(_drawn_inputs(seed))
    spreads = {'g_ffn': (-1.0, 0.2), 'L1_ffn_e_bias': (0.0, 0.1)}
    factors = {}
    for name, (base, spread) in spreads.items():
        noise = np.random.default_rng([zlib.crc32(name.encode()), seed]).standard_normal(out[name].shape)
        drawn = base * np.exp(spread * noise) if base else spread * noise
        out[name] = jnp.asarray(drawn.astype(out[name].dtype))
    for name, factor in factors.items():
        out[name] = (out[name] * factor).astype(out[name].dtype)
    return out
```

```python
import numpy as np

import concourse.bass as bass
from concourse import mybir
from contextlib import ExitStack

F32 = mybir.dt.float32
F16 = mybir.dt.float16
U32 = mybir.dt.uint32
ALU = mybir.AluOpType
ACT = mybir.ActivationFunctionType
AX = mybir.AxisListType

P = 128
B, S, D = 32, 64, 256
TOK = B * S
TILES = TOK // P
T = 64
DC = 64
EPS_LN = 1e-5
KVH, G, HD = 8, 4, 8
DE = 1024
ME = DE // P
CH = 512
CHUNKS = TOK // CH
QT = CH // P
XS = 2048.0
H1, HK, DCQ = 16, 128, 192
HP = H1 // 2
QR = 2 * DCQ // P
E, I1, NG, TOPG, TOPK, CAP = 64, 88, 8, 4, 8, 128
RSCALE = 2.5
NB = 8
NY = 4
LEAD = 5
XW = D + E
ROWS = TOK + CAP

C_ID, C_ONES, C_TRI, C_KM, C_K1, C_CQ, C_SQ, C_CK, C_SK, C_GT, C_TOK, C_EB, C_POS, C_PAD = np.cumsum(
    [0, 128, 128, 128, 8, 1024, 192, 192, 64, 64, 64, 16, 64, 128]).tolist()
C_ALL = C_PAD + 1


def constants():
    def rope(length, dim):
        inv = (np.float32(1.0) / np.float32(10000.0) ** (np.arange(0, dim, 2, dtype=np.float32) / np.float32(dim))).astype(np.float32)
        f = np.arange(length, dtype=np.float32)[:, None] * inv[None, :]
        return np.repeat(np.sin(f), 2, axis=-1).astype(np.float32), np.repeat(np.cos(f), 2, axis=-1).astype(np.float32)
    c = np.zeros((P, C_ALL), np.float32)
    p = np.arange(P)
    c[:, C_ID:C_ID + P] = np.eye(P)
    c[:, C_ONES:C_ONES + P] = 1.0
    c[:, C_TRI:C_TRI + P] = p[:, None] < p[None, :]
    c[0:64, C_KM:C_KM + 8] = (np.arange(64)[:, None] // 8) == np.arange(8)[None, :]
    ones = np.zeros((8, 2, 8, 64), np.float32)
    for j in range(8):
        ones[j, :, j, :] = 1.0
    c[64:72, C_K1:C_K1 + 1024] = ones.reshape(8, 1024)
    sin, cos = rope(S, DCQ)
    for r in range(QR):
        q = (r * P + p) % DCQ
        half = DCQ // 2
        c[:, C_CQ + r * 64:C_CQ + r * 64 + 64] = cos[:, q].T
        c[:, C_SQ + r * 64:C_SQ + r * 64 + 64] = np.where(q < half, sin[:, (q + half) % DCQ], -sin[:, (q - half) % DCQ]).T
    sin, cos = rope(T, DC)
    sin[:, :DC // 2] *= -1.0
    c[:, C_CK:C_CK + 64] = cos[p % 64]
    c[:, C_SK:C_SK + 64] = sin[p % 64]
    g = np.arange(NG)
    c[:, C_GT:C_GT + 64] = (g[None, :] < g[:, None]).astype(np.float32).reshape(1, 64)
    c[:, C_TOK:C_TOK + TILES] = p[:, None] + P * np.arange(TILES)[None, :] + 1.0
    c[:, C_EB:C_EB + E] = np.arange(1, E + 1)[None, :] * CAP
    c[:, C_POS:C_POS + CAP] = np.arange(CAP)[None, :]
    c[:, C_PAD] = TOK + p + 1.0
    return c


def wait(eng, sem, value):
    if not isinstance(value, int) or value > 0:
        eng.wait_ge(sem, value)


def over_tiles(eng, step):
    for t in (0, 1):
        step(t, t % 2)
    with eng.Fori(1, TILES // 2 - 1) as it:
        step(2 * it, 0)
        step(2 * it + 1, 1)
    for t in (TILES - 2, TILES - 1):
        step(t, t % 2)


def within(t, n=TILES):
    return not isinstance(t, int) or t < n


class Mem:

    def __init__(self, nc, ctx, stage):
        self.nc, self.ctx, self.stage = nc, ctx, stage

    def sb(self, name, shape, dt=F32):
        return self.ctx.enter_context(self.nc.sbuf_tensor(f"{self.stage}_{name}", shape, dt))

    def ps(self, name, shape, dt=F32):
        return self.ctx.enter_context(self.nc.psum_tensor(f"{self.stage}_{name}", shape, dt))

    def sem(self, name):
        return self.nc.alloc_semaphore(f"{self.stage}_{name}")


def program(nc, a, out, xg_dram, acc_dram):
    ctx = ExitStack()
    with ctx:
        g = Mem(nc, ctx, "g")
        cst = g.sb("cst", [P, C_ALL])
        x = g.sb("x", [P, TILES, D])
        gat = g.sb("gat", [P, 4])
        ln_mv = g.sb("ln_mv", [P, TILES, 2])
        ln_rs = g.sb("ln_rs", [P, TILES])
        ident = cst[:, C_ID:C_ID + P]
        with ExitStack() as layers:
            w = Mem(nc, layers, "w")
            ctxT = w.sb("ctxT", [64, TILES, P])
            ctxd = w.sb("ctxd", [P, B, DC])
            k_up = w.sb("k_up", [P, 2, DE], F16)
            k_gate = w.sb("k_gate", [P, 2, DE], F16)
            k_down = w.sb("k_down", [P, ME, D], F16)
            tern = w.sb("tern", [P, 3, 3])
            fsc = w.sb("fsc", [P, 4])
            Cw = w.sb("Cw", [P, 2, HP, 2 * DCQ])
            NBc = w.sb("NBc", [P, HP, QR, P])
            NBs = w.sb("NBs", [P, HP, QR, P])
            VT = w.sb("VT", [P, HP, D])
            kvr = w.sb("kvr", [P, B, DC])
            for phase in range(2):
                prep(nc, a, phase, cst, x, gat, ident, ctxT, ctxd, k_up, k_gate, k_down, tern, fsc, Cw, NBc, NBs, VT, kvr, ln_mv)
            inverse_std(nc, "i0", ln_mv, ln_rs)
            attention0(nc, cst, x, ln_mv, ln_rs, gat, ident, ctxT, ctxd)
            inverse_std(nc, "i1", ln_mv, ln_rs)
            ffn0(nc, x, ln_mv, ln_rs, ident, k_up, k_gate, k_down, fsc)
            inverse_std(nc, "i2", ln_mv, ln_rs)
            attention1(nc, cst, x, ln_mv, ln_rs, gat, ident, Cw, NBc, NBs, VT, kvr)
        inverse_std(nc, "i3", ln_mv, ln_rs)
        moe(nc, a, cst, x, ln_mv, ln_rs, gat, ident, out, xg_dram, acc_dram)


def prep(nc, a, phase, cst, x, gat, ident, ctxT, ctxd, k_up, k_gate, k_down, tern, fsc, Cw, NBc, NBs, VT, kvr, ln_mv):
    with ExitStack() as ctx:
        m = Mem(nc, ctx, f"p{phase}")
        if phase == 0:
            ctx_tok = m.sb("ctx_tok", [P, TILES, DC])
            w3 = [m.sb(n, [P, 2048]) for n in ("w_up", "w_gate", "w_down")]
            pos = m.sb("pos", [P, 2048], F16)
            q3 = [m.sb(n, [P, 2048], F16) for n in ("q_up", "q_gate", "q_down")]
            identh = m.sb("identh", [P, P], F16)
            rot = m.sb("rot", [P, B, DC])
            part = m.sb("part", [P, 3])
            stats = m.sb("stats", [P, TILES, 6])
            graw = m.sb("graw", [P, 4])
        else:
            wq = m.sb("wq", [P, H1, D])
            wcq = m.sb("wcq", [P, H1, DCQ])
            wck = m.sb("wck", [P, H1, DC])
            wqr = m.sb("wqr", [96, H1, 2, 64])
            wkr = m.sb("wkr", [64, H1, 64])
            wo = m.sb("wo", [P, 2, 2048])
            qrT = m.sb("qrT", [P, HP, 2 * DCQ])
            qrTs = m.sb("qrTs", [P, HP, 2 * DCQ])
            krT = m.sb("krT", [P, HP, P])
            woT = wq
        banks = [m.ps(f"bank{n}", [P, 512]) for n in range(8)]

        loaded = {n: m.sem(f"ld_{n}") for n in (("cst", "ctx", "ctxd", "w0", "w1", "w2", "g", "x") if phase == 0 else
                                                  ("wq", "wcq", "wck", "wqr", "wkr", "wo"))}
        done = m.sem("done")
        act_out = m.sem("act_out")
        dve_out = m.sem("dve_out")
        zeroed = m.sem("zeroed")
        if phase == 0:
            absum = m.sem("absum")
            quant = m.sem("quant")
            chain = m.sem("dve_chain")
            pchain = m.sem("pool_chain")
            gats = m.sem("gats")

        if phase == 0:
            jobs = [("ctx", n) for n in range(4)] + [("sum", 0), ("up", 0), ("up", 1), ("gate", 0), ("gate", 1), ("down", 0), ("down", 1)]
        else:
            jobs = [("qr", n) for n in range(HP)] + [("kr", 0)] + [("C", n) for n in range(H1)] + [("wo", n) for n in range(HP)]
            jobs += [("N", n) for n in range(HP)] + [("Ns", n) for n in range(HP)] + [("V", n) for n in range(HP)]
        at = {j: n for n, j in enumerate(jobs)}

        def copied_out(eng, n):
            wait(eng, act_out, n // 2 + 1)
            wait(eng, dve_out, (n + 1) // 2)

        def copy_out(copy, job, bank, sem):
            kind, n = job
            if kind == "ctx":
                copy(ctxT[:, 4 * n:4 * n + 4, :], bank[0:64, :]).then_inc(sem, 1)
            elif kind == "qr":
                for h in range(2):
                    rows = slice(64 * h, 64 * h + 64)
                    src = bank[0:64, 192 * h:192 * h + 192]
                    copy(qrT[rows, n, DCQ * h:DCQ * h + DCQ], src)
                    copy(qrTs[rows, n, DCQ * h:DCQ * h + 96], src[:, 96:192])
                    last = copy(qrTs[rows, n, DCQ * h + 96:DCQ * h + DCQ], src[:, 0:96])
                last.then_inc(sem, 1)
            elif kind == "kr":
                for h in range(2):
                    rows = slice(64 * h, 64 * h + 64)
                    last = copy(krT[rows, :, 64 * h:64 * h + 64], bank[rows, :].rearrange("p (n c) -> p n c", n=HP))
                last.then_inc(sem, 1)
            elif kind == "C":
                copy(Cw[:, :, n // 2, DCQ * (n % 2):DCQ * (n % 2) + DCQ],
                     bank[:, 0:2 * DCQ].rearrange("p (u q) -> p u q", u=2)).then_inc(sem, 1)
            elif kind == "wo":
                copy(woT[:, 2 * n:2 * n + 2, :], bank[:]).then_inc(sem, 1)
            elif kind in ("N", "Ns"):
                copy((NBc if kind == "N" else NBs)[:, n, :, :], bank[:, 0:QR * P]).then_inc(sem, 1)
            elif kind == "V":
                copy(VT[:, n, :], bank[:, 0:D]).then_inc(sem, 1)
            elif kind in ("up", "gate"):
                copy((k_up if kind == "up" else k_gate)[:, n, :], bank[:].bitcast(F16)).then_inc(sem, 1)
            elif kind == "down":
                copy(k_down[:, :, P * n:P * n + P], bank[:].bitcast(F16).rearrange("p (m i) -> p m i", m=ME)).then_inc(sem, 1)
            elif kind == "sum":
                copy(tern[:, :, 0], bank[:, 0:3]).then_inc(sem, 1)

        with nc.Block() as block:
            @block.sync
            def _(sp):
                def load(dst, src, name):
                    sp.dma_start(dst, src).then_inc(loaded[name], 16)
                if phase == 0:
                    load(cst[:], a["consts"], "cst")
                    load(ctx_tok[:], a["ctx_512"].rearrange("(n b) t d -> (b t) n d", b=2), "ctx")
                    for h in range(2):
                        load(ctxd[64 * h:64 * h + 64], a["ctx_512"].rearrange("b t d -> t b d"), "ctxd")
                    return
                load(wqr[:], a["L1_xattn_W_qr"].rearrange("h (u q) r -> q h u r", u=2), "wqr")
                load(wkr[:], a["L1_xattn_W_kr"].rearrange("h c r -> c h r"), "wkr")
                load(wq[:], a["L1_xattn_Wq"].rearrange("(h k) d -> k h d", h=H1), "wq")
                load(wcq[:], a["L1_xattn_w_kc_q"].rearrange("h k q -> k h q"), "wcq")
                load(wo[:], a["L1_xattn_Wo"].rearrange("(u i) k -> i u k", u=2), "wo")
                load(wck[:], a["L1_xattn_w_kc_kv"].rearrange("h k c -> k h c"), "wck")

            @block.scalar
            def _(act):
                if phase == 0:
                    for k, name in enumerate(("L0_ffn_W_up", "L0_ffn_W_gate", "L0_ffn_W_down")):
                        act.dma_start(w3[k][:], a[name].rearrange("(u p) d -> p u d", p=P)).then_inc(loaded[f"w{k}"], 16)
                    act.dma_start(graw[:, 0:2], a["g_xattn"].rearrange("(o g) -> o g", o=1).to_broadcast([P, 2])).then_inc(loaded["g"], 16)
                    act.dma_start(graw[:, 2:4], a["g_ffn"].rearrange("(o g) -> o g", o=1).to_broadcast([P, 2])).then_inc(loaded["g"], 16)
                    act.dma_start(x[:], a["x"].rearrange("b s d -> (b s) d").rearrange("(n p) d -> p n d", p=P)).then_inc(loaded["x"], 16)
                    act.wait_ge(loaded["g"], 32)
                    act.activation(gat[:], graw[:], ACT.Tanh).then_inc(gats, 1)
                act.wait_ge(zeroed, 1 if phase == 0 else 3)
                for n in range(0, len(jobs), 2):
                    act.wait_ge(done, n + 1)
                    copy_out(act.copy, jobs[n], banks[n % 8], act_out)

            @block.gpsimd
            def _(pool):
                if phase == 1:
                    for w in (qrT, qrTs, krT):
                        pool.memset(w[:], 0.0).then_inc(zeroed, 1)
                    return
                pool.wait_ge(loaded["cst"], 16)
                pool.wait_ge(loaded["ctxd"], 32)
                pool.tensor_copy(identh[:], ident).then_inc(zeroed, 1)
                half = DC // 2
                sin = cst[:, C_SK:C_SK + DC].unsqueeze(1)
                pool.tensor_tensor(rot[:, :, 0:half], ctxd[:, :, half:DC], sin[:, :, 0:half].to_broadcast([P, B, half]), ALU.mult)
                pool.tensor_tensor(rot[:, :, half:DC], ctxd[:, :, 0:half], sin[:, :, half:DC].to_broadcast([P, B, half]), ALU.mult)
                pool.tensor_tensor(kvr[:], ctxd[:], cst[:, C_CK:C_CK + DC].unsqueeze(1).to_broadcast([P, B, DC]), ALU.mult).then_inc(pchain, 1)
                pool.wait_ge(pchain, 1)
                pool.tensor_tensor(kvr[:], kvr[:], rot[:], ALU.add).then_inc(pchain, 1)
                pool.wait_ge(pchain, 2)
                pool.wait_ge(loaded["x"], 16)

            @block.vector
            def _(dve):
                n_chain = [0]

                def link(ins):
                    n_chain[0] += 1
                    ins.then_inc(chain, 1)
                    dve.wait_ge(chain, n_chain[0])

                if phase == 1:
                    dve.wait_ge(zeroed, 3)
                    for n in range(1, len(jobs), 2):
                        dve.wait_ge(done, n + 1)
                        copy_out(dve.tensor_copy, jobs[n], banks[n % 8], dve_out)
                    return
                for k in range(3):
                    dve.wait_ge(loaded[f"w{k}"], 16)
                    dve.tensor_reduce(part[:, k:k + 1], w3[k][:], AX.X, ALU.add, apply_absolute_value=True).then_inc(absum, 1)

                def quantise():
                    dve.wait_ge(act_out, at["sum", 0] // 2 + 1)
                    link(dve.tensor_scalar(tern[:, :, 0], tern[:, :, 0], 1.0 / (DE * D), 1e-8, ALU.mult, ALU.add))
                    dve.tensor_scalar(tern[:, :, 1], tern[:, :, 0], 0.5, None, ALU.mult)
                    link(dve.tensor_scalar(tern[:, :, 2], tern[:, :, 0], -0.5, None, ALU.mult))
                    for k in range(3):
                        wait(dve, quant, k)
                        link(dve.tensor_scalar(pos[:], w3[k][:], tern[:, k, 2:3], None, ALU.is_lt))
                        dve.scalar_tensor_tensor(q3[k][:], w3[k][:], tern[:, k, 1:2], pos[:], ALU.is_gt, ALU.subtract).then_inc(quant, 1)
                    dve.wait_ge(gats, 1)
                    dve.tensor_scalar(fsc[:, 0:1], tern[:, 0, 0:1], 1.0 / XS, None, ALU.mult)
                    link(dve.tensor_scalar(fsc[:, 3:4], tern[:, 0, 0:1], 4.0 * XS, None, ALU.mult))
                    link(dve.reciprocal(fsc[:, 1:2], fsc[:, 3:4]))
                    link(dve.tensor_tensor(fsc[:, 2:3], tern[:, 0, 0:1], tern[:, 1, 0:1], ALU.mult))
                    link(dve.tensor_tensor(fsc[:, 3:4], tern[:, 2, 0:1], gat[:, 2:3], ALU.mult))
                    link(dve.tensor_tensor(fsc[:, 2:3], fsc[:, 2:3], fsc[:, 3:4], ALU.mult))
                    link(dve.tensor_scalar(fsc[:, 2:3], fsc[:, 2:3], 4.0, None, ALU.mult))

                dve.wait_ge(loaded["x"], 16)
                for t in range(TILES):
                    dve.bn_stats(stats[:, t, :], x[:, t, :]).then_inc(chain, 1)
                n_chain[0] += TILES
                dve.wait_ge(chain, n_chain[0])
                for t in range(TILES):
                    dve.bn_aggr(ln_mv[:, t, :], stats[:, t, :])
                dve.wait_ge(zeroed, 1 if phase == 0 else 3)
                for n in range(1, len(jobs), 2):
                    dve.wait_ge(done, n + 1)
                    copy_out(dve.tensor_copy, jobs[n], banks[n % 8], dve_out)
                    if n == at["sum", 0] - 1:
                        quantise()

            @block.tensor
            def _(pe):
                if phase == 0:
                    pe.wait_ge(loaded["cst"], 16)
                pe.wait_ge(zeroed, 1 if phase == 0 else 3)
                for n, (kind, k) in enumerate(jobs):
                    bank = banks[n % 8]
                    if n >= 8:
                        copied_out(pe, n - 8)
                    if kind == "ctx":
                        pe.wait_ge(loaded["ctx"], 16)
                        for q in range(4):
                            last = pe.transpose(bank[0:64, P * q:P * q + P], ctx_tok[:, 4 * k + q, :], ident)
                    elif kind == "sum":
                        pe.wait_ge(absum, 3)
                        last = pe.matmul(bank[:, 0:3], cst[:, C_ONES:C_ONES + P], part[:], start=True, stop=True)
                    elif kind == "qr":
                        pe.wait_ge(loaded["wqr"], 16)
                        for h in range(2):
                            for u in range(2):
                                c = 192 * h + 96 * u
                                last = pe.transpose(bank[0:64, c:c + 96], wqr[:, 2 * k + h, u, :], ident[0:96, 0:96])
                    elif kind == "kr":
                        pe.wait_ge(loaded["wkr"], 16)
                        for hp in range(HP):
                            last = pe.transpose(bank[:, 64 * hp:64 * hp + 64],
                                                wkr[:, 2 * hp:2 * hp + 2, :].rearrange("c h r -> c (h r)"), ident[0:64, 0:64])
                    elif kind == "C":
                        pe.wait_ge(loaded["wq"], 16)
                        pe.wait_ge(loaded["wcq"], 16)
                        for u in range(2):
                            last = pe.matmul(bank[:, DCQ * u:DCQ * u + DCQ], wq[:, k, P * u:P * u + P], wcq[:, k, :], start=True, stop=True)
                    elif kind == "wo":
                        pe.wait_ge(loaded["wo"], 16)
                        for h in range(2):
                            for u in range(2):
                                c = D * h + P * u
                                last = pe.transpose(bank[:, c:c + P], wo[:, u, P * (2 * k + h):P * (2 * k + h) + P], ident)
                    elif kind in ("N", "Ns"):
                        copied_out(pe, max(at["qr", k], at["kr", 0]))
                        src = qrT if kind == "N" else qrTs
                        for r in range(QR):
                            last = pe.matmul(bank[:, P * r:P * r + P], src[:, k, P * r:P * r + P], krT[:, k, :], start=True, stop=True)
                    elif kind == "V":
                        copied_out(pe, at["wo", k])
                        pe.wait_ge(loaded["wck"], 16)
                        for h in range(2):
                            last = pe.matmul(bank[64 * h:64 * h + 64, 0:D], wck[:, 2 * k + h, :], woT[:, 2 * k + h, :], start=True, stop=True)
                    elif kind in ("up", "gate"):
                        pe.wait_ge(quant, {"up": 1, "gate": 2}[kind])
                        src = q3[{"up": 0, "gate": 1}[kind]][:].rearrange("p (u d) -> p u d", u=ME)
                        for u in range(ME):
                            last = pe.transpose(bank[:].bitcast(F16)[:, P * u:P * u + P], src[:, u, P * k:P * k + P], identh[:])
                    elif kind == "down":
                        pe.wait_ge(quant, 3)
                        for u in range(ME):
                            last = pe.transpose(bank[:].bitcast(F16)[:, P * u:P * u + P],
                                                q3[2][:, DE * k + P * u:DE * k + P * u + P], identh[:])
                    last.then_inc(done, 1)


def inverse_std(nc, stage, ln_mv, ln_rs):
    with ExitStack() as ctx:
        m = Mem(nc, ctx, stage)
        ve = m.sb("ve", [P, TILES])
        root = m.sb("root", [P, TILES])
        tmp = m.sb("tmp", [P, TILES])
        ve_ready = m.sem("ve_ready")
        rooted = m.sem("rooted")
        newton = m.sem("newton")
        with nc.Block() as block:
            @block.scalar
            def _(act):
                act.wait_ge(ve_ready, 1)
                act.activation(root[:], ve[:], ACT.Sqrt).then_inc(rooted, 1)

            @block.vector
            def _(dve):
                dve.tensor_scalar(ve[:], ln_mv[:, :, 1], EPS_LN, None, ALU.add).then_inc(ve_ready, 1)
                dve.wait_ge(rooted, 1)
                dve.reciprocal(ln_rs[:], root[:]).then_inc(newton, 1)
                dve.wait_ge(newton, 1)
                dve.tensor_tensor(tmp[:], ln_rs[:], ln_rs[:], ALU.mult).then_inc(newton, 1)
                dve.wait_ge(newton, 2)
                dve.tensor_tensor(tmp[:], tmp[:], ve[:], ALU.mult).then_inc(newton, 1)
                dve.wait_ge(newton, 3)
                dve.tensor_scalar(tmp[:], tmp[:], -0.5, 1.5, ALU.mult, ALU.add).then_inc(newton, 1)
                dve.wait_ge(newton, 4)
                dve.tensor_tensor(ln_rs[:], ln_rs[:], tmp[:], ALU.mult).then_inc(newton, 1)
                dve.wait_ge(newton, 5)


def add_and_count(dve, t, n, y, scale, x, xt, st, mv, ln_mv, added):
    dve.scalar_tensor_tensor(xt[:], y, scale, x[:, t, :], ALU.mult, ALU.add).then_inc(added, 1)
    dve.wait_ge(added, 4 * n + 1)
    dve.bn_stats(st[:], xt[:]).then_inc(added, 1)
    dve.wait_ge(added, 4 * n + 2)
    dve.tensor_scalar(x[:, t, :], xt[:], 1.0, None, ALU.mult)
    dve.bn_aggr(mv[:], st[:]).then_inc(added, 1)
    dve.wait_ge(added, 4 * n + 3)
    dve.tensor_scalar(ln_mv[:, t, :], mv[:], 1.0, None, ALU.mult).then_inc(added, 1)


def attention0(nc, cst, x, ln_mv, ln_rs, gat, ident, ctxT, ctxd):
    with ExitStack() as ctx:
        m = Mem(nc, ctx, "a")
        xn = [m.sb(f"xn{u}", [P, D]) for u in range(2)]
        st = m.sb("st", [P, 6])
        mv = m.sb("mv", [P, 2])
        xt = m.sb("xt", [P, D])
        qT = [m.sb(f"qT{u}", [72, 2, G, S]) for u in range(2)]
        kT = [m.sb(f"kT{u}", [72, 2, KVH, T]) for u in range(2)]
        vB = [m.sb(f"vB{u}", [P, 2, 4, 2, HD + 1]) for u in range(2)]
        pr = [m.sb(f"pr{u}", [P, 2, 4, G, S]) for u in range(2)]
        mx = [m.sb(f"mx{u}", [P, 4, KVH]) for u in range(2)]
        rden = m.sb("rden", [P, 32])
        att = m.sb("att", [P, D])
        q_ps = m.ps("q_ps", [P, 2, P])
        m_ps = [m.ps(f"m_ps{n}", [P, 512]) for n in range(2)]
        mT_ps = m.ps("mT_ps", [8, 4, P])
        s_ps = [m.ps(f"s_ps{n}", [P, 512]) for n in range(2)]
        o_ps = m.ps("o_ps", [P, 4 * G * 2 * (HD + 1)])
        SC = float(HD) ** -0.5

        xn_ready = m.sem("xn_ready")
        q_done = m.sem("q_done")
        q_copied = m.sem("q_copied")
        kv_ready = m.sem("kv_ready")
        scored = m.sem("scored")
        maxed = m.sem("maxed")
        mT_done = m.sem("mT_done")
        mT_copied = m.sem("mT_copied")
        sT_done = m.sem("sT_done")
        exped = m.sem("exped")
        pv_done = m.sem("pv_done")
        nrm = m.sem("nrm")
        added = m.sem("added")
        init = m.sem("init")

        with nc.Block() as block:
            @block.gpsimd
            def _(pool):
                for u in range(2):
                    pool.memset(vB[u][:], 0.0).then_inc(init, 1)
                pool.wait_ge(init, 2)
                for u in range(2):
                    for h in range(2):
                        pool.memset(vB[u][64 * h:64 * h + 64, :, :, h, HD:HD + 1], 1.0)
                    pool.tensor_copy(kT[u][64:72], cst[64:72, C_K1:C_K1 + 1024])

                def step(t, u):
                    wait(pool, pv_done, t - 1)
                    for b in range(2):
                        src = ctxT[:, t, T * b:T * b + T].unsqueeze(1).to_broadcast([64, KVH, T])
                        pool.tensor_tensor(kT[u][0:64, b], src, cst[0:64, C_KM:C_KM + 8].unsqueeze(2).to_broadcast([64, KVH, T]), ALU.mult)
                    for h in range(2):
                        rows = slice(64 * h, 64 * h + 64)
                        for b in range(2):
                            src = ctxd[rows, 2 * t + b, :].rearrange("p (n h d) -> p n h d", n=4, h=2)[:, :, h, :]
                            last = pool.tensor_copy(vB[u][rows, b, :, h, 0:HD], src)
                    last.then_inc(kv_ready, 1)
                over_tiles(pool, step)

            @block.vector
            def _(dve):
                def norm(t, u):
                    wait(dve, q_done, t - 1)
                    dve.tensor_scalar(xn[u][:].rearrange("p (g j d) -> p j g d", g=G, j=KVH), x[:, t, :].rearrange("p (j g d) -> p j g d", j=KVH, g=G),
                                      ln_mv[:, t, 0:1], ln_rs[:, bass.ds(t, 1)], ALU.subtract, ALU.mult).then_inc(xn_ready, 1)

                def maxima(t, u):
                    wait(dve, mT_done, t - 1)
                    for n in range(4):
                        dve.wait_ge(scored, 4 * t + n + 1)
                        dve.tensor_reduce(mx[u][:, n, :], m_ps[n % 2][:].rearrange("p (j t) -> p j t", j=KVH), AX.X, ALU.max).then_inc(maxed, 1)

                def output(t, u):
                    wait(dve, added, 4 * t)
                    dve.wait_ge(pv_done, t + 1)
                    o = o_ps[:].rearrange("p (n g h d) -> p n g h d", n=4, g=G, h=2)
                    dve.reciprocal(rden[:].rearrange("p (n g h) -> p n g h", n=4, g=G), o[:, :, :, :, HD]).then_inc(nrm, 1)
                    dve.wait_ge(nrm, 5 * t + 1)
                    for n in range(4):
                        dst = att[:].rearrange("p (n h g d) -> p n g h d", n=4, h=2, g=G)[:, n]
                        r = rden[:].rearrange("p (n g h) -> p n g h", n=4, g=G)[:, n].unsqueeze(3).to_broadcast([P, G, 2, HD])
                        dve.tensor_tensor(dst, o[:, n, :, :, 0:HD], r, ALU.mult).then_inc(nrm, 1)
                    dve.wait_ge(nrm, 5 * t + 5)
                    add_and_count(dve, t, t, att[:], gat[:, 0:1], x, xt, st, mv, ln_mv, added)

                def step(t, u):
                    if within(t + 2):
                        norm(t + 2, u)
                    if within(t + 1):
                        maxima(t + 1, 1 - u)
                    output(t, u)
                norm(0, 0)
                norm(1, 1)
                maxima(0, 0)
                over_tiles(dve, step)

            @block.scalar
            def _(act):
                def queries(t, u):
                    act.wait_ge(q_done, t + 1)
                    wait(act, pv_done, t - 1)
                    for h in range(2):
                        src = q_ps[64 * h:64 * h + 64].rearrange("p n (b s) -> p n b s", b=2)
                        last = act.copy(qT[u][0:64].rearrange("p b (n h) s -> p h n b s", h=2)[:, h], src)
                    last.then_inc(q_copied, 1)

                def step(t, u):
                    if within(t + 1):
                        queries(t + 1, 1 - u)
                    act.wait_ge(mT_done, t + 1)
                    act.mul(qT[u][64:72], mT_ps[:], -1.0).then_inc(mT_copied, 1)
                    for n in range(4):
                        act.wait_ge(sT_done, 4 * t + n + 1)
                        act.activation(pr[u][:, n // 2, 2 * (n % 2):2 * (n % 2) + 2], s_ps[n % 2][:], ACT.Exp, scale=SC).then_inc(exped, 1)
                queries(0, 0)
                over_tiles(act, step)

            @block.tensor
            def _(pe):
                def head(t, u):
                    pe.wait_ge(xn_ready, t + 1)
                    wait(pe, q_copied, t)
                    for n in range(2):
                        last = pe.transpose(q_ps[:, n, :], xn[u][:, P * n:P * n + P], ident)
                    last.then_inc(q_done, 1)
                    pe.wait_ge(q_copied, t + 1)
                    pe.wait_ge(kv_ready, t + 1)
                    for n in range(4):
                        wait(pe, maxed, 4 * t + n - 1)
                        b, gp = n // 2, n % 2
                        pe.matmul(m_ps[n % 2][:], qT[u][0:64, b, 2 * gp:2 * gp + 2, :], kT[u][0:64, b], start=True, stop=True).then_inc(scored, 1)

                def tail(t, u):
                    pe.wait_ge(maxed, 4 * t + 4)
                    wait(pe, mT_copied, t)
                    for n in range(4):
                        last = pe.transpose(mT_ps[:, n, :], mx[u][:, n, :], ident)
                    last.then_inc(mT_done, 1)
                    pe.wait_ge(mT_copied, t + 1)
                    for n in range(4):
                        wait(pe, exped, 4 * t + n - 1)
                        b = n // 2
                        for k in range(2):
                            jp = 2 * (n % 2) + k
                            last = pe.matmul(s_ps[n % 2][:, 256 * k:256 * k + 256], kT[u][:, b, 2 * jp:2 * jp + 2, :], qT[u][:, b], start=True, stop=True)
                        last.then_inc(sT_done, 1)
                    pe.wait_ge(exped, 4 * t + 4)
                    wait(pe, nrm, 5 * t)
                    W = HD + 1
                    for b in range(2):
                        for jp in range(4):
                            for gq in range(G):
                                c = (jp * G + gq) * 2 * W
                                last = pe.matmul(o_ps[64 * b:64 * b + 64, c:c + 2 * W], pr[u][:, b, jp, gq, :], vB[u][:, b, jp], start=True, stop=True)
                    last.then_inc(pv_done, 1)

                def step(t, u):
                    if within(t + 1):
                        head(t + 1, 1 - u)
                    tail(t, u)
                head(0, 0)
                over_tiles(pe, step)


def normalise_chunk(dve, c, x, ln_mv, ln_rs, xn, xn_ready):
    for q in range(QT):
        t = QT * c + q
        last = dve.tensor_scalar(xn[:, q, :], x[:, t, :], ln_mv[:, t, 0:1], ln_rs[:, bass.ds(t, 1)], ALU.subtract, ALU.mult)
    last.then_inc(xn_ready, 1)


def over_chunks(eng, step):
    step(0)
    with eng.Fori(1, CHUNKS - 1) as c:
        step(c)
    step(CHUNKS - 1)


def ffn0(nc, x, ln_mv, ln_rs, ident, k_up, k_gate, k_down, fsc):
    with ExitStack() as ctx:
        m = Mem(nc, ctx, "f")
        st = m.sb("st", [P, 6])
        mv = m.sb("mv", [P, 2])
        xt = m.sb("xt", [P, D])
        xn = m.sb("xn", [P, QT, D])
        xh = m.sb("xh", [P, 2, CH], F16)
        xl = m.sb("xl", [P, 2, CH], F16)
        sg = [m.sb(f"sg{n}", [P, CH]) for n in range(2)]
        h = [m.sb(f"h{n}", [P, CH]) for n in range(2)]
        hh = m.sb("hh", [P, ME, CH], F16)
        hl = m.sb("hl", [P, ME, CH], F16)
        xT_ps = m.ps("xT_ps", [P, 2, CH])
        u_ps = [m.ps(f"u_ps{n}", [P, CH]) for n in range(2)]
        g_ps = [m.ps(f"g_ps{n}", [P, CH]) for n in range(2)]
        d_ps = [m.ps(f"d_ps{n}", [P, D]) for n in range(2)]

        xn_ready = m.sem("xn_ready")
        xT_done = m.sem("xT_done")
        xh_done = m.sem("xh_done")
        xl_done = m.sem("xl_done")
        u_done = m.sem("u_done")
        g_done = m.sem("g_done")
        silu = m.sem("silu")
        h_done = m.sem("h_done")
        hh_done = m.sem("hh_done")
        hl_done = m.sem("hl_done")
        d_done = m.sem("d_done")
        added = m.sem("added")

        with nc.Block() as block:
            @block.vector
            def _(dve):
                def norm(c):
                    wait(dve, xT_done, 1 * c)
                    normalise_chunk(dve, c, x, ln_mv, ln_rs, xn, xn_ready)

                def x_low(c):
                    for k in range(2):
                        dve.wait_ge(xh_done, 2 * c + k + 1)
                        dve.scalar_tensor_tensor(xl[:, k, :], xT_ps[:, k, :], XS, xh[:, k, :], ALU.mult, ALU.subtract).then_inc(xl_done, 1)

                def product(c, n):
                    dve.wait_ge(silu, 8 * c + n + 1)
                    dve.wait_ge(g_done, 8 * c + n + 1)
                    wait(dve, hl_done, 8 * c + n - 1)
                    dve.scalar_tensor_tensor(h[n % 2][:], sg[n % 2][:], fsc[:, 1:2], g_ps[n % 2][:], ALU.mult, ALU.mult).then_inc(h_done, 1)

                def low(c, n):
                    dve.wait_ge(hh_done, 8 * c + n + 1)
                    dve.tensor_tensor(hl[:, n, :], h[n % 2][:], hh[:, n, :], ALU.subtract).then_inc(hl_done, 1)

                def step(c):
                    if within(c + 1, CHUNKS):
                        norm(c + 1)
                    product(c, 0)
                    for n in range(ME):
                        if n + 1 < ME:
                            product(c, n + 1)
                        low(c, n)
                    if within(c + 1, CHUNKS):
                        x_low(c + 1)
                    for q in range(QT):
                        dve.wait_ge(d_done, QT * c + q + 1)
                        wait(dve, added, 4 * (QT * c + q))
                        add_and_count(dve, QT * c + q, QT * c + q, d_ps[q % 2][:], fsc[:, 2:3], x, xt, st, mv, ln_mv, added)
                norm(0)
                x_low(0)
                over_chunks(dve, step)

            @block.scalar
            def _(act):
                def x_high(c):
                    act.wait_ge(xT_done, c + 1)
                    for k in range(2):
                        act.mul(xh[:, k, :], xT_ps[:, k, :], XS).then_inc(xh_done, 1)

                def silus(c, n):
                    act.wait_ge(u_done, 8 * c + n + 1)
                    wait(act, h_done, 8 * c + n - 1)
                    act.activation(sg[n % 2][:], u_ps[n % 2][:], ACT.Silu, scale=fsc[:, 0:1]).then_inc(silu, 1)

                def step(c):
                    silus(c, 0)
                    for n in range(ME):
                        if n + 1 < ME:
                            silus(c, n + 1)
                        act.wait_ge(h_done, 8 * c + n + 1)
                        if n == 0:
                            wait(act, d_done, QT * c)
                        act.copy(hh[:, n, :], h[n % 2][:]).then_inc(hh_done, 1)
                    if within(c + 1, CHUNKS):
                        x_high(c + 1)
                x_high(0)
                over_chunks(act, step)

            @block.tensor
            def _(pe):
                def transposes(c):
                    pe.wait_ge(xn_ready, c + 1)
                    wait(pe, xl_done, 2 * c)
                    for k in range(2):
                        for q in range(QT):
                            last = pe.transpose(xT_ps[:, k, P * q:P * q + P], xn[:, q, P * k:P * k + P], ident)
                    last.then_inc(xT_done, 1)

                def step(c):
                    pe.wait_ge(xl_done, 2 * c + 2)
                    for n in range(ME):
                        for w, ps, sem, used in ((k_up, u_ps, u_done, silu), (k_gate, g_ps, g_done, h_done)):
                            wait(pe, used, 8 * c + n - 1)
                            for k in range(2):
                                for part in (xh, xl):
                                    last = pe.matmul(ps[n % 2][:], w[:, k, P * n:P * n + P], part[:, k, :],
                                                     start=(k == 0 and part is xh), stop=(k == 1 and part is xl))
                            last.then_inc(sem, 1)
                    if within(c + 1, CHUNKS):
                        transposes(c + 1)
                    pe.wait_ge(hl_done, 8 * c + 8)
                    for q in range(QT):
                        wait(pe, added, 4 * (QT * c + q) - 7)
                        for n in range(ME):
                            for part in (hh, hl):
                                last = pe.matmul(d_ps[q % 2][:], part[:, n, P * q:P * q + P], k_down[:, n, :],
                                                 start=(n == 0 and part is hh), stop=(n == ME - 1 and part is hl))
                        last.then_inc(d_done, 1)
                transposes(0)
                over_chunks(pe, step)


def attention1(nc, cst, x, ln_mv, ln_rs, gat, ident, Cw, NBc, NBs, VT, kvr):
    with ExitStack() as ctx:
        m = Mem(nc, ctx, "c")
        st = m.sb("st", [P, 6])
        mv = m.sb("mv", [P, 2])
        xt = m.sb("xt", [P, D])
        xn = m.sb("xn", [P, QT, D])
        xT = m.sb("xT", [P, 2, CH])
        qc = [m.sb(f"qc{n}", [P, CH]) for n in range(2)]
        qs = [m.sb(f"qs{n}", [P, CH]) for n in range(2)]
        qn = m.sb("qn", [P, HP, CH])
        vB = [m.sb(f"vB{u}", [P, 2, P]) for u in range(2)]
        kB = [m.sb(f"kB{u}", [P, 2, P]) for u in range(2)]
        sc = m.sb("sc", [P, H1, T])
        mx = m.sb("mx", [P, H1])
        sm = m.sb("sm", [P, H1])
        rs = m.sb("rs", [P, H1])
        pT = m.sb("pT", [P, HP, P])
        cT = m.sb("cT", [P, HP, P])
        q_ps = [m.ps(f"q_ps{n}", [P, CH]) for n in range(2)]
        n_ps = m.ps("n_ps", [P, CH])
        s_ps = [m.ps(f"s_ps{n}", [P, 512]) for n in range(2)]
        v_ps = [m.ps(f"v_ps{n}", [P, 512]) for n in range(2)]
        o_ps = m.ps("o_ps", [P, D])

        zeroed = m.sem("zeroed")
        xn_ready = m.sem("xn_ready")
        xT_done = m.sem("xT_done")
        xT_copied = m.sem("xT_copied")
        q_done = m.sem("q_done")
        c_done = m.sem("c_done")
        r_done = m.sem("r_done")
        n_used = m.sem("n_used")
        n_copied = m.sem("n_copied")
        vB_ready = m.sem("vB_ready")
        kB_done = m.sem("kB_done")
        kB_copied = m.sem("kB_copied")
        s_done = m.sem("s_done")
        smx = m.sem("smx")
        exped = m.sem("exped")
        pnorm = m.sem("pnorm")
        p_done = m.sem("p_done")
        p_copied = m.sem("p_copied")
        v_done = m.sem("v_done")
        v_copied = m.sem("v_copied")
        o_done = m.sem("o_done")
        added = m.sem("added")
        NB = HP * QR

        with nc.Block() as block:
            @block.gpsimd
            def _(pool):
                for u in range(2):
                    pool.memset(vB[u][:], 0.0).then_inc(zeroed, 1)
                pool.wait_ge(zeroed, 2)

                def blocks(t, u):
                    wait(pool, pnorm, t)
                    wait(pool, v_done, 2 * t - 2)
                    for h in range(2):
                        rows = slice(64 * h, 64 * h + 64)
                        last = pool.tensor_copy(vB[u][rows, :, 64 * h:64 * h + 64], kvr[rows, bass.ds(2 * t, 2), :])
                    last.then_inc(vB_ready, 1)

                def step(c):
                    for q in range(QT):
                        t = QT * c + q
                        blocks(t, q % 2)
                        pool.wait_ge(smx, 5 * t + 5)
                        pool.tensor_tensor(sc[:], sc[:], rs[:].unsqueeze(2).to_broadcast([P, H1, T]), ALU.mult).then_inc(pnorm, 1)
                over_chunks(pool, step)

            @block.vector
            def _(dve):
                cos = cst[:, C_CQ:C_CQ + QR * S].rearrange("p (r s) -> p r s", r=QR)
                sin = cst[:, C_SQ:C_SQ + QR * S].rearrange("p (r s) -> p r s", r=QR)

                def rotate(c, n):
                    dve.wait_ge(q_done, NB * c + n + 1)
                    wait(dve, n_used, NB * c + n - 1)
                    for dst, tab, sem in ((qc, cos, c_done), (qs, sin, r_done)):
                        dve.tensor_tensor(dst[n % 2][:].rearrange("p (b s) -> p b s", s=S), q_ps[n % 2][:].rearrange("p (b s) -> p b s", s=S),
                                          tab[:, n % QR, :].unsqueeze(1).to_broadcast([P, CH // S, S]), ALU.mult).then_inc(sem, 1)

                def softmax(t):
                    dve.wait_ge(s_done, t + 1)
                    wait(dve, pnorm, t)
                    for k in range(2):
                        dve.tensor_reduce(mx[:, 8 * k:8 * k + 8], s_ps[k][:].rearrange("p (h t) -> p h t", t=T), AX.X, ALU.max).then_inc(smx, 1)
                    dve.wait_ge(smx, 5 * t + 2)
                    wait(dve, p_done, 2 * t)
                    for k in range(2):
                        last = dve.tensor_tensor(sc[:, 8 * k:8 * k + 8, :], s_ps[k][:].rearrange("p (h t) -> p h t", t=T),
                                                 mx[:, 8 * k:8 * k + 8].unsqueeze(2).to_broadcast([P, 8, T]), ALU.subtract)
                    last.then_inc(smx, 1)
                    dve.wait_ge(exped, t + 1)
                    dve.tensor_reduce(sm[:], sc[:], AX.X, ALU.add).then_inc(smx, 1)
                    dve.wait_ge(smx, 5 * t + 4)
                    dve.reciprocal(rs[:], sm[:]).then_inc(smx, 1)

                def output(t):
                    wait(dve, added, 4 * t)
                    dve.wait_ge(o_done, t + 1)
                    add_and_count(dve, t, t, o_ps[:], gat[:, 1:2], x, xt, st, mv, ln_mv, added)

                def step(c):
                    wait(dve, xT_done, 1 * c)
                    normalise_chunk(dve, c, x, ln_mv, ln_rs, xn, xn_ready)
                    for n in range(NB):
                        rotate(c, n)
                    for q in range(QT):
                        softmax(QT * c + q)
                        if q:
                            output(QT * c + q - 1)
                    output(QT * c + QT - 1)
                over_chunks(dve, step)

            @block.scalar
            def _(act):
                def step(c):
                    act.wait_ge(xT_done, c + 1)
                    for k in range(2):
                        last = act.copy(xT[:, k, :], s_ps[k][:])
                    last.then_inc(xT_copied, 1)
                    for hp in range(HP):
                        act.wait_ge(n_used, NB * c + QR * hp + QR)
                        wait(act, o_done, QT * c)
                        act.copy(qn[:, hp, :], n_ps[:]).then_inc(n_copied, 1)
                    for q in range(QT):
                        t = QT * c + q
                        act.wait_ge(kB_done, t + 1)
                        wait(act, s_done, t - 1)
                        act.copy(kB[q % 2][:], q_ps[q % 2][:, 0:2 * P]).then_inc(kB_copied, 1)
                        act.wait_ge(smx, 5 * t + 3)
                        act.activation(sc[:], sc[:], ACT.Exp).then_inc(exped, 1)
                        if q:
                            values(t - 1)
                    values(QT * c + QT - 1)

                def values(t):
                    for k in range(2):
                        act.wait_ge(p_done, 2 * t + k + 1)
                        if k == 0:
                            wait(act, v_done, 2 * t)
                        act.copy(pT[:, 4 * k:4 * k + 4, :], n_ps[:] if k == 0 else v_ps[0][:]).then_inc(p_copied, 1)
                    for b in range(2):
                        act.wait_ge(v_done, 2 * t + b + 1)
                        if b == 0:
                            wait(act, o_done, t)
                        act.copy(cT[:, :, S * b:S * b + S], v_ps[1 - b][:].rearrange("p (h s) -> p h s", s=S)).then_inc(v_copied, 1)
                over_chunks(act, step)

            @block.tensor
            def _(pe):
                def project(c, n):
                    hp, r = n // QR, n % QR
                    wait(pe, r_done, NB * c + n - 1)
                    for k in range(2):
                        last = pe.matmul(q_ps[n % 2][:], Cw[:, k, hp, P * r:P * r + P], xT[:, k, :], start=(k == 0), stop=(k == 1))
                    last.then_inc(q_done, 1)

                def combine(c, n):
                    hp, r = n // QR, n % QR
                    if r == 0:
                        wait(pe, n_copied, HP * c + hp)
                    pe.wait_ge(c_done, NB * c + n + 1)
                    pe.matmul(n_ps[:], NBc[:, hp, r, :], qc[n % 2][:], start=(r == 0), stop=False)
                    pe.wait_ge(r_done, NB * c + n + 1)
                    pe.matmul(n_ps[:], NBs[:, hp, r, :], qs[n % 2][:], start=False, stop=(r == QR - 1)).then_inc(n_used, 1)

                def scores(c, q):
                    t = QT * c + q
                    pe.wait_ge(vB_ready, t + 1)
                    if q < 2:
                        pe.wait_ge(r_done, NB * c + NB)
                    else:
                        pe.wait_ge(kB_copied, t - 1)
                    for b in range(2):
                        last = pe.transpose(q_ps[q % 2][:, P * b:P * b + P], vB[q % 2][:, b, :], ident)
                    last.then_inc(kB_done, 1)
                    pe.wait_ge(kB_copied, t + 1)
                    wait(pe, smx, 5 * t - 2)
                    for b in range(2):
                        for hp in range(HP):
                            cols = slice(P * (hp % 4), P * (hp % 4) + P)
                            last = pe.matmul(s_ps[hp // 4][64 * b:64 * b + 64, cols], qn[:, hp, P * q + S * b:P * q + S * b + S],
                                             kB[q % 2][:, b, :], start=True, stop=True)
                    last.then_inc(s_done, 1)

                def values(c, q):
                    t = QT * c + q
                    pe.wait_ge(pnorm, t + 1)
                    for k in range(2):
                        dst = n_ps if k == 0 else v_ps[0]
                        if k == 0:
                            wait(pe, n_copied, HP * c + HP)
                            wait(pe, p_copied, 2 * t)
                        else:
                            wait(pe, v_copied, 2 * t)
                        for n in range(4):
                            hp = 4 * k + n
                            last = pe.transpose(dst[:, P * n:P * n + P], sc[:, 2 * hp:2 * hp + 2, :].rearrange("p h t -> p (h t)"), ident)
                        last.then_inc(p_done, 1)
                    pe.wait_ge(p_copied, 2 * t + 2)
                    for b in range(2):
                        pe.matmul(v_ps[1 - b][:].rearrange("p (h s) -> p h s", s=S), vB[q % 2][:, b, :], pT[:, :, S * b:S * b + S],
                                  start=True, stop=True).then_inc(v_done, 1)
                    pe.wait_ge(v_copied, 2 * t + 2)
                    wait(pe, added, 4 * t - 3)
                    for hp in range(HP):
                        last = pe.matmul(o_ps[:], cT[:, hp, :], VT[:, hp, :], start=(hp == 0), stop=(hp == HP - 1))
                    last.then_inc(o_done, 1)

                def step(c):
                    pe.wait_ge(xn_ready, c + 1)
                    wait(pe, smx, 5 * QT * c - 2)
                    for k in range(2):
                        for q in range(QT):
                            last = pe.transpose(s_ps[k][:, P * q:P * q + P], xn[:, q, P * k:P * k + P], ident)
                    last.then_inc(xT_done, 1)
                    pe.wait_ge(xT_copied, c + 1)
                    wait(pe, kB_copied, QT * c)
                    wait(pe, p_copied, 2 * QT * c)
                    project(c, 0)
                    for n in range(NB):
                        if n + 1 < NB:
                            project(c, n + 1)
                        combine(c, n)
                    scores(c, 0)
                    for q in range(QT):
                        if q + 1 < QT:
                            scores(c, q + 1)
                        values(c, q)
                over_chunks(pe, step)


def moe(nc, a, cst, x, ln_mv, ln_rs, gat, ident, out, xg_dram, acc_dram):
    with ExitStack() as ctx:
        m = Mem(nc, ctx, "m")
        idT = m.sb("idT", [CAP, E], U32)
        wg = [m.sb(f"wg{b}", [P, 2, I1]) for b in range(NB)]
        wu = [m.sb(f"wu{b}", [P, 2, I1]) for b in range(NB)]
        wd = [m.sb(f"wd{b}", [I1, D]) for b in range(NB)]
        weights = [m.sem(f"weights{b}") for b in range(NB)]

        def load_expert(sp, e, b):
            sp.dma_start(wg[b][:], a["L1_ffn_w_gate"][bass.ds(e, 1)].rearrange("o (k d) i -> d (o k) i", k=2)).then_inc(weights[b], 16)
            sp.dma_start(wu[b][:], a["L1_ffn_w_up"][bass.ds(e, 1)].rearrange("o (k d) i -> d (o k) i", k=2)).then_inc(weights[b], 16)
            sp.dma_start(wd[b][:], a["L1_ffn_w_down"][bass.ds(e, 1)].rearrange("o i d -> (o i) d")).then_inc(weights[b], 16)
        with ExitStack() as inner:
            r = Mem(nc, inner, "s")
            scores = r.sb("scores", [P, TILES, E])
            biased = r.sb("biased", [P, TILES, E])
            shared_and_router(nc, a, cst, x, ln_mv, ln_rs, gat, ident, xg_dram, acc_dram, scores, biased)
            route(nc, cst, x, gat, xg_dram, acc_dram, scores, biased, idT, load_expert)
        experts(nc, ident, xg_dram, acc_dram, idT, wg, wu, wd, weights, load_expert)
        total(nc, out, acc_dram)


def shared_and_router(nc, a, cst, x, ln_mv, ln_rs, gat, ident, xg_dram, acc_dram, scores, biased):
    with ExitStack() as ctx:
        m = Mem(nc, ctx, "r")
        rw = m.sb("rw", [E, D])
        rwT = m.sb("rwT", [P, 2, E])
        bias = m.sb("bias", [P, E])
        zero = m.sb("zero", [P, XW])
        wg = m.sb("wg", [P, 2, I1])
        wu = m.sb("wu", [P, 2, I1])
        wd = m.sb("wd", [I1, D])
        xn = [m.sb(f"xn{u}", [P, D]) for u in range(2)]
        xT = [m.sb(f"xT{u}", [P, 2, P]) for u in range(2)]
        rs = [m.sb(f"rs{u}", [P, E]) for u in range(2)]
        sg = [m.sb(f"sg{u}", [I1, P]) for u in range(2)]
        ha = [m.sb(f"ha{u}", [I1, P]) for u in range(2)]
        hb = [m.sb(f"hb{u}", [I1, P]) for u in range(2)]
        xT_ps = [m.ps(f"xT_ps{u}", [P, 2, P]) for u in range(2)]
        r_ps = [m.ps(f"r_ps{u}", [P, E]) for u in range(2)]
        gu_ps = [m.ps(f"gu_ps{u}", [I1, 2, P]) for u in range(2)]
        o_ps = [m.ps(f"o_ps{u}", [P, D]) for u in range(2)]

        loaded = m.sem("loaded")
        zeroed = m.sem("zeroed")
        cleared = m.sem("cleared")
        rw_done = m.sem("rw_done")
        rw_copied = m.sem("rw_copied")
        xn_ready = m.sem("xn_ready")
        stored = [m.sem(f"stored{u}") for u in range(2)]
        xT_done = m.sem("xT_done")
        xT_copied = m.sem("xT_copied")
        gu_done = m.sem("gu_done")
        sig = m.sem("sig")
        hid = m.sem("hid")
        o_done = m.sem("o_done")
        added = m.sem("added")

        with nc.Block() as block:
            @block.sync
            def _(sp):
                for dst, src in ((rw, a["L1_ffn_router_weight"]), (wg, a["L1_ffn_sh_gate"].rearrange("(k d) i -> d k i", k=2)),
                                 (wu, a["L1_ffn_sh_up"].rearrange("(k d) i -> d k i", k=2)), (wd, a["L1_ffn_sh_down"]),
                                 (bias, a["L1_ffn_e_bias"].rearrange("(o e) -> o e", o=1).to_broadcast([P, E]))):
                    sp.dma_start(dst[:], src).then_inc(loaded, 16)

                sp.wait_ge(zeroed, 1)
                sp.dma_start(acc_dram[1].rearrange("(n p) d -> p n d", p=P), zero[:, 0:D].unsqueeze(1).to_broadcast([P, ROWS // P, D])).then_inc(cleared, 16)
                sp.dma_start(acc_dram[0][TOK:ROWS], zero[0:CAP, 0:D]).then_inc(cleared, 16)
                sp.dma_start(xg_dram[TOK:ROWS], zero[0:CAP, :]).then_inc(cleared, 16)

                def step(t, u):
                    sp.wait_ge(xn_ready, t + 1)
                    sp.dma_start(xg_dram[bass.ds(P * t, P), 0:D], xn[u][:]).then_inc(stored[u], 16)
                over_tiles(sp, step)
                for u in range(2):
                    sp.wait_ge(stored[u], 16 * TILES // 2)
                sp.wait_ge(cleared, 48)

            @block.gpsimd
            def _(pool):
                pool.memset(zero[:], 0.0).then_inc(zeroed, 1)

            @block.vector
            def _(dve):
                def norm(t, u):
                    wait(dve, xT_done, t - 1)
                    wait(dve, stored[u], 8 * (t - u))
                    dve.tensor_scalar(xn[u][:], x[:, t, :], ln_mv[:, t, 0:1], ln_rs[:, bass.ds(t, 1)], ALU.subtract, ALU.mult).then_inc(xn_ready, 1)

                def step(t, u):
                    if within(t + 1):
                        norm(t + 1, 1 - u)
                    dve.wait_ge(sig, t + 1)
                    wait(dve, hid, 4 * t - 4)
                    dve.tensor_tensor(ha[u][:], sg[u][:], gu_ps[u][:, 0, :], ALU.mult).then_inc(hid, 1)
                    dve.wait_ge(hid, 4 * t + 1)
                    wait(dve, o_done, t - 1)
                    dve.tensor_tensor(hb[u][:], ha[u][:], gu_ps[u][:, 1, :], ALU.mult).then_inc(hid, 1)
                    dve.tensor_tensor(biased[:, t, :], rs[u][:], bias[:], ALU.add).then_inc(hid, 1)
                    dve.tensor_scalar(scores[:, t, :], rs[u][:], 1.0, None, ALU.mult).then_inc(hid, 1)
                    dve.wait_ge(o_done, t + 1)
                    dve.scalar_tensor_tensor(x[:, t, :], o_ps[u][:], gat[:, 3:4], x[:, t, :], ALU.mult, ALU.add).then_inc(added, 1)
                dve.wait_ge(loaded, 80)
                dve.wait_ge(rw_done, 1)
                dve.tensor_copy(rwT[:], xT_ps[0][:, 0, :]).then_inc(rw_copied, 1)
                norm(0, 0)
                over_tiles(dve, step)

            @block.scalar
            def _(act):
                def step(t, u):
                    act.wait_ge(xT_done, t + 1)
                    wait(act, gu_done, t - 1)
                    act.copy(xT[u][:], xT_ps[u][:]).then_inc(xT_copied, 1)
                    act.wait_ge(gu_done, t + 1)
                    wait(act, hid, 4 * t - 4)
                    act.activation(rs[u][:], r_ps[u][:], ACT.Sigmoid)
                    act.activation(sg[u][:], gu_ps[u][:, 0, :], ACT.Sigmoid).then_inc(sig, 1)
                over_tiles(act, step)

            @block.tensor
            def _(pe):
                pe.wait_ge(loaded, 80)
                for k in range(2):
                    last = pe.transpose(xT_ps[0][:, 0, E * k:E * k + E], rw[:, P * k:P * k + P], ident[0:E, 0:E])
                last.then_inc(rw_done, 1)
                pe.wait_ge(rw_copied, 1)

                def step(t, u):
                    pe.wait_ge(xn_ready, t + 1)
                    wait(pe, xT_copied, t - 1)
                    for k in range(2):
                        last = pe.transpose(xT_ps[u][:, k, :], xn[u][:, P * k:P * k + P], ident)
                    last.then_inc(xT_done, 1)
                    pe.wait_ge(xT_copied, t + 1)
                    wait(pe, hid, 4 * t - 4)
                    for k in range(2):
                        pe.matmul(r_ps[u][:], xT[u][:, k, :], rwT[:, k, :], start=(k == 0), stop=(k == 1))
                    for n, w in enumerate((wg, wu)):
                        for k in range(2):
                            last = pe.matmul(gu_ps[u][:, n, :], w[:, k, :], xT[u][:, k, :], start=(k == 0), stop=(k == 1))
                    last.then_inc(gu_done, 1)
                    pe.wait_ge(hid, 4 * t + 2)
                    wait(pe, added, t - 1)
                    pe.matmul(o_ps[u][:], hb[u][:], wd[:], start=True, stop=True).then_inc(o_done, 1)
                over_tiles(pe, step)


def route(nc, cst, x, gat, xg_dram, acc_dram, scores, biased, idT, load_expert):
    N = TILES * E
    with ExitStack() as ctx:
        m = Mem(nc, ctx, "t")
        hi = m.sb("hi", [P, TILES * NG, 4])
        lo = m.sb("lo", [P, TILES * NG, 4])
        hi2 = m.sb("hi2", [P, TILES * NG, 2])
        mi2 = m.sb("mi2", [P, TILES * NG, 2])
        lo2 = m.sb("lo2", [P, TILES * NG, 2])
        gs = m.sb("gs", [P, TILES, NG])
        g2 = m.sb("g2", [P, TILES, NG])
        w1 = m.sb("w1", [P, TILES, E])
        w2 = m.sb("w2", [P, TILES, E])
        sel = m.sb("sel", [P, TILES, E])
        prev = m.sb("prev", [P, TILES, E])
        top = m.sb("top", [P, TILES, TOPK])
        top_e = m.sb("top_e", [P, TILES, TOPK])
        at_pos = m.sb("at_pos", [P, TILES, TOPK, CAP], F16)
        at_e = m.sb("at_e", [P, TILES, TOPK, E], F16)
        tok_e = [m.sb(f"tok_e{u}", [P, TOPK, E], F16) for u in range(2)]
        idv = m.sb("idv", [CAP, E])
        ide = m.sb("ide", [CAP, E])
        s16 = m.sb("s16", [P, TILES])
        id_ps = m.ps("id_ps", [CAP, E])
        pos_ps = [m.ps(f"pos_ps{k}", [P, 512]) for k in range(2)]
        chain = m.sem("chain")
        selected = m.sem("selected")
        gated = m.sem("gated")
        counted = m.sem("counted")
        stored = m.sem("stored")
        hot = m.sem("hot")
        tok_ready = m.sem("tok_ready")
        listed = m.sem("listed")

        with nc.Block() as block:
            @block.sync
            def _(sp):
                sp.dma_start(acc_dram[0][0:TOK].rearrange("(n p) d -> p n d", p=P), x[:]).then_inc(stored, 16)
                for b in range(NB):
                    load_expert(sp, b, b)
                sp.wait_ge(gated, 1)
                sp.dma_start(xg_dram[0:TOK].rearrange("(n p) w -> p n w", p=P)[:, :, D:XW], w2[:]).then_inc(stored, 16)
                sp.wait_ge(stored, 32)

            @block.scalar
            def _(act):
                for t in range(TILES):
                    act.wait_ge(hot, t + 1)
                    wait(act, listed, t - 1)
                    act.activation(tok_e[t % 2][:], at_e[:, t], ACT.Copy, scale=cst[:, C_TOK + t:C_TOK + t + 1]).then_inc(tok_ready, 1)

            @block.tensor
            def _(pe):
                pe.wait_ge(selected, 1)
                for k in range(2):
                    pe.matmul(pos_ps[k][:], cst[:, C_TRI:C_TRI + P], sel[:, 8 * k:8 * k + 8, :], start=True, stop=False)
                    last = pe.matmul(pos_ps[k][:], cst[:, C_ONES:C_ONES + P], prev[:, 8 * k:8 * k + 8, :], start=False, stop=True)
                last.then_inc(counted, 1)
                for t in range(TILES):
                    pe.wait_ge(tok_ready, t + 1)
                    for k in range(TOPK):
                        last = pe.matmul(id_ps[:], at_pos[:, t, k, :], tok_e[t % 2][:, k, :],
                                         start=(t == 0 and k == 0), stop=(t == TILES - 1 and k == TOPK - 1))
                    last.then_inc(listed, 1)

            @block.vector
            def _(dve):
                n_chain = [0]

                def link(ins):
                    n_chain[0] += 1
                    ins.then_inc(chain, 1)
                    dve.wait_ge(chain, n_chain[0])
                tt = dve.tensor_tensor
                v = biased[:].rearrange("p t (g e) -> p (t g) e", g=NG)
                tt(hi[:], v[:, :, 0:4], v[:, :, 4:8], ALU.max)
                link(tt(lo[:], v[:, :, 0:4], v[:, :, 4:8], ALU.min))
                tt(hi2[:], hi[:, :, 0:2], hi[:, :, 2:4], ALU.max)
                tt(mi2[:], hi[:, :, 0:2], hi[:, :, 2:4], ALU.min)
                link(tt(lo2[:], lo[:, :, 0:2], lo[:, :, 2:4], ALU.max))
                link(tt(lo2[:], lo2[:], mi2[:], ALU.max))
                one = gs[:].rearrange("p t g -> p (t g)")
                two = g2[:].rearrange("p t g -> p (t g)")
                tt(one, hi2[:, :, 0], hi2[:, :, 1], ALU.max)
                tt(mi2[:, :, 0], hi2[:, :, 0], hi2[:, :, 1], ALU.min)
                link(tt(two, lo2[:, :, 0], lo2[:, :, 1], ALU.max))
                link(tt(two, two, mi2[:, :, 0], ALU.max))
                link(tt(one, one, two, ALU.add))
                mine = gs[:].unsqueeze(3).to_broadcast([P, TILES, NG, NG])
                other = gs[:].unsqueeze(2).to_broadcast([P, TILES, NG, NG])
                v1 = w1[:].rearrange("p t (g h) -> p t g h", g=NG)
                v2 = w2[:].rearrange("p t (g h) -> p t g h", g=NG)
                tt(v1, other, mine, ALU.is_gt)
                link(tt(v2, other, mine, ALU.is_equal))
                link(tt(w2[:], w2[:], cst[:, C_GT:C_GT + E].unsqueeze(1).to_broadcast([P, TILES, E]), ALU.mult))
                link(tt(w1[:], w1[:], w2[:], ALU.add))
                link(dve.tensor_reduce(g2[:], v1, AX.X, ALU.add))
                link(dve.tensor_scalar(g2[:], g2[:], float(TOPG), None, ALU.is_lt))
                link(tt(w1[:].rearrange("p t (g e) -> p (t g) e", g=NG), v,
                        g2[:].rearrange("p t g -> p (t g)").unsqueeze(2).to_broadcast([P, TILES * NG, E // NG]), ALU.mult))
                for t in range(TILES):
                    last = dve.max(top[:, t, :], w1[:, t, :])
                link(last)
                for t in range(TILES):
                    last = dve.match_replace(w2[:, t, :], top[:, t, :], w1[:, t, :], -3.0e38)
                link(last)
                link(tt(sel[:], w1[:], w2[:], ALU.not_equal))
                dve.memset(prev[:, 0, :], 0.0)
                link(dve.tensor_copy(prev[:, 1, :], sel[:, 0, :]))
                for t in range(2, TILES):
                    link(tt(prev[:, t, :], prev[:, t - 1, :], sel[:, t - 1, :], ALU.add))
                link(tt(w2[:], scores[:], sel[:], ALU.mult))
                dve.sem_inc(selected, 1)
                link(dve.tensor_reduce(s16[:], w2[:], AX.X, ALU.add))
                link(dve.tensor_scalar(s16[:], s16[:], 1e-20, None, ALU.add))
                link(dve.reciprocal(s16[:], s16[:]))
                link(dve.tensor_scalar(s16[:], s16[:], gat[:, 3:4], RSCALE, ALU.mult, ALU.mult))
                tt(w2[:], w2[:], s16[:].unsqueeze(2).to_broadcast([P, TILES, E]), ALU.mult).then_inc(gated, 1)
                dve.wait_ge(counted, 1)
                for k in range(2):
                    part = slice(8 * k, 8 * k + 8)
                    ps = pos_ps[k][:].rearrange("p (t e) -> p t e", e=E)
                    tt(w1[:, part, :], ps, cst[:, C_EB:C_EB + E].unsqueeze(1).to_broadcast([P, 8, E]), ALU.add)
                    link(dve.scalar_tensor_tensor(sel[:, part, :], ps, float(CAP), sel[:, part, :], ALU.is_lt, ALU.mult))
                link(tt(w1[:], w1[:], sel[:], ALU.mult))
                link(tt(sel[:], sel[:], cst[:, C_EB:C_EB + E].unsqueeze(1).to_broadcast([P, TILES, E]), ALU.mult))
                for t in range(TILES):
                    dve.max(top[:, t, :], w1[:, t, :])
                    last = dve.max(top_e[:, t, :], sel[:, t, :])
                link(last)
                link(tt(top[:], top[:], top_e[:], ALU.subtract))
                for t in range(TILES):
                    tt(at_pos[:, t], cst[:, C_POS:C_POS + CAP].unsqueeze(1).to_broadcast([P, TOPK, CAP]),
                       top[:, t, :].unsqueeze(2).to_broadcast([P, TOPK, CAP]), ALU.is_equal)
                    tt(at_e[:, t], cst[:, C_EB:C_EB + E].unsqueeze(1).to_broadcast([P, TOPK, E]),
                       top_e[:, t, :].unsqueeze(2).to_broadcast([P, TOPK, E]), ALU.is_equal).then_inc(hot, 1)
                dve.wait_ge(listed, TILES)
                link(dve.tensor_scalar(ide[:], id_ps[:], 0.0, cst[:, C_PAD:C_PAD + 1], ALU.is_equal, ALU.mult))
                link(dve.scalar_tensor_tensor(idv[:], id_ps[:], -1.0, ide[:], ALU.add, ALU.add))
                link(dve.tensor_copy(idT[:], idv[:]))


def experts(nc, ident, xg_dram, acc_dram, idT, wg, wu, wd, weights, load_expert):
    ROUNDS = E // NB
    with ExitStack() as ctx:
        m = Mem(nc, ctx, "e")
        xg = [m.sb(f"xg{b}", [P, XW]) for b in range(NB)]
        ys = [m.sb(f"ys{b}", [P, D]) for b in range(NY)]
        xT = [m.sb(f"xT{u}", [P, 2, P]) for u in range(2)]
        sg = [m.sb(f"sg{u}", [I1, P]) for u in range(2)]
        ha = [m.sb(f"ha{u}", [I1, P]) for u in range(2)]
        hb = [m.sb(f"hb{u}", [I1, P]) for u in range(2)]
        xT_ps = [m.ps(f"xT_ps{u}", [P, 2, P]) for u in range(2)]
        gu_ps = [m.ps(f"gu_ps{u}", [I1, 2, P]) for u in range(2)]
        y_ps = [m.ps(f"y_ps{u}", [P, D]) for u in range(2)]

        gathered = [m.sem(f"gathered{b}") for b in range(NB)]
        summed = [m.sem(f"summed{u}") for u in range(2)]
        xT_done = m.sem("xT_done")
        xT_copied = m.sem("xT_copied")
        gu_done = m.sem("gu_done")
        sig = m.sem("sig")
        hid = m.sem("hid")
        y_done = m.sem("y_done")
        y_out = m.sem("y_out")

        def over_experts(eng, step):
            for b in range(NB):
                step(b, 0, b)
            with eng.Fori(1, ROUNDS - 1) as r:
                for b in range(NB):
                    step(NB * r + b, r, b)
            for b in range(NB):
                step(E - NB + b, ROUNDS - 1, b)

        with nc.Block() as block:
            @block.gpsimd
            def _(pool):
                for n in range(E + LEAD):
                    if n < E:
                        wait(pool, y_out, n - NB + 1)
                        pool.indirect_dma_start(out=xg[n % NB][:], out_offset=None, in_=xg_dram,
                                                in_offset=bass.IndirectOffsetOnAxis(ap=idT[:, n:n + 1], axis=0),
                                                bounds_check=ROWS - 1, oob_is_err=True).then_inc(gathered[n % NB], 16)
                    if n >= LEAD:
                        e = n - LEAD
                        pool.wait_ge(y_out, e + 1)
                        wait(pool, summed[e % 2], 16 * (e // 2))
                        pool.indirect_dma_start(out=acc_dram[e % 2],
                                                out_offset=bass.IndirectOffsetOnAxis(ap=idT[:, e:e + 1], axis=0),
                                                in_=ys[e % NY][:], in_offset=None, bounds_check=ROWS - 1, oob_is_err=True,
                                                compute_op=ALU.add).then_inc(summed[e % 2], 16)
                for u in range(2):
                    pool.wait_ge(summed[u], 16 * E // 2)

            @block.sync
            def _(sp):
                def step(e, r, b):
                    if not isinstance(e, int) or e + NB < E:
                        sp.wait_ge(y_done, e + 1)
                        load_expert(sp, e + NB, b)
                over_experts(sp, step)

            @block.scalar
            def _(act):
                def step(e, r, b):
                    u = b % 2
                    act.wait_ge(xT_done, e + 1)
                    wait(act, gu_done, e - 1)
                    act.copy(xT[u][:], xT_ps[u][:]).then_inc(xT_copied, 1)
                    act.wait_ge(gu_done, e + 1)
                    wait(act, hid, 2 * e - 2)
                    act.activation(sg[u][:], gu_ps[u][:, 0, :], ACT.Sigmoid).then_inc(sig, 1)
                over_experts(act, step)

            @block.vector
            def _(dve):
                def leave(e, r, b):
                    dve.wait_ge(y_done, e + 1)
                    wait(dve, summed[b % 2], 8 * (e - b % 2) - 8 * NY + 16)
                    dve.tensor_scalar(ys[b % NY][:], y_ps[b % 2][:], xg[b][:, bass.ds(D + e, 1)], None, ALU.mult).then_inc(y_out, 1)

                def step(e, r, b):
                    u = b % 2
                    dve.wait_ge(sig, e + 1)
                    wait(dve, hid, 2 * e - 2)
                    dve.tensor_tensor(ha[u][:], sg[u][:], gu_ps[u][:, 0, :], ALU.mult).then_inc(hid, 1)
                    dve.wait_ge(hid, 2 * e + 1)
                    wait(dve, y_done, e - 1)
                    dve.tensor_tensor(hb[u][:], ha[u][:], gu_ps[u][:, 1, :], ALU.mult).then_inc(hid, 1)
                    if b:
                        leave(e - 1, r, b - 1)
                    elif not isinstance(e, int) or e > 0:
                        leave(e - 1, r - 1, NB - 1)
                over_experts(dve, step)
                leave(E - 1, ROUNDS - 1, NB - 1)

            @block.tensor
            def _(pe):
                def rows(e, r, b):
                    pe.wait_ge(gathered[b], 16 * (r + 1))
                    wait(pe, xT_copied, e - 1)
                    for k in range(2):
                        last = pe.transpose(xT_ps[b % 2][:, k, :], xg[b][:, P * k:P * k + P], ident)
                    last.then_inc(xT_done, 1)

                def down(e, b):
                    pe.wait_ge(hid, 2 * e + 2)
                    wait(pe, y_out, e - 1)
                    pe.matmul(y_ps[b % 2][:], hb[b % 2][:], wd[b][:], start=True, stop=True).then_inc(y_done, 1)

                def step(e, r, b):
                    u = b % 2
                    if b + 1 < NB:
                        rows(e + 1, r, b + 1)
                    elif not isinstance(e, int) or e + 1 < E:
                        rows(e + 1, r + 1, 0)
                    pe.wait_ge(xT_copied, e + 1)
                    pe.wait_ge(weights[b], 48 * (r + 1))
                    wait(pe, hid, 2 * e - 2)
                    for n, w in enumerate((wg, wu)):
                        for k in range(2):
                            last = pe.matmul(gu_ps[u][:, n, :], w[b][:, k, :], xT[u][:, k, :], start=(k == 0), stop=(k == 1))
                    last.then_inc(gu_done, 1)
                    if not isinstance(e, int) or e > 0:
                        down(e - 1, (b - 1) % NB)
                rows(0, 0, 0)
                over_experts(pe, step)
                down(E - 1, NB - 1)


def total(nc, out, acc_dram):
    with ExitStack() as ctx:
        m = Mem(nc, ctx, "f")
        part = [m.sb(f"part{u}", [P, TILES, D]) for u in range(2)]
        loaded = [m.sem(f"loaded{c}") for c in range(CHUNKS)]
        summed = m.sem("summed")
        stored = m.sem("stored")
        rows = out.rearrange("b s d -> (b s) d").rearrange("(n p) d -> p n d", p=P)
        with nc.Block() as block:
            def load(eng, u):
                for c in range(CHUNKS):
                    n = slice(QT * c, QT * c + QT)
                    eng.dma_start(part[u][:, n], acc_dram[u][0:TOK].rearrange("(n p) d -> p n d", p=P)[:, n]).then_inc(loaded[c], 16)

            @block.sync
            def _(sp):
                load(sp, 0)
                for c in range(CHUNKS):
                    n = slice(QT * c, QT * c + QT)
                    sp.wait_ge(summed, c + 1)
                    sp.dma_start(rows[:, n], part[0][:, n]).then_inc(stored, 16)
                sp.wait_ge(stored, 16 * CHUNKS)

            @block.scalar
            def _(act):
                load(act, 1)

            @block.vector
            def _(dve):
                for c in range(CHUNKS):
                    n = slice(QT * c, QT * c + QT)
                    dve.wait_ge(loaded[c], 32)
                    dve.tensor_tensor(part[0][:, n], part[0][:, n], part[1][:, n], ALU.add).then_inc(summed, 1)


_INS = ['x', 'ctx_512', 'g_xattn', 'g_ffn', 'L0_ffn_W_up', 'L0_ffn_W_gate', 'L0_ffn_W_down', 'L1_xattn_Wq', 'L1_xattn_w_kc_q',
        'L1_xattn_w_kc_kv', 'L1_xattn_W_qr', 'L1_xattn_W_kr', 'L1_xattn_Wo', 'L1_ffn_router_weight', 'L1_ffn_e_bias',
        'L1_ffn_w_gate', 'L1_ffn_w_up', 'L1_ffn_w_down', 'L1_ffn_sh_gate', 'L1_ffn_sh_up', 'L1_ffn_sh_down']


def kernel(**inputs):
    import concourse.bacc as bacc
    from concourse.bass_utils import run_bass_kernel_spmd as run

    nc = bacc.Bacc("TRN2", target_bir_lowering=False, num_devices=1)
    arrays = {f"in_{name}": np.ascontiguousarray(inputs[name]) for name in _INS}
    arrays["in_consts"] = constants()
    a = {name[3:]: nc.dram_tensor(name, v.shape, mybir.dt.from_np(v.dtype), kind="ExternalInput").ap() for name, v in arrays.items()}
    out = nc.dram_tensor("out_0", (B, S, D), F32, kind="ExternalOutput").ap()
    xg_dram = nc.dram_tensor("xg_dram", (ROWS, XW), F32, kind="Internal").ap()
    acc_dram = [nc.dram_tensor(f"acc{u}_dram", (ROWS, D), F32, kind="Internal").ap() for u in range(2)]
    program(nc, a, out, xg_dram, acc_dram)
    r = run(nc, [arrays], core_ids=[0])
    return r.results[0]["out_0"]
```

```python
import numpy as np

import concourse.bass as bass
from concourse import mybir
from contextlib import ExitStack

F32 = mybir.dt.float32
F16 = mybir.dt.float16
F32R = mybir.dt.float32r
U32 = mybir.dt.uint32
ALU = mybir.AluOpType
ACT = mybir.ActivationFunctionType
AX = mybir.AxisListType

P = 128
B, S, D = 32, 64, 256
TOK = B * S
TILES = TOK // P
T = 64
DC = 64
EPS_LN = 1e-5
KVH, G, HD = 8, 4, 8
DE = 1024
ME = DE // P
CH = 512
CHUNKS = TOK // CH
QT = CH // P
XS = 2048.0
H1, HK, DCQ = 16, 128, 192
HP = H1 // 2
QR = 2 * DCQ // P
E, I1, NG, TOPG, TOPK, CAP = 64, 88, 8, 4, 8, 128
RSCALE = 2.5
XB = 8
NY = 4
LEAD = 5
XW = D + E
ROWS = TOK + CAP

C_ID, C_ONES, C_TRI, C_KM, C_K1, C_CQ, C_SQ, C_CK, C_SK, C_GT, C_TOK, C_EB, C_POS, C_PAD = np.cumsum(
    [0, 128, 128, 128, 8, 1024, 192, 192, 64, 64, 64, 16, 64, 128]).tolist()
C_ALL = C_PAD + 1


def constants():
    def rope(length, dim):
        inv = (np.float32(1.0) / np.float32(10000.0) ** (np.arange(0, dim, 2, dtype=np.float32) / np.float32(dim))).astype(np.float32)
        f = np.arange(length, dtype=np.float32)[:, None] * inv[None, :]
        return np.repeat(np.sin(f), 2, axis=-1).astype(np.float32), np.repeat(np.cos(f), 2, axis=-1).astype(np.float32)
    c = np.zeros((P, C_ALL), np.float32)
    p = np.arange(P)
    c[:, C_ID:C_ID + P] = np.eye(P)
    c[:, C_ONES:C_ONES + P] = 1.0
    c[:, C_TRI:C_TRI + P] = p[:, None] < p[None, :]
    c[:, C_KM:C_KM + 8] = (p[:, None] % 64 // 8) == np.arange(8)[None, :]
    ones = np.zeros((8, 2, 8, 64), np.float32)
    for j in range(8):
        ones[j, :, j, :] = 1.0
    c[64:80, C_K1:C_K1 + 1024] = np.tile(ones.reshape(8, 1024), (2, 1))
    sin, cos = rope(S, DCQ)
    half = DCQ // 2
    low = np.where(p < half, p, p - half)
    for r, q in enumerate((low, low + half, np.where(p < 64, p + 32, p + 64))):
        c[:, C_CQ + r * 64:C_CQ + r * 64 + 64] = cos[:, q].T
        c[:, C_SQ + r * 64:C_SQ + r * 64 + 64] = np.where(q < half, -sin[:, q], sin[:, q]).T
    sin, cos = rope(T, DC)
    sin[:, :DC // 2] *= -1.0
    c[:, C_CK:C_CK + 64] = cos[p % 64]
    c[:, C_SK:C_SK + 64] = sin[p % 64]
    g = np.arange(NG)
    c[:, C_GT:C_GT + 64] = (g[None, :] < g[:, None]).astype(np.float32).reshape(1, 64)
    c[:, C_TOK:C_TOK + TILES] = p[:, None] + P * np.arange(TILES)[None, :] + 1.0
    c[:, C_EB:C_EB + E] = np.arange(1, E + 1)[None, :] * CAP
    c[:, C_POS:C_POS + CAP] = np.arange(CAP)[None, :]
    c[:, C_PAD] = TOK + p + 1.0
    return c


def wait(eng, sem, value):
    if not isinstance(value, int) or value > 0:
        eng.wait_ge(sem, value)


def over_tiles(eng, step, alone=2):
    for t in range(alone):
        step(t, t % 2)
    with eng.Fori(alone // 2, TILES // 2 - 1) as it:
        step(2 * it, 0)
        step(2 * it + 1, 1)
    for t in (TILES - 2, TILES - 1):
        step(t, t % 2)


def within(t, n=TILES):
    return not isinstance(t, int) or t < n


class Mem:

    def __init__(self, nc, ctx, stage):
        self.nc, self.ctx, self.stage = nc, ctx, stage

    def sb(self, name, shape, dt=F32):
        return self.ctx.enter_context(self.nc.sbuf_tensor(f"{self.stage}_{name}", shape, dt))

    def ps(self, name, shape, dt=F32):
        return self.ctx.enter_context(self.nc.psum_tensor(f"{self.stage}_{name}", shape, dt))

    def sem(self, name):
        return self.nc.alloc_semaphore(f"{self.stage}_{name}")


def program(nc, a, out, xg_dram, acc_dram):
    ctx = ExitStack()
    with ctx:
        g = Mem(nc, ctx, "g")
        cst = g.sb("cst", [P, C_ALL])
        x = g.sb("x", [P, TILES, D])
        gat = g.sb("gat", [P, 4])
        ln_mv = g.sb("ln_mv", [P, TILES, 2])
        ln_rs = g.sb("ln_rs", [P, TILES])
        ident = cst[:, C_ID:C_ID + P]
        with ExitStack() as both:
            w = Mem(nc, both, "b")
            kvr = w.sb("kvr", [P, B, DC])
            with ExitStack() as layer:
                w = Mem(nc, layer, "l0")
                ctxK = w.sb("ctxK", [P, TILES, P], F32R)
                ctxd = w.sb("ctxd", [P, B, DC])
                k_up = w.sb("k_up", [P, 2, DE], F16)
                k_gate = w.sb("k_gate", [P, 2, DE], F16)
                k_down = w.sb("k_down", [P, ME, D], F16)
                tern = w.sb("tern", [P, 3, 3])
                fsc = w.sb("fsc", [P, 4])
                prep(nc, a, 0, cst, x, gat, ident, ctxK, ctxd, k_up, k_gate, k_down, tern, fsc, None, None, None, kvr, ln_mv)
                inverse_std(nc, "i0", ln_mv, ln_rs)
                attention0(nc, cst, x, ln_mv, ln_rs, gat, ident, ctxK, ctxd)
                inverse_std(nc, "i1", ln_mv, ln_rs)
                ffn0(nc, x, ln_mv, ln_rs, ident, k_up, k_gate, k_down, fsc)
            with ExitStack() as layer:
                w = Mem(nc, layer, "l1")
                Cw = [w.sb(f"Cw{n}", [P, 2, HP, 2 * DCQ], F32R) for n in range(2)]
                NB = w.sb("NB", [P, HP, QR, P])
                VT = w.sb("VT", [P, HP, D])
                prep(nc, a, 1, cst, x, gat, ident, None, None, None, None, None, None, None, Cw, NB, VT, kvr, ln_mv)
                inverse_std(nc, "i2", ln_mv, ln_rs)
                attention1(nc, cst, x, ln_mv, ln_rs, gat, ident, Cw, NB, VT, kvr)
        inverse_std(nc, "i3", ln_mv, ln_rs)
        moe(nc, a, cst, x, ln_mv, ln_rs, gat, ident, out, xg_dram, acc_dram)


def by_pair(h, dst, src):
    src = src.rearrange("p u (s q) -> p u s q", s=2)
    first = dst[:, :, 0:2 * P].rearrange("p u (s q) -> p u s q", s=2)
    if h == 0:
        return [(first[:, :, :, 0:96], src)]
    return [(first[:, :, :, 96:P], src[:, :, :, 0:32]),
            (dst[:, :, 2 * P:3 * P].rearrange("p u (s q) -> p u s q", s=2), src[:, :, :, 32:96])]


def prep(nc, a, phase, cst, x, gat, ident, ctxK, ctxd, k_up, k_gate, k_down, tern, fsc, Cw, NB, VT, kvr, ln_mv):
    with ExitStack() as ctx:
        m = Mem(nc, ctx, f"p{phase}")
        if phase == 0:
            ctx_tok = m.sb("ctx_tok", [P, TILES, DC])
            w3 = [m.sb(n, [P, 2048]) for n in ("w_up", "w_gate", "w_down")]
            pos = m.sb("pos", [P, 2048], F16)
            q3 = [m.sb(n, [P, 2048], F16) for n in ("q_up", "q_gate", "q_down")]
            identh = m.sb("identh", [P, P], F16)
            rot = m.sb("rot", [P, B, DC])
            part = m.sb("part", [P, 3])
            stats = m.sb("stats", [P, TILES, 6])
            graw = m.sb("graw", [P, 4])
        else:
            wq = m.sb("wq", [P, H1, D])
            wcq = m.sb("wcq", [P, H1, DCQ])
            wck = m.sb("wck", [P, H1, DC])
            wqr = m.sb("wqr", [96, H1, 2, 64])
            wkr = m.sb("wkr", [64, H1, 64])
            wo = m.sb("wo", [P, 2, 2048])
            qrT = m.sb("qrT", [P, HP, 2 * DCQ])
            krT = m.sb("krT", [P, HP, P])
            woT = wq
        banks = [m.ps(f"bank{n}", [P, 512]) for n in range(8)]

        loaded = {n: m.sem(f"ld_{n}") for n in (("cst", "ctx", "ctxd", "w0", "w1", "w2", "g", "x") if phase == 0 else
                                                  ("wq", "wcq", "wck", "wqr", "wkr", "wo"))}
        done = m.sem("done")
        act_out = m.sem("act_out")
        dve_out = m.sem("dve_out")
        zeroed = m.sem("zeroed")
        if phase == 0:
            absum = m.sem("absum")
            quant = m.sem("quant")
            chain = m.sem("dve_chain")
            pchain = m.sem("pool_chain")
            gats = m.sem("gats")

        if phase == 0:
            jobs = [(kind, n) for n in range(4) for kind in ("ctx", "ctxl")] + [("sum", 0), ("up", 0), ("up", 1), ("gate", 0), ("gate", 1), ("down", 0), ("down", 1)]
        else:
            jobs = [("qr", n) for n in range(HP)] + [(kind, n) for n in range(H1) for kind in ("C", "Cl")] + [("kr", 0)]
            jobs += [("wo", n) for n in range(HP)] + [("N", n) for n in range(HP)] + [("V", n) for n in range(HP)]
        at = {j: n for n, j in enumerate(jobs)}

        def copied_out(eng, n):
            wait(eng, act_out, n // 2 + 1)
            wait(eng, dve_out, (n + 1) // 2)

        def copy_out(copy, job, bank, sem):
            kind, n = job
            if kind == "ctx":
                copy(ctxK[0:64, 4 * n:4 * n + 4, :], bank[0:64, :]).then_inc(sem, 1)
            elif kind == "qr":
                for h in range(2):
                    rows = slice(64 * h, 64 * h + 64)
                    for dst, src in by_pair(h, qrT[rows, n, :].unsqueeze(1), bank[0:64, 192 * h:192 * h + 192].unsqueeze(1)):
                        last = copy(dst, src)
                last.then_inc(sem, 1)
            elif kind == "kr":
                for h in range(2):
                    rows = slice(64 * h, 64 * h + 64)
                    last = copy(krT[rows, :, 64 * h:64 * h + 64], bank[rows, :].rearrange("p (n c) -> p n c", n=HP))
                last.then_inc(sem, 1)
            elif kind == "C":
                for dst, src in by_pair(n % 2, Cw[0][:, :, n // 2, :], bank[:, 0:2 * DCQ].rearrange("p (u q) -> p u q", u=2)):
                    last = copy(dst, src)
                last.then_inc(sem, 1)
            elif kind == "wo":
                copy(woT[:, 2 * n:2 * n + 2, :], bank[:]).then_inc(sem, 1)
            elif kind == "N":
                copy(NB[:, n, :, :], bank[:, 0:QR * P]).then_inc(sem, 1)
            elif kind == "V":
                copy(VT[:, n, :], bank[:, 0:D]).then_inc(sem, 1)
            elif kind in ("up", "gate"):
                copy((k_up if kind == "up" else k_gate)[:, n, :], bank[:].bitcast(F16)).then_inc(sem, 1)
            elif kind == "down":
                copy(k_down[:, :, P * n:P * n + P], bank[:].bitcast(F16).rearrange("p (m i) -> p m i", m=ME)).then_inc(sem, 1)
            elif kind == "sum":
                copy(tern[:, :, 0], bank[:, 0:3]).then_inc(sem, 1)

        with nc.Block() as block:
            @block.sync
            def _(sp):
                def load(dst, src, name):
                    sp.dma_start(dst, src).then_inc(loaded[name], 16)
                if phase == 0:
                    load(cst[:], a["consts"], "cst")
                    load(ctx_tok[:], a["ctx_512"].rearrange("(n b) t d -> (b t) n d", b=2), "ctx")
                    for h in range(2):
                        load(ctxd[64 * h:64 * h + 64], a["ctx_512"].rearrange("b t d -> t b d"), "ctxd")
                    return
                load(wqr[:], a["L1_xattn_W_qr"].rearrange("h (u q) r -> q h u r", u=2), "wqr")
                load(wkr[:], a["L1_xattn_W_kr"].rearrange("h c r -> c h r"), "wkr")
                load(wq[:], a["L1_xattn_Wq"].rearrange("(h k) d -> k h d", h=H1), "wq")
                load(wcq[:], a["L1_xattn_w_kc_q"].rearrange("h k q -> k h q"), "wcq")
                load(wo[:], a["L1_xattn_Wo"].rearrange("(u i) k -> i u k", u=2), "wo")
                load(wck[:], a["L1_xattn_w_kc_kv"].rearrange("h k c -> k h c"), "wck")

            @block.scalar
            def _(act):
                if phase == 0:
                    for k, name in enumerate(("L0_ffn_W_up", "L0_ffn_W_gate", "L0_ffn_W_down")):
                        act.dma_start(w3[k][:], a[name].rearrange("(u p) d -> p u d", p=P)).then_inc(loaded[f"w{k}"], 16)
                    act.dma_start(graw[:, 0:2], a["g_xattn"].rearrange("(o g) -> o g", o=1).to_broadcast([P, 2])).then_inc(loaded["g"], 16)
                    act.dma_start(graw[:, 2:4], a["g_ffn"].rearrange("(o g) -> o g", o=1).to_broadcast([P, 2])).then_inc(loaded["g"], 16)
                    act.dma_start(x[:], a["x"].rearrange("b s d -> (b s) d").rearrange("(n p) d -> p n d", p=P)).then_inc(loaded["x"], 16)
                    act.wait_ge(loaded["g"], 32)
                    act.activation(gat[:], graw[:], ACT.Tanh).then_inc(gats, 1)
                act.wait_ge(zeroed, 1 if phase == 0 else 2)
                for n in range(0, len(jobs), 2):
                    act.wait_ge(done, n + 1)
                    copy_out(act.copy, jobs[n], banks[n % 8], act_out)

            @block.gpsimd
            def _(pool):
                if phase == 1:
                    for w in (qrT, krT):
                        pool.memset(w[:], 0.0).then_inc(zeroed, 1)
                    return
                pool.wait_ge(loaded["cst"], 16)
                pool.wait_ge(loaded["ctxd"], 32)
                pool.tensor_copy(identh[:], ident).then_inc(zeroed, 1)
                half = DC // 2
                sin = cst[:, C_SK:C_SK + DC].unsqueeze(1)
                pool.tensor_tensor(rot[:, :, 0:half], ctxd[:, :, half:DC], sin[:, :, 0:half].to_broadcast([P, B, half]), ALU.mult)
                pool.tensor_tensor(rot[:, :, half:DC], ctxd[:, :, 0:half], sin[:, :, half:DC].to_broadcast([P, B, half]), ALU.mult)
                pool.tensor_tensor(kvr[:], ctxd[:], cst[:, C_CK:C_CK + DC].unsqueeze(1).to_broadcast([P, B, DC]), ALU.mult).then_inc(pchain, 1)
                pool.wait_ge(pchain, 1)
                pool.tensor_tensor(kvr[:], kvr[:], rot[:], ALU.add).then_inc(pchain, 1)
                pool.wait_ge(pchain, 2)
                pool.wait_ge(loaded["x"], 16)

            @block.vector
            def _(dve):
                n_chain = [0]

                def link(ins):
                    n_chain[0] += 1
                    ins.then_inc(chain, 1)
                    dve.wait_ge(chain, n_chain[0])

                if phase == 1:
                    dve.wait_ge(zeroed, 2)
                    for n in range(1, len(jobs), 2):
                        kind, k = jobs[n]
                        if kind == "Cl":
                            dve.wait_ge(act_out, n // 2 + 1)
                            high = Cw[0][:, :, k // 2, :].bitcast(F32)
                            prod = banks[(n - 1) % 8][:, 0:2 * DCQ].rearrange("p (u q) -> p u q", u=2)
                            for (dst, src), (lead, _) in zip(by_pair(k % 2, Cw[1][:, :, k // 2, :], prod), by_pair(k % 2, high, prod)):
                                last = dve.tensor_tensor(dst, src, lead, ALU.subtract)
                            last.then_inc(dve_out, 1)
                        else:
                            dve.wait_ge(done, n + 1)
                            copy_out(dve.tensor_copy, jobs[n], banks[n % 8], dve_out)
                    return
                for k in range(3):
                    dve.wait_ge(loaded[f"w{k}"], 16)
                    dve.tensor_reduce(part[:, k:k + 1], w3[k][:], AX.X, ALU.add, apply_absolute_value=True).then_inc(absum, 1)

                def quantise():
                    dve.wait_ge(act_out, at["sum", 0] // 2 + 1)
                    link(dve.tensor_scalar(tern[:, :, 0], tern[:, :, 0], 1.0 / (DE * D), 1e-8, ALU.mult, ALU.add))
                    dve.tensor_scalar(tern[:, :, 1], tern[:, :, 0], 0.5, None, ALU.mult)
                    link(dve.tensor_scalar(tern[:, :, 2], tern[:, :, 0], -0.5, None, ALU.mult))
                    for k in range(3):
                        wait(dve, quant, k)
                        link(dve.tensor_scalar(pos[:], w3[k][:], tern[:, k, 2:3], None, ALU.is_lt))
                        dve.scalar_tensor_tensor(q3[k][:], w3[k][:], tern[:, k, 1:2], pos[:], ALU.is_gt, ALU.subtract).then_inc(quant, 1)
                    dve.wait_ge(gats, 1)
                    dve.tensor_scalar(fsc[:, 0:1], tern[:, 0, 0:1], 1.0 / XS, None, ALU.mult)
                    link(dve.tensor_scalar(fsc[:, 3:4], tern[:, 0, 0:1], 4.0 * XS, None, ALU.mult))
                    link(dve.reciprocal(fsc[:, 1:2], fsc[:, 3:4]))
                    link(dve.tensor_tensor(fsc[:, 2:3], tern[:, 0, 0:1], tern[:, 1, 0:1], ALU.mult))
                    link(dve.tensor_tensor(fsc[:, 3:4], tern[:, 2, 0:1], gat[:, 2:3], ALU.mult))
                    link(dve.tensor_tensor(fsc[:, 2:3], fsc[:, 2:3], fsc[:, 3:4], ALU.mult))
                    link(dve.tensor_scalar(fsc[:, 2:3], fsc[:, 2:3], 4.0, None, ALU.mult))

                dve.wait_ge(loaded["x"], 16)
                for t in range(TILES):
                    dve.bn_stats(stats[:, t, :], x[:, t, :]).then_inc(chain, 1)
                n_chain[0] += TILES
                dve.wait_ge(chain, n_chain[0])
                for t in range(TILES):
                    dve.bn_aggr(ln_mv[:, t, :], stats[:, t, :])
                dve.wait_ge(zeroed, 1 if phase == 0 else 2)
                for n in range(1, len(jobs), 2):
                    kind, k = jobs[n]
                    if kind == "ctxl":
                        dve.wait_ge(act_out, n // 2 + 1)
                        four = slice(4 * k, 4 * k + 4)
                        dve.tensor_tensor(ctxK[64:P, four, :], banks[(n - 1) % 8][0:64, :].rearrange("p (n c) -> p n c", n=4),
                                          ctxK[0:64, four, :].bitcast(F32), ALU.subtract).then_inc(dve_out, 1)
                    else:
                        dve.wait_ge(done, n + 1)
                        copy_out(dve.tensor_copy, jobs[n], banks[n % 8], dve_out)
                    if n == at["sum", 0] - 1:
                        quantise()

            @block.tensor
            def _(pe):
                if phase == 0:
                    pe.wait_ge(loaded["cst"], 16)
                pe.wait_ge(zeroed, 1 if phase == 0 else 2)
                for n, (kind, k) in enumerate(jobs):
                    bank = banks[n % 8]
                    if kind in ("Cl", "ctxl"):
                        continue
                    if n >= 8:
                        copied_out(pe, n - 7)
                    if kind == "ctx":
                        pe.wait_ge(loaded["ctx"], 16)
                        for q in range(4):
                            last = pe.transpose(bank[0:64, P * q:P * q + P], ctx_tok[:, 4 * k + q, :], ident)
                    elif kind == "sum":
                        pe.wait_ge(absum, 3)
                        last = pe.matmul(bank[:, 0:3], cst[:, C_ONES:C_ONES + P], part[:], start=True, stop=True)
                    elif kind == "qr":
                        pe.wait_ge(loaded["wqr"], 16)
                        for h in range(2):
                            for u in range(2):
                                c = 192 * h + 96 * u
                                last = pe.transpose(bank[0:64, c:c + 96], wqr[:, 2 * k + h, u, :], ident[0:96, 0:96])
                    elif kind == "kr":
                        pe.wait_ge(loaded["wkr"], 16)
                        for hp in range(HP):
                            last = pe.transpose(bank[:, 64 * hp:64 * hp + 64],
                                                wkr[:, 2 * hp:2 * hp + 2, :].rearrange("c h r -> c (h r)"), ident[0:64, 0:64])
                    elif kind == "C":
                        pe.wait_ge(loaded["wq"], 16)
                        pe.wait_ge(loaded["wcq"], 16)
                        for u in range(2):
                            last = pe.matmul(bank[:, DCQ * u:DCQ * u + DCQ], wq[:, k, P * u:P * u + P], wcq[:, k, :], start=True, stop=True)
                    elif kind == "wo":
                        pe.wait_ge(loaded["wo"], 16)
                        for h in range(2):
                            for u in range(2):
                                c = D * h + P * u
                                last = pe.transpose(bank[:, c:c + P], wo[:, u, P * (2 * k + h):P * (2 * k + h) + P], ident)
                    elif kind == "N":
                        copied_out(pe, max(at["qr", k], at["kr", 0]))
                        for r in range(QR):
                            last = pe.matmul(bank[:, P * r:P * r + P], qrT[:, k, P * r:P * r + P], krT[:, k, :], start=True, stop=True)
                    elif kind == "V":
                        copied_out(pe, at["wo", k])
                        pe.wait_ge(loaded["wck"], 16)
                        for h in range(2):
                            last = pe.matmul(bank[64 * h:64 * h + 64, 0:D], wck[:, 2 * k + h, :], woT[:, 2 * k + h, :], start=True, stop=True)
                    elif kind in ("up", "gate"):
                        pe.wait_ge(quant, {"up": 1, "gate": 2}[kind])
                        src = q3[{"up": 0, "gate": 1}[kind]][:].rearrange("p (u d) -> p u d", u=ME)
                        for u in range(ME):
                            last = pe.transpose(bank[:].bitcast(F16)[:, P * u:P * u + P], src[:, u, P * k:P * k + P], identh[:])
                    elif kind == "down":
                        pe.wait_ge(quant, 3)
                        for u in range(ME):
                            last = pe.transpose(bank[:].bitcast(F16)[:, P * u:P * u + P],
                                                q3[2][:, DE * k + P * u:DE * k + P * u + P], identh[:])
                    last.then_inc(done, 2 if kind in ("C", "ctx") else 1)


def inverse_std(nc, stage, ln_mv, ln_rs):
    with ExitStack() as ctx:
        m = Mem(nc, ctx, stage)
        ve = m.sb("ve", [P, TILES])
        root = m.sb("root", [P, TILES])
        tmp = m.sb("tmp", [P, TILES])
        ve_ready = m.sem("ve_ready")
        rooted = m.sem("rooted")
        newton = m.sem("newton")
        with nc.Block() as block:
            @block.scalar
            def _(act):
                act.wait_ge(ve_ready, 1)
                act.activation(root[:], ve[:], ACT.Sqrt).then_inc(rooted, 1)

            @block.vector
            def _(dve):
                dve.tensor_scalar(ve[:], ln_mv[:, :, 1], EPS_LN, None, ALU.add).then_inc(ve_ready, 1)
                dve.wait_ge(rooted, 1)
                dve.reciprocal(ln_rs[:], root[:]).then_inc(newton, 1)
                dve.wait_ge(newton, 1)
                dve.tensor_tensor(tmp[:], ln_rs[:], ln_rs[:], ALU.mult).then_inc(newton, 1)
                dve.wait_ge(newton, 2)
                dve.tensor_tensor(tmp[:], tmp[:], ve[:], ALU.mult).then_inc(newton, 1)
                dve.wait_ge(newton, 3)
                dve.tensor_scalar(tmp[:], tmp[:], -0.5, 1.5, ALU.mult, ALU.add).then_inc(newton, 1)
                dve.wait_ge(newton, 4)
                dve.tensor_tensor(ln_rs[:], ln_rs[:], tmp[:], ALU.mult).then_inc(newton, 1)
                dve.wait_ge(newton, 5)


def add_and_count(dve, t, n, y, scale, x, xt, st, mv, ln_mv, added):
    dve.scalar_tensor_tensor(xt[:], y, scale, x[:, t, :], ALU.mult, ALU.add).then_inc(added, 1)
    dve.wait_ge(added, 4 * n + 1)
    dve.bn_stats(st[:], xt[:]).then_inc(added, 1)
    dve.wait_ge(added, 4 * n + 2)
    dve.tensor_scalar(x[:, t, :], xt[:], 1.0, None, ALU.mult)
    dve.bn_aggr(mv[:], st[:]).then_inc(added, 1)
    dve.wait_ge(added, 4 * n + 3)
    dve.tensor_scalar(ln_mv[:, t, :], mv[:], 1.0, None, ALU.mult).then_inc(added, 1)


def attention0(nc, cst, x, ln_mv, ln_rs, gat, ident, ctxK, ctxd):
    with ExitStack() as ctx:
        m = Mem(nc, ctx, "a")
        xn = [m.sb(f"xn{u}", [P, G, 2, 64]) for u in range(2)]
        st = m.sb("st", [P, 6])
        mv = m.sb("mv", [P, 2])
        xt = m.sb("xt", [P, D])
        q1 = [m.sb(f"q1_{u}", [P, 2, G, S], F32R) for u in range(2)]
        q2 = [m.sb(f"q2_{u}", [80, 2, G, S], F32R) for u in range(2)]
        k1 = [m.sb(f"k1_{u}", [P, 2, KVH, T], F32R) for u in range(2)]
        k2 = [m.sb(f"k2_{u}", [80, 2, KVH, T], F32R) for u in range(2)]
        vB = [m.sb(f"vB{u}", [P, 2, 4, 2, 16]) for u in range(2)]
        pr = [m.sb(f"pr{u}", [P, 2, 4, G, S]) for u in range(2)]
        mx = m.sb("mx", [P, 4, KVH])
        ms = m.sb("ms", [P, 4, 2 * KVH], F32R)
        oT = m.sb("oT", [P, G, 2, S])
        rden = m.sb("rden", [P, G, KVH])
        att = m.sb("att", [P, D])
        q_ps = m.ps("q_ps", [P, G, P])
        m_ps = [m.ps(f"m_ps{n}", [P, 512]) for n in range(2)]
        mT_ps = m.ps("mT_ps", [2 * KVH, 4, P])
        s_ps = [m.ps(f"s_ps{n}", [P, 512]) for n in range(2)]
        oT_ps = m.ps("oT_ps", [P, 2, G * S])
        o_ps = m.ps("o_ps", [P, G, KVH, 16])
        SC = float(HD) ** -0.5

        xn_ready = m.sem("xn_ready")
        q_done = m.sem("q_done")
        q_lead = m.sem("q_lead")
        q_rest = m.sem("q_rest")
        k_ready = m.sem("k_ready")
        k_copied = m.sem("k_copied")
        v_ready = m.sem("v_ready")
        scored = m.sem("scored")
        maxed = m.sem("maxed")
        split = m.sem("split")
        mT_done = m.sem("mT_done")
        mT_copied = m.sem("mT_copied")
        sT_done = m.sem("sT_done")
        exped = m.sem("exped")
        pv_done = m.sem("pv_done")
        oT_copied = m.sem("oT_copied")
        o_done = m.sem("o_done")
        nrm = m.sem("nrm")
        added = m.sem("added")
        init = m.sem("init")

        with nc.Block() as block:
            @block.gpsimd
            def _(pool):
                for u in range(2):
                    pool.memset(vB[u][:], 0.0).then_inc(init, 1)
                pool.wait_ge(init, 2)
                for u in range(2):
                    for h in range(2):
                        pool.memset(vB[u][64 * h:64 * h + 64, :, :, h, HD:HD + 1], 1.0).then_inc(init, 1)
                    pool.tensor_copy(k2[u][64:80], cst[64:80, C_K1:C_K1 + 1024]).then_inc(init, 1)
                pool.wait_ge(init, 8)

                def keys(t, u):
                    for b in range(2):
                        wait(pool, sT_done, 4 * t - 6 + 2 * b)
                        wait(pool, k_copied, 2 * t - 3 + b)
                        src = ctxK[:, t, T * b:T * b + T].bitcast(F32).unsqueeze(1).to_broadcast([P, KVH, T])
                        mask = cst[:, C_KM:C_KM + 8].unsqueeze(2).to_broadcast([P, KVH, T])
                        pool.tensor_tensor(k1[u][:, b], src, mask, ALU.mult).then_inc(k_ready, 1)

                def values(t, u):
                    wait(pool, pv_done, t - 1)
                    for h in range(2):
                        rows = slice(64 * h, 64 * h + 64)
                        for b in range(2):
                            src = ctxd[rows, 2 * t + b, :].rearrange("p (n h d) -> p n h d", n=4, h=2)[:, :, h, :]
                            last = pool.tensor_copy(vB[u][rows, b, :, h, 0:HD], src)
                    last.then_inc(v_ready, 1)

                def step(t, u):
                    if within(t + 2):
                        pool.wait_ge(v_ready, t + 1)
                        keys(t + 2, u)
                    if within(t + 1):
                        pool.wait_ge(k_ready, 2 * t + 6 if within(t + 2) else 2 * TILES)
                        values(t + 1, 1 - u)
                keys(0, 0)
                keys(1, 1)
                pool.wait_ge(k_ready, 4)
                values(0, 0)
                over_tiles(pool, step, 4)

            @block.vector
            def _(dve):
                def norm(t, u):
                    wait(dve, q_done, t - 1)
                    for k in range(2):
                        last = dve.tensor_scalar(xn[u][:, :, k, :].rearrange("p g (j d) -> p j g d", j=KVH), x[:, t, :].rearrange("p (j g d) -> p j g d", j=KVH, g=G),
                                                 ln_mv[:, t, 0:1], ln_rs[:, bass.ds(t, 1)], ALU.subtract, ALU.mult)
                    last.then_inc(xn_ready, 1)

                def rest(t, u):
                    dve.wait_ge(q_lead, t + 1)
                    wait(dve, sT_done, 4 * t - 4)
                    dve.tensor_tensor(q2[u][0:64].rearrange("p b g s -> p g b s"), q_ps[0:64].rearrange("p g (b s) -> p g b s", b=2),
                                      q1[u][0:64].bitcast(F32).rearrange("p b g s -> p g b s"), ALU.subtract).then_inc(q_rest, 1)

                def maxima(t, u):
                    wait(dve, split, 2 * t)
                    for n in range(4):
                        dve.wait_ge(scored, 4 * t + n + 1)
                        dve.tensor_reduce(mx[:, n, :], m_ps[n % 2][:].rearrange("p (j t) -> p j t", j=KVH), AX.X, ALU.max).then_inc(maxed, 1)
                        if n == 1 and (not isinstance(t, int) or 0 < t < TILES - 1):
                            norm(t + 1, 1 - u)
                    dve.wait_ge(maxed, 4 * t + 4)
                    wait(dve, mT_done, 1 * t)
                    dve.tensor_scalar(ms[:, :, 0:KVH], mx[:], -1.0, None, ALU.mult).then_inc(split, 1)
                    dve.wait_ge(split, 2 * t + 1)
                    dve.scalar_tensor_tensor(ms[:, :, KVH:2 * KVH], mx[:], -1.0, ms[:, :, 0:KVH].bitcast(F32), ALU.mult, ALU.subtract).then_inc(split, 1)

                def output(t):
                    wait(dve, added, 4 * t)
                    dve.wait_ge(o_done, t + 1)
                    dve.reciprocal(rden[:], o_ps[:, :, :, HD]).then_inc(nrm, 1)
                    dve.wait_ge(nrm, 2 * t + 1)
                    dve.tensor_tensor(att[:].rearrange("p (j g d) -> p g j d", j=KVH, g=G), o_ps[:, :, :, 0:HD],
                                      rden[:].unsqueeze(3).to_broadcast([P, G, KVH, HD]), ALU.mult).then_inc(nrm, 1)

                def add(t):
                    dve.wait_ge(nrm, 2 * t + 2)
                    add_and_count(dve, t, t, att[:], gat[:, 0:1], x, xt, st, mv, ln_mv, added)

                def step(t, u):
                    if within(t + 1):
                        maxima(t + 1, 1 - u)
                    if not isinstance(t, int) or t > 1:
                        output(t - 2)
                    if within(t + 2):
                        rest(t + 2, u)
                    if not isinstance(t, int) or t > 1:
                        add(t - 2)
                norm(0, 0)
                norm(1, 1)
                rest(0, 0)
                rest(1, 1)
                maxima(0, 0)
                over_tiles(dve, step, 4)
                for t in (TILES - 2, TILES - 1):
                    output(t)
                    add(t)

            @block.scalar
            def _(act):
                def lead(t, u):
                    act.wait_ge(q_done, t + 1)
                    wait(act, sT_done, 4 * t - 4)
                    act.copy(q1[u][:].rearrange("p b g s -> p g b s"), q_ps[:].rearrange("p g (b s) -> p g b s", b=2)).then_inc(q_lead, 1)

                def keys(t, u, b):
                    act.wait_ge(k_ready, 2 * t + b + 1)
                    wait(act, sT_done, 4 * t - 6 + 2 * b)
                    act.copy(k2[u][0:64, b], k1[u][0:64, b].bitcast(F32)).then_inc(k_copied, 1)

                def maximum(t, u):
                    act.wait_ge(mT_done, t + 1)
                    wait(act, sT_done, 4 * t - 4)
                    act.copy(q2[u][64:80], mT_ps[:]).then_inc(mT_copied, 1)

                def output(t):
                    act.wait_ge(pv_done, t + 1)
                    wait(act, o_done, 1 * t)
                    act.copy(oT[:].rearrange("p g b s -> p b g s"), oT_ps[:].rearrange("p b (g s) -> p b g s", g=G)).then_inc(oT_copied, 1)

                def step(t, u):
                    wait(act, pv_done, t - 1)
                    for n in range(4):
                        act.wait_ge(sT_done, 4 * t + n + 1)
                        act.activation(pr[u][:, n // 2, 2 * (n % 2):2 * (n % 2) + 2], s_ps[n % 2][:], ACT.Exp, scale=SC).then_inc(exped, 1)
                    if not isinstance(t, int) or t > 0:
                        output(t - 1)
                    if within(t + 2):
                        lead(t + 2, u)
                    if within(t + 1):
                        maximum(t + 1, 1 - u)
                    if within(t + 2):
                        keys(t + 2, u, 0)
                        keys(t + 2, u, 1)
                lead(0, 0)
                lead(1, 1)
                for t in range(2):
                    for b in range(2):
                        keys(t, t, b)
                maximum(0, 0)
                over_tiles(act, step, 4)
                output(TILES - 1)

            @block.tensor
            def _(pe):
                def queries(t, u):
                    pe.wait_ge(xn_ready, t + 1)
                    wait(pe, q_lead, 1 * t)
                    wait(pe, q_rest, 1 * t)
                    for g in range(G):
                        last = pe.transpose(q_ps[:, g, :], xn[u][:, g].rearrange("p c f -> p (c f)"), ident)
                    last.then_inc(q_done, 1)

                def score(t, u, n):
                    if n == 0:
                        pe.wait_ge(q_lead, t + 1)
                        pe.wait_ge(q_rest, t + 1)
                    wait(pe, maxed, 4 * t + n - 1)
                    if n % 2 == 0:
                        pe.wait_ge(k_copied, 2 * t + n // 2 + 1)
                    b, g = n // 2, slice(2 * (n % 2), 2 * (n % 2) + 2)
                    pe.matmul(m_ps[n % 2][:], q1[u][:, b, g, :], k1[u][:, b], start=True, stop=False)
                    pe.matmul(m_ps[n % 2][:], q2[u][0:64, b, g, :], k2[u][0:64, b], start=False, stop=True).then_inc(scored, 1)

                def maximum(t, u):
                    pe.wait_ge(split, 2 * t + 2)
                    wait(pe, mT_copied, 1 * t)
                    for n in range(4):
                        last = pe.transpose(mT_ps[:, n, :], ms[:, n, :].bitcast(F32), ident)
                    last.then_inc(mT_done, 1)

                def score_less_maximum(t, u, n):
                    pe.wait_ge(mT_copied, t + 1)
                    wait(pe, exped, 4 * t + n - 1)
                    b = n // 2
                    for k in range(2):
                        jp = 2 * (n % 2) + k
                        dst = s_ps[n % 2][:, 256 * k:256 * k + 256]
                        pe.matmul(dst, k1[u][:, b, 2 * jp:2 * jp + 2, :], q1[u][:, b], start=True, stop=False)
                        last = pe.matmul(dst, k2[u][:, b, 2 * jp:2 * jp + 2, :], q2[u][:, b], start=False, stop=True)
                    last.then_inc(sT_done, 1)

                def values(t, u):
                    pe.wait_ge(exped, 4 * t + 4)
                    pe.wait_ge(v_ready, t + 1)
                    wait(pe, oT_copied, 1 * t)
                    for b in range(2):
                        for jp in range(4):
                            last = pe.matmul(oT_ps[32 * jp:32 * jp + 32, b, :], vB[u][:, b, jp].rearrange("p h d -> p (h d)"), pr[u][:, b, jp], start=True, stop=True)
                    last.then_inc(pv_done, 1)

                def output(t):
                    pe.wait_ge(oT_copied, t + 1)
                    wait(pe, nrm, 2 * t)
                    for g in range(G):
                        last = pe.transpose(o_ps[:, g].rearrange("p j d -> p (j d)"), oT[:, g].rearrange("p b s -> p (b s)"), ident)
                    last.then_inc(o_done, 1)

                def step(t, u):
                    for ahead, banks in ((1, (0, 1)), (0, (0, 1)), (1, (2,)), (0, (2,)), (1, (3,)), (0, (3,))):
                        for n in banks:
                            if ahead == 0:
                                score_less_maximum(t, u, n)
                            elif within(t + 1):
                                score(t + 1, 1 - u, n)
                        if ahead == 0 and n == 1 and (not isinstance(t, int) or t > 1):
                            output(t - 2)
                    if not isinstance(t, int) or t > 0:
                        values(t - 1, 1 - u)
                    if within(t + 2):
                        queries(t + 2, u)
                    if within(t + 1):
                        maximum(t + 1, 1 - u)
                queries(0, 0)
                queries(1, 1)
                for n in range(4):
                    score(0, 0, n)
                maximum(0, 0)
                over_tiles(pe, step, 4)
                output(TILES - 2)
                values(TILES - 1, 1)
                output(TILES - 1)


def normalise_chunk(dve, c, x, ln_mv, ln_rs, xn, xn_ready):
    for q in range(QT):
        t = QT * c + q
        last = dve.tensor_scalar(xn[:, q, :], x[:, t, :], ln_mv[:, t, 0:1], ln_rs[:, bass.ds(t, 1)], ALU.subtract, ALU.mult)
    last.then_inc(xn_ready, 1)


def over_chunks(eng, step):
    step(0)
    with eng.Fori(1, CHUNKS - 1) as c:
        step(c)
    step(CHUNKS - 1)


def ffn0(nc, x, ln_mv, ln_rs, ident, k_up, k_gate, k_down, fsc):
    with ExitStack() as ctx:
        m = Mem(nc, ctx, "f")
        st = m.sb("st", [P, 6])
        mv = m.sb("mv", [P, 2])
        xt = m.sb("xt", [P, D])
        xn = m.sb("xn", [P, QT, D])
        xh = m.sb("xh", [P, 2, CH], F16)
        xl = m.sb("xl", [P, 2, CH], F16)
        sg = [m.sb(f"sg{n}", [P, CH]) for n in range(2)]
        h = [m.sb(f"h{n}", [P, CH]) for n in range(2)]
        hh = m.sb("hh", [P, ME, CH], F16)
        hl = m.sb("hl", [P, ME, CH], F16)
        xT_ps = m.ps("xT_ps", [P, 2, CH])
        u_ps = [m.ps(f"u_ps{n}", [P, CH]) for n in range(2)]
        g_ps = [m.ps(f"g_ps{n}", [P, CH]) for n in range(2)]
        d_ps = [m.ps(f"d_ps{n}", [P, D]) for n in range(2)]

        xn_ready = m.sem("xn_ready")
        xT_done = m.sem("xT_done")
        xh_done = m.sem("xh_done")
        xl_done = m.sem("xl_done")
        u_done = m.sem("u_done")
        g_done = m.sem("g_done")
        silu = m.sem("silu")
        h_done = m.sem("h_done")
        hh_done = m.sem("hh_done")
        hl_done = m.sem("hl_done")
        d_done = m.sem("d_done")
        added = m.sem("added")

        with nc.Block() as block:
            @block.vector
            def _(dve):
                def norm(c):
                    wait(dve, xT_done, 1 * c)
                    normalise_chunk(dve, c, x, ln_mv, ln_rs, xn, xn_ready)

                def x_low(c):
                    for k in range(2):
                        dve.wait_ge(xh_done, 2 * c + k + 1)
                        dve.scalar_tensor_tensor(xl[:, k, :], xT_ps[:, k, :], XS, xh[:, k, :], ALU.mult, ALU.subtract).then_inc(xl_done, 1)

                def product(c, n):
                    dve.wait_ge(silu, 8 * c + n + 1)
                    dve.wait_ge(g_done, 8 * c + n + 1)
                    wait(dve, hl_done, 8 * c + n - 1)
                    dve.scalar_tensor_tensor(h[n % 2][:], sg[n % 2][:], fsc[:, 1:2], g_ps[n % 2][:], ALU.mult, ALU.mult).then_inc(h_done, 1)

                def low(c, n):
                    dve.wait_ge(hh_done, 8 * c + n + 1)
                    dve.tensor_tensor(hl[:, n, :], h[n % 2][:], hh[:, n, :], ALU.subtract).then_inc(hl_done, 1)

                def step(c):
                    if within(c + 1, CHUNKS):
                        norm(c + 1)
                    product(c, 0)
                    for n in range(ME):
                        if n + 1 < ME:
                            product(c, n + 1)
                        low(c, n)
                    if within(c + 1, CHUNKS):
                        x_low(c + 1)
                    for q in range(QT):
                        dve.wait_ge(d_done, QT * c + q + 1)
                        wait(dve, added, 4 * (QT * c + q))
                        add_and_count(dve, QT * c + q, QT * c + q, d_ps[q % 2][:], fsc[:, 2:3], x, xt, st, mv, ln_mv, added)
                norm(0)
                x_low(0)
                over_chunks(dve, step)

            @block.scalar
            def _(act):
                def x_high(c):
                    act.wait_ge(xT_done, c + 1)
                    for k in range(2):
                        act.mul(xh[:, k, :], xT_ps[:, k, :], XS).then_inc(xh_done, 1)

                def silus(c, n):
                    act.wait_ge(u_done, 8 * c + n + 1)
                    wait(act, h_done, 8 * c + n - 1)
                    act.activation(sg[n % 2][:], u_ps[n % 2][:], ACT.Silu, scale=fsc[:, 0:1]).then_inc(silu, 1)

                def step(c):
                    silus(c, 0)
                    for n in range(ME):
                        if n + 1 < ME:
                            silus(c, n + 1)
                        act.wait_ge(h_done, 8 * c + n + 1)
                        if n == 0:
                            wait(act, d_done, QT * c)
                        act.copy(hh[:, n, :], h[n % 2][:]).then_inc(hh_done, 1)
                    if within(c + 1, CHUNKS):
                        x_high(c + 1)
                x_high(0)
                over_chunks(act, step)

            @block.tensor
            def _(pe):
                def transposes(c):
                    pe.wait_ge(xn_ready, c + 1)
                    wait(pe, xl_done, 2 * c)
                    for k in range(2):
                        for q in range(QT):
                            last = pe.transpose(xT_ps[:, k, P * q:P * q + P], xn[:, q, P * k:P * k + P], ident)
                    last.then_inc(xT_done, 1)

                def step(c):
                    pe.wait_ge(xl_done, 2 * c + 2)
                    for n in range(ME):
                        for w, ps, sem, used in ((k_up, u_ps, u_done, silu), (k_gate, g_ps, g_done, h_done)):
                            wait(pe, used, 8 * c + n - 1)
                            for k in range(2):
                                for part in (xh, xl):
                                    last = pe.matmul(ps[n % 2][:], w[:, k, P * n:P * n + P], part[:, k, :],
                                                     start=(k == 0 and part is xh), stop=(k == 1 and part is xl))
                            last.then_inc(sem, 1)
                    if within(c + 1, CHUNKS):
                        transposes(c + 1)
                    pe.wait_ge(hl_done, 8 * c + 8)
                    for q in range(QT):
                        wait(pe, added, 4 * (QT * c + q) - 7)
                        for n in range(ME):
                            for part in (hh, hl):
                                last = pe.matmul(d_ps[q % 2][:], part[:, n, P * q:P * q + P], k_down[:, n, :],
                                                 start=(n == 0 and part is hh), stop=(n == ME - 1 and part is hl))
                        last.then_inc(d_done, 1)
                transposes(0)
                over_chunks(pe, step)


def attention1(nc, cst, x, ln_mv, ln_rs, gat, ident, Cw, NB, VT, kvr):
    with ExitStack() as ctx:
        m = Mem(nc, ctx, "c")
        st = m.sb("st", [P, 6])
        mv = m.sb("mv", [P, 2])
        xt = m.sb("xt", [P, D])
        xn = m.sb("xn", [P, QT, D])
        xT = [m.sb(f"xT{n}", [P, 2, CH], F32R) for n in range(2)]
        qc = [m.sb(f"qc{r}", [P, CH]) for r in range(QR)]
        qs = [m.sb(f"qs{r}", [P, CH]) for r in range(QR)]
        qr = [[m.sb(f"qr{u}_{r}", [P, CH]) for r in range(QR)] for u in range(2)]
        EARLY = HP - 2
        qe = m.sb("qe", [P, EARLY, CH])
        qn = m.sb("qn", [P, HP, CH])
        vB = [m.sb(f"vB{u}", [P, 2, P]) for u in range(2)]
        kB = [m.sb(f"kB{u}", [P, 2, P]) for u in range(2)]
        sc = m.sb("sc", [P, H1, T])
        mx = m.sb("mx", [P, H1])
        sm = m.sb("sm", [P, H1])
        rs = m.sb("rs", [P, H1])
        pT = m.sb("pT", [P, HP, P])
        cT = m.sb("cT", [P, HP, P])
        q_ps = [m.ps(f"q_ps{r}", [P, CH]) for r in range(QR)]
        n_ps = m.ps("n_ps", [P, CH])
        s_ps = [m.ps(f"s_ps{n}", [P, 512]) for n in range(2)]
        v_ps = [m.ps(f"v_ps{n}", [P, 512]) for n in range(2)]

        zeroed = m.sem("zeroed")
        xn_ready = m.sem("xn_ready")
        xT_done = m.sem("xT_done")
        xT_lead = m.sem("xT_lead")
        xT_rest = m.sem("xT_rest")
        q_done = m.sem("q_done")
        q_used = m.sem("q_used")
        roped = m.sem("roped")
        n_used = m.sem("n_used")
        n_copied = m.sem("n_copied")
        moved = m.sem("moved")
        vB_ready = m.sem("vB_ready")
        kB_done = m.sem("kB_done")
        kB_copied = m.sem("kB_copied")
        s_done = m.sem("s_done")
        maxed = m.sem("maxed")
        shifted = m.sem("shifted")
        exped = m.sem("exped")
        summed = m.sem("summed")
        pnorm = m.sem("pnorm")
        p_done = m.sem("p_done")
        p_copied = m.sem("p_copied")
        v_done = m.sem("v_done")
        v_copied = m.sem("v_copied")
        o_done = m.sem("o_done")
        added = m.sem("added")

        def from_round(c, n):
            return not isinstance(c, int) or c >= n

        def projects(c):
            return not isinstance(c, int) or c < CHUNKS

        def over_rounds(eng, step):
            step(0)
            step(1)
            with eng.Fori(2, CHUNKS) as c:
                step(c)
            step(CHUNKS)

        with nc.Block() as block:
            @block.gpsimd
            def _(pool):
                for u in range(2):
                    pool.memset(vB[u][:], 0.0).then_inc(zeroed, 1)
                pool.wait_ge(zeroed, 2)

                def blocks(t, u):
                    wait(pool, v_done, t - 1)
                    for h in range(2):
                        rows = slice(64 * h, 64 * h + 64)
                        last = pool.tensor_copy(vB[u][rows, :, 64 * h:64 * h + 64], kvr[rows, bass.ds(2 * t, 2), :])
                    last.then_inc(vB_ready, 1)

                def rotate(c, i):
                    n = HP * c + i
                    wait(pool, n_used, n - 1)
                    for r in range(QR):
                        pool.wait_ge(q_used, QR * n + max(r, 1) + 1)
                        pool.tensor_tensor(qr[i % 2][r][:], qc[r][:], qs[r][:], ALU.add).then_inc(roped, 1)

                def step(c):
                    for i in range(HP):
                        if from_round(c, 1) and i % 2 == 0:
                            t = QT * c - QT + i // 2
                            pool.wait_ge(roped, QR * HP * c + (QR * i if projects(c) else 0))
                            blocks(t, i // 2 % 2)
                            if projects(c):
                                pool.wait_ge(vB_ready, t + 1)
                        if projects(c):
                            rotate(c, i)
                over_rounds(pool, step)

            @block.vector
            def _(dve):
                cos = cst[:, C_CQ:C_CQ + QR * S].rearrange("p (r s) -> p r s", r=QR)
                sin = cst[:, C_SQ:C_SQ + QR * S].rearrange("p (r s) -> p r s", r=QR)

                def times(dst, q, tab, to=slice(0, P), of=slice(0, P)):
                    rows = to.stop - to.start
                    return dve.tensor_tensor(dst[to].rearrange("p (b s) -> p b s", s=S), q[of].rearrange("p (b s) -> p b s", s=S),
                                             tab[to].unsqueeze(1).to_broadcast([rows, CH // S, S]), ALU.mult)

                def rotate(c, i):
                    n = HP * c + i
                    wait(dve, roped, QR * n)
                    for r in range(2):
                        dve.wait_ge(q_done, QR * n + r + 1)
                        times(qc[r], q_ps[r], cos[:, r, :])
                        times(qs[1 - r], q_ps[r], sin[:, 1 - r, :]).then_inc(q_used, 1)
                    dve.wait_ge(q_done, QR * n + 3)
                    times(qc[2], q_ps[2], cos[:, 2, :])
                    low, high = slice(0, 64), slice(64, P)
                    times(qs[2], q_ps[2], sin[:, 2, :], to=low, of=high)
                    times(qs[2], q_ps[2], sin[:, 2, :], to=high, of=low).then_inc(q_used, 1)

                def shift(t):
                    dve.wait_ge(s_done, t + 1)
                    for k in range(2):
                        dve.tensor_reduce(mx[:, 8 * k:8 * k + 8], s_ps[k][:].rearrange("p (h t) -> p h t", t=T), AX.X, ALU.max).then_inc(maxed, 1)
                    dve.wait_ge(maxed, 2 * t + 2)
                    wait(dve, p_done, 2 * t)
                    for k in range(2):
                        last = dve.tensor_tensor(sc[:, 8 * k:8 * k + 8, :], s_ps[k][:].rearrange("p (h t) -> p h t", t=T),
                                                 mx[:, 8 * k:8 * k + 8].unsqueeze(2).to_broadcast([P, 8, T]), ALU.subtract)
                    last.then_inc(shifted, 1)

                def normalise(t):
                    dve.wait_ge(exped, t + 1)
                    dve.tensor_reduce(sm[:], sc[:], AX.X, ALU.add).then_inc(summed, 1)
                    dve.wait_ge(summed, 2 * t + 1)
                    dve.reciprocal(rs[:], sm[:]).then_inc(summed, 1)
                    dve.wait_ge(summed, 2 * t + 2)
                    dve.tensor_tensor(sc[:], sc[:], rs[:].unsqueeze(2).to_broadcast([P, H1, T]), ALU.mult).then_inc(pnorm, 1)

                def output(t):
                    wait(dve, added, 4 * t)
                    dve.wait_ge(o_done, t + 1)
                    add_and_count(dve, t, t, v_ps[0][:, 0:D], gat[:, 1:2], x, xt, st, mv, ln_mv, added)

                def step(c):
                    if projects(c):
                        normalise_chunk(dve, c, x, ln_mv, ln_rs, xn, xn_ready)
                        dve.wait_ge(xT_lead, c + 1)
                        for k in range(2):
                            last = dve.tensor_tensor(xT[1][:, k, :], s_ps[k][:], xT[0][:, k, :].bitcast(F32), ALU.subtract)
                        last.then_inc(xT_rest, 1)
                    for i in range(HP):
                        t = QT * c - QT + i // 2
                        if projects(c):
                            rotate(c, i)
                        if from_round(c, 1) and i % 2 == 0:
                            shift(t)
                        if from_round(c, 1) and i % 2 == 1:
                            normalise(t)
                            if i > 1 or from_round(c, 2):
                                output(t - 1)
                over_rounds(dve, step)
                output(TILES - 1)

            @block.scalar
            def _(act):
                def values(t):
                    act.wait_ge(v_done, t + 1)
                    wait(act, o_done, t)
                    for b in range(2):
                        last = act.copy(cT[:, :, S * b:S * b + S], v_ps[b][:].rearrange("p (h s) -> p h s", s=S))
                    last.then_inc(v_copied, 1)

                def queries(c, i):
                    n = HP * c + i - 1
                    hp = (i - 1) % HP
                    act.wait_ge(n_used, n + 1)
                    if hp < EARLY:
                        wait(act, moved, 1 * c)
                        dst = qe
                    else:
                        dst = qn
                        wait(act, s_done, QT * (c - 1) if i == 0 else QT * c)
                    act.copy(dst[:, hp, :], n_ps[:]).then_inc(n_copied, 1)

                def step(c):
                    for i in range(HP):
                        t = QT * c - QT + i // 2
                        attends = from_round(c, 1)
                        if attends and i % 2 == 0 and (i or from_round(c, 2)):
                            values(t - 1)
                        if i == 0 and projects(c):
                            act.wait_ge(xT_done, c + 1)
                            for k in range(2):
                                last = act.copy(xT[0][:, k, :], s_ps[k][:])
                            last.then_inc(xT_lead, 1)
                        if i == 0 and attends:
                            queries(c, i)
                        if attends and i % 2 == 0:
                            act.wait_ge(kB_done, t + 1)
                            wait(act, s_done, t - 1)
                            act.copy(kB[i // 2 % 2][:], s_ps[0][:, 0:2 * P]).then_inc(kB_copied, 1)
                        if i and projects(c):
                            queries(c, i)
                        if attends and i % 2 == 0:
                            act.wait_ge(shifted, t + 1)
                            act.activation(sc[:], sc[:], ACT.Exp).then_inc(exped, 1)
                        if attends and i % 2 == 1:
                            for k in range(2):
                                act.wait_ge(p_done, 2 * t + k + 1)
                                if k == 0:
                                    wait(act, v_done, t)
                                act.copy(pT[:, 4 * k:4 * k + 4, :], v_ps[k][:]).then_inc(p_copied, 1)
                    if projects(c):
                        wait(act, s_done, QT * c)
                        act.wait_ge(n_copied, HP * c + EARLY)
                        act.copy(qn[:, 0:EARLY, :], qe[:]).then_inc(moved, 1)
                over_rounds(act, step)
                values(TILES - 1)

            @block.tensor
            def _(pe):
                def transpose_chunk(c):
                    pe.wait_ge(xn_ready, c + 1)
                    wait(pe, shifted, QT * (c - 1))
                    for k in range(2):
                        for q in range(QT):
                            last = pe.transpose(s_ps[k][:, P * q:P * q + P], xn[:, q, P * k:P * k + P], ident)
                    last.then_inc(xT_done, 1)

                def project(c, i):
                    n = HP * c + i
                    if i == 0:
                        pe.wait_ge(xT_lead, c + 1)
                        pe.wait_ge(xT_rest, c + 1)
                    for r in range(QR):
                        wait(pe, q_used, QR * n - QR + min(r + 1, 3))
                        parts = [(k, w, v) for k in range(2) for w, v in ((0, 0), (0, 1), (1, 0))]
                        for j, (k, w, v) in enumerate(parts):
                            last = pe.matmul(q_ps[r][:], Cw[w][:, k, i, P * r:P * r + P], xT[v][:, k, :], start=(j == 0), stop=(j == 5))
                        last.then_inc(q_done, 1)

                def combine(c, i):
                    n = HP * c + i - 1
                    wait(pe, n_copied, n)
                    for r in range(QR):
                        pe.wait_ge(roped, QR * n + r + 1)
                        last = pe.matmul(n_ps[:], NB[:, (i - 1) % HP, r, :], qr[(i - 1) % 2][r][:], start=(r == 0), stop=(r == QR - 1))
                    last.then_inc(n_used, 1)

                def keys(c, t, q):
                    pe.wait_ge(vB_ready, t + 1)
                    if q == 0 and projects(c):
                        pe.wait_ge(xT_lead, c + 1)
                        pe.wait_ge(xT_rest, c + 1)
                    wait(pe, shifted, t)
                    for b in range(2):
                        last = pe.transpose(s_ps[0][:, P * b:P * b + P], vB[q % 2][:, b, :], ident)
                    last.then_inc(kB_done, 1)

                def scores(c, t, q):
                    pe.wait_ge(kB_copied, t + 1)
                    pe.wait_ge(n_copied, HP * c)
                    pe.wait_ge(moved, 1 * c)
                    for b in range(2):
                        for hp in range(HP):
                            cols = slice(P * (hp % 4), P * (hp % 4) + P)
                            last = pe.matmul(s_ps[hp // 4][64 * b:64 * b + 64, cols], qn[:, hp, P * q + S * b:P * q + S * b + S],
                                             kB[q % 2][:, b, :], start=True, stop=True)
                    last.then_inc(s_done, 1)

                def transpose_probs(t):
                    pe.wait_ge(pnorm, t + 1)
                    wait(pe, added, 4 * t - 3)
                    wait(pe, v_copied, t)
                    for k in range(2):
                        for n in range(4):
                            hp = 4 * k + n
                            last = pe.transpose(v_ps[k][:, P * n:P * n + P], sc[:, 2 * hp:2 * hp + 2, :].rearrange("p h t -> p (h t)"), ident)
                        last.then_inc(p_done, 1)

                def values(t, u):
                    pe.wait_ge(p_copied, 2 * t + 2)
                    for b in range(2):
                        last = pe.matmul(v_ps[b][:].rearrange("p (h s) -> p h s", s=S), vB[u][:, b, :], pT[:, :, S * b:S * b + S],
                                         start=True, stop=True)
                    last.then_inc(v_done, 1)

                def output(t):
                    pe.wait_ge(v_copied, t + 1)
                    for hp in range(HP):
                        last = pe.matmul(v_ps[0][:, 0:D], cT[:, hp, :], VT[:, hp, :], start=(hp == 0), stop=(hp == HP - 1))
                    last.then_inc(o_done, 1)

                def step(c):
                    attends = from_round(c, 1)
                    for i in range(HP):
                        q = i // 2
                        t = QT * c - QT + q
                        before = i > 1 or from_round(c, 2)
                        if i and projects(c):
                            project(c, i)
                        if attends and i % 2 == 0 and before:
                            values(t - 1, (q - 1) % 2)
                        if i == 0 and projects(c):
                            transpose_chunk(c)
                        if attends and i % 2 == 0 and i:
                            keys(c, t, q)
                        if attends and i % 2 == 1 and before:
                            output(t - 1)
                        if (i or attends) and (projects(c) or i == 0):
                            combine(c, i)
                        if i == 0 and attends:
                            keys(c, t, q)
                        if i == 0 and projects(c):
                            project(c, 0)
                        if attends and i % 2 == 0:
                            scores(c, t, q)
                        if attends and i % 2 == 1:
                            transpose_probs(t)
                over_rounds(pe, step)
                values(TILES - 1, 1)
                output(TILES - 1)


def moe(nc, a, cst, x, ln_mv, ln_rs, gat, ident, out, xg_dram, acc_dram):
    with ExitStack() as ctx:
        m = Mem(nc, ctx, "m")
        idT = m.sb("idT", [CAP, E], U32)
        wg = [m.sb(f"wg{b}", [P, 2, I1]) for b in range(XB)]
        wu = [m.sb(f"wu{b}", [P, 2, I1]) for b in range(XB)]
        wd = [m.sb(f"wd{b}", [I1, D]) for b in range(XB)]
        weights = [m.sem(f"weights{b}") for b in range(XB)]

        def load_expert(sp, e, b):
            sp.dma_start(wg[b][:], a["L1_ffn_w_gate"][bass.ds(e, 1)].rearrange("o (k d) i -> d (o k) i", k=2)).then_inc(weights[b], 16)
            sp.dma_start(wu[b][:], a["L1_ffn_w_up"][bass.ds(e, 1)].rearrange("o (k d) i -> d (o k) i", k=2)).then_inc(weights[b], 16)
            sp.dma_start(wd[b][:], a["L1_ffn_w_down"][bass.ds(e, 1)].rearrange("o i d -> (o i) d")).then_inc(weights[b], 16)
        with ExitStack() as inner:
            r = Mem(nc, inner, "s")
            scores = r.sb("scores", [P, TILES, E])
            biased = r.sb("biased", [P, TILES, E])
            shared_and_router(nc, a, cst, x, ln_mv, ln_rs, gat, ident, xg_dram, acc_dram, scores, biased)
            route(nc, cst, x, gat, xg_dram, acc_dram, scores, biased, idT, load_expert)
        experts(nc, ident, xg_dram, acc_dram, idT, wg, wu, wd, weights, load_expert)
        total(nc, out, acc_dram)


def shared_and_router(nc, a, cst, x, ln_mv, ln_rs, gat, ident, xg_dram, acc_dram, scores, biased):
    with ExitStack() as ctx:
        m = Mem(nc, ctx, "r")
        rw = m.sb("rw", [E, D])
        rwT = m.sb("rwT", [P, 2, E])
        bias = m.sb("bias", [P, E])
        zero = m.sb("zero", [P, XW])
        wg = m.sb("wg", [P, 2, I1])
        wu = m.sb("wu", [P, 2, I1])
        wd = m.sb("wd", [I1, D])
        xn = [m.sb(f"xn{u}", [P, D]) for u in range(2)]
        xT = [m.sb(f"xT{u}", [P, 2, P]) for u in range(2)]
        rs = [m.sb(f"rs{u}", [P, E]) for u in range(2)]
        sg = [m.sb(f"sg{u}", [I1, P]) for u in range(2)]
        ha = [m.sb(f"ha{u}", [I1, P]) for u in range(2)]
        hb = [m.sb(f"hb{u}", [I1, P]) for u in range(2)]
        xT_ps = [m.ps(f"xT_ps{u}", [P, 2, P]) for u in range(2)]
        r_ps = [m.ps(f"r_ps{u}", [P, E]) for u in range(2)]
        gu_ps = [m.ps(f"gu_ps{u}", [I1, 2, P]) for u in range(2)]
        o_ps = [m.ps(f"o_ps{u}", [P, D]) for u in range(2)]

        loaded = m.sem("loaded")
        zeroed = m.sem("zeroed")
        cleared = m.sem("cleared")
        rw_done = m.sem("rw_done")
        rw_copied = m.sem("rw_copied")
        xn_ready = m.sem("xn_ready")
        stored = [m.sem(f"stored{u}") for u in range(2)]
        xT_done = m.sem("xT_done")
        xT_copied = m.sem("xT_copied")
        gu_done = m.sem("gu_done")
        sig = m.sem("sig")
        hid = m.sem("hid")
        o_done = m.sem("o_done")
        added = m.sem("added")

        with nc.Block() as block:
            @block.sync
            def _(sp):
                for dst, src in ((rw, a["L1_ffn_router_weight"]), (wg, a["L1_ffn_sh_gate"].rearrange("(k d) i -> d k i", k=2)),
                                 (wu, a["L1_ffn_sh_up"].rearrange("(k d) i -> d k i", k=2)), (wd, a["L1_ffn_sh_down"]),
                                 (bias, a["L1_ffn_e_bias"].rearrange("(o e) -> o e", o=1).to_broadcast([P, E]))):
                    sp.dma_start(dst[:], src).then_inc(loaded, 16)

                sp.wait_ge(zeroed, 1)
                sp.dma_start(acc_dram[1].rearrange("(n p) d -> p n d", p=P), zero[:, 0:D].unsqueeze(1).to_broadcast([P, ROWS // P, D])).then_inc(cleared, 16)
                sp.dma_start(acc_dram[0][TOK:ROWS], zero[0:CAP, 0:D]).then_inc(cleared, 16)
                sp.dma_start(xg_dram[TOK:ROWS], zero[0:CAP, :]).then_inc(cleared, 16)

                def step(t, u):
                    sp.wait_ge(xn_ready, t + 1)
                    sp.dma_start(xg_dram[bass.ds(P * t, P), 0:D], xn[u][:]).then_inc(stored[u], 16)
                over_tiles(sp, step)
                for u in range(2):
                    sp.wait_ge(stored[u], 16 * TILES // 2)
                sp.wait_ge(cleared, 48)

            @block.gpsimd
            def _(pool):
                pool.memset(zero[:], 0.0).then_inc(zeroed, 1)

            @block.vector
            def _(dve):
                def norm(t, u):
                    wait(dve, xT_done, t - 1)
                    wait(dve, stored[u], 8 * (t - u))
                    dve.tensor_scalar(xn[u][:], x[:, t, :], ln_mv[:, t, 0:1], ln_rs[:, bass.ds(t, 1)], ALU.subtract, ALU.mult).then_inc(xn_ready, 1)

                def step(t, u):
                    if within(t + 1):
                        norm(t + 1, 1 - u)
                    dve.wait_ge(sig, t + 1)
                    wait(dve, hid, 4 * t - 4)
                    dve.tensor_tensor(ha[u][:], sg[u][:], gu_ps[u][:, 0, :], ALU.mult).then_inc(hid, 1)
                    dve.wait_ge(hid, 4 * t + 1)
                    wait(dve, o_done, t - 1)
                    dve.tensor_tensor(hb[u][:], ha[u][:], gu_ps[u][:, 1, :], ALU.mult).then_inc(hid, 1)
                    dve.tensor_tensor(biased[:, t, :], rs[u][:], bias[:], ALU.add).then_inc(hid, 1)
                    dve.tensor_scalar(scores[:, t, :], rs[u][:], 1.0, None, ALU.mult).then_inc(hid, 1)
                    dve.wait_ge(o_done, t + 1)
                    dve.scalar_tensor_tensor(x[:, t, :], o_ps[u][:], gat[:, 3:4], x[:, t, :], ALU.mult, ALU.add).then_inc(added, 1)
                dve.wait_ge(loaded, 80)
                dve.wait_ge(rw_done, 1)
                dve.tensor_copy(rwT[:], xT_ps[0][:, 0, :]).then_inc(rw_copied, 1)
                norm(0, 0)
                over_tiles(dve, step)

            @block.scalar
            def _(act):
                def step(t, u):
                    act.wait_ge(xT_done, t + 1)
                    wait(act, gu_done, t - 1)
                    act.copy(xT[u][:], xT_ps[u][:]).then_inc(xT_copied, 1)
                    act.wait_ge(gu_done, t + 1)
                    wait(act, hid, 4 * t - 4)
                    act.activation(rs[u][:], r_ps[u][:], ACT.Sigmoid)
                    act.activation(sg[u][:], gu_ps[u][:, 0, :], ACT.Sigmoid).then_inc(sig, 1)
                over_tiles(act, step)

            @block.tensor
            def _(pe):
                pe.wait_ge(loaded, 80)
                for k in range(2):
                    last = pe.transpose(xT_ps[0][:, 0, E * k:E * k + E], rw[:, P * k:P * k + P], ident[0:E, 0:E])
                last.then_inc(rw_done, 1)
                pe.wait_ge(rw_copied, 1)

                def step(t, u):
                    pe.wait_ge(xn_ready, t + 1)
                    wait(pe, xT_copied, t - 1)
                    for k in range(2):
                        last = pe.transpose(xT_ps[u][:, k, :], xn[u][:, P * k:P * k + P], ident)
                    last.then_inc(xT_done, 1)
                    pe.wait_ge(xT_copied, t + 1)
                    wait(pe, hid, 4 * t - 4)
                    for k in range(2):
                        pe.matmul(r_ps[u][:], xT[u][:, k, :], rwT[:, k, :], start=(k == 0), stop=(k == 1))
                    for n, w in enumerate((wg, wu)):
                        for k in range(2):
                            last = pe.matmul(gu_ps[u][:, n, :], w[:, k, :], xT[u][:, k, :], start=(k == 0), stop=(k == 1))
                    last.then_inc(gu_done, 1)
                    pe.wait_ge(hid, 4 * t + 2)
                    wait(pe, added, t - 1)
                    pe.matmul(o_ps[u][:], hb[u][:], wd[:], start=True, stop=True).then_inc(o_done, 1)
                over_tiles(pe, step)


def route(nc, cst, x, gat, xg_dram, acc_dram, scores, biased, idT, load_expert):
    N = TILES * E
    with ExitStack() as ctx:
        m = Mem(nc, ctx, "t")
        hi = m.sb("hi", [P, TILES * NG, 4])
        lo = m.sb("lo", [P, TILES * NG, 4])
        hi2 = m.sb("hi2", [P, TILES * NG, 2])
        mi2 = m.sb("mi2", [P, TILES * NG, 2])
        lo2 = m.sb("lo2", [P, TILES * NG, 2])
        gs = m.sb("gs", [P, TILES, NG])
        g2 = m.sb("g2", [P, TILES, NG])
        w1 = m.sb("w1", [P, TILES, E])
        w2 = m.sb("w2", [P, TILES, E])
        sel = m.sb("sel", [P, TILES, E])
        prev = m.sb("prev", [P, TILES, E])
        top = m.sb("top", [P, TILES, TOPK])
        top_e = m.sb("top_e", [P, TILES, TOPK])
        at_pos = m.sb("at_pos", [P, TILES, TOPK, CAP], F16)
        at_e = m.sb("at_e", [P, TILES, TOPK, E], F16)
        tok_e = [m.sb(f"tok_e{u}", [P, TOPK, E], F16) for u in range(2)]
        idv = m.sb("idv", [CAP, E])
        ide = m.sb("ide", [CAP, E])
        s16 = m.sb("s16", [P, TILES])
        id_ps = m.ps("id_ps", [CAP, E])
        pos_ps = [m.ps(f"pos_ps{k}", [P, 512]) for k in range(2)]
        chain = m.sem("chain")
        selected = m.sem("selected")
        gated = m.sem("gated")
        counted = m.sem("counted")
        stored = m.sem("stored")
        hot = m.sem("hot")
        tok_ready = m.sem("tok_ready")
        listed = m.sem("listed")

        with nc.Block() as block:
            @block.sync
            def _(sp):
                sp.dma_start(acc_dram[0][0:TOK].rearrange("(n p) d -> p n d", p=P), x[:]).then_inc(stored, 16)
                for b in range(XB):
                    load_expert(sp, b, b)
                sp.wait_ge(gated, 1)
                sp.dma_start(xg_dram[0:TOK].rearrange("(n p) w -> p n w", p=P)[:, :, D:XW], w2[:]).then_inc(stored, 16)
                sp.wait_ge(stored, 32)

            @block.scalar
            def _(act):
                for t in range(TILES):
                    act.wait_ge(hot, t + 1)
                    wait(act, listed, t - 1)
                    act.activation(tok_e[t % 2][:], at_e[:, t], ACT.Copy, scale=cst[:, C_TOK + t:C_TOK + t + 1]).then_inc(tok_ready, 1)

            @block.tensor
            def _(pe):
                pe.wait_ge(selected, 1)
                for k in range(2):
                    pe.matmul(pos_ps[k][:], cst[:, C_TRI:C_TRI + P], sel[:, 8 * k:8 * k + 8, :], start=True, stop=False)
                    last = pe.matmul(pos_ps[k][:], cst[:, C_ONES:C_ONES + P], prev[:, 8 * k:8 * k + 8, :], start=False, stop=True)
                last.then_inc(counted, 1)
                for t in range(TILES):
                    pe.wait_ge(tok_ready, t + 1)
                    for k in range(TOPK):
                        last = pe.matmul(id_ps[:], at_pos[:, t, k, :], tok_e[t % 2][:, k, :],
                                         start=(t == 0 and k == 0), stop=(t == TILES - 1 and k == TOPK - 1))
                    last.then_inc(listed, 1)

            @block.vector
            def _(dve):
                n_chain = [0]

                def link(ins):
                    n_chain[0] += 1
                    ins.then_inc(chain, 1)
                    dve.wait_ge(chain, n_chain[0])
                tt = dve.tensor_tensor
                v = biased[:].rearrange("p t (g e) -> p (t g) e", g=NG)
                tt(hi[:], v[:, :, 0:4], v[:, :, 4:8], ALU.max)
                link(tt(lo[:], v[:, :, 0:4], v[:, :, 4:8], ALU.min))
                tt(hi2[:], hi[:, :, 0:2], hi[:, :, 2:4], ALU.max)
                tt(mi2[:], hi[:, :, 0:2], hi[:, :, 2:4], ALU.min)
                link(tt(lo2[:], lo[:, :, 0:2], lo[:, :, 2:4], ALU.max))
                link(tt(lo2[:], lo2[:], mi2[:], ALU.max))
                one = gs[:].rearrange("p t g -> p (t g)")
                two = g2[:].rearrange("p t g -> p (t g)")
                tt(one, hi2[:, :, 0], hi2[:, :, 1], ALU.max)
                tt(mi2[:, :, 0], hi2[:, :, 0], hi2[:, :, 1], ALU.min)
                link(tt(two, lo2[:, :, 0], lo2[:, :, 1], ALU.max))
                link(tt(two, two, mi2[:, :, 0], ALU.max))
                link(tt(one, one, two, ALU.add))
                mine = gs[:].unsqueeze(3).to_broadcast([P, TILES, NG, NG])
                other = gs[:].unsqueeze(2).to_broadcast([P, TILES, NG, NG])
                v1 = w1[:].rearrange("p t (g h) -> p t g h", g=NG)
                v2 = w2[:].rearrange("p t (g h) -> p t g h", g=NG)
                tt(v1, other, mine, ALU.is_gt)
                link(tt(v2, other, mine, ALU.is_equal))
                link(tt(w2[:], w2[:], cst[:, C_GT:C_GT + E].unsqueeze(1).to_broadcast([P, TILES, E]), ALU.mult))
                link(tt(w1[:], w1[:], w2[:], ALU.add))
                link(dve.tensor_reduce(g2[:], v1, AX.X, ALU.add))
                link(dve.tensor_scalar(g2[:], g2[:], float(TOPG), None, ALU.is_lt))
                link(tt(w1[:].rearrange("p t (g e) -> p (t g) e", g=NG), v,
                        g2[:].rearrange("p t g -> p (t g)").unsqueeze(2).to_broadcast([P, TILES * NG, E // NG]), ALU.mult))
                for t in range(TILES):
                    last = dve.max(top[:, t, :], w1[:, t, :])
                link(last)
                for t in range(TILES):
                    last = dve.match_replace(w2[:, t, :], top[:, t, :], w1[:, t, :], -3.0e38)
                link(last)
                link(tt(sel[:], w1[:], w2[:], ALU.not_equal))
                dve.memset(prev[:, 0, :], 0.0)
                link(dve.tensor_copy(prev[:, 1, :], sel[:, 0, :]))
                for t in range(2, TILES):
                    link(tt(prev[:, t, :], prev[:, t - 1, :], sel[:, t - 1, :], ALU.add))
                link(tt(w2[:], scores[:], sel[:], ALU.mult))
                dve.sem_inc(selected, 1)
                link(dve.tensor_reduce(s16[:], w2[:], AX.X, ALU.add))
                link(dve.tensor_scalar(s16[:], s16[:], 1e-20, None, ALU.add))
                link(dve.reciprocal(s16[:], s16[:]))
                link(dve.tensor_scalar(s16[:], s16[:], gat[:, 3:4], RSCALE, ALU.mult, ALU.mult))
                tt(w2[:], w2[:], s16[:].unsqueeze(2).to_broadcast([P, TILES, E]), ALU.mult).then_inc(gated, 1)
                dve.wait_ge(counted, 1)
                for k in range(2):
                    part = slice(8 * k, 8 * k + 8)
                    ps = pos_ps[k][:].rearrange("p (t e) -> p t e", e=E)
                    tt(w1[:, part, :], ps, cst[:, C_EB:C_EB + E].unsqueeze(1).to_broadcast([P, 8, E]), ALU.add)
                    link(dve.scalar_tensor_tensor(sel[:, part, :], ps, float(CAP), sel[:, part, :], ALU.is_lt, ALU.mult))
                link(tt(w1[:], w1[:], sel[:], ALU.mult))
                link(tt(sel[:], sel[:], cst[:, C_EB:C_EB + E].unsqueeze(1).to_broadcast([P, TILES, E]), ALU.mult))
                for t in range(TILES):
                    dve.max(top[:, t, :], w1[:, t, :])
                    last = dve.max(top_e[:, t, :], sel[:, t, :])
                link(last)
                link(tt(top[:], top[:], top_e[:], ALU.subtract))
                for t in range(TILES):
                    tt(at_pos[:, t], cst[:, C_POS:C_POS + CAP].unsqueeze(1).to_broadcast([P, TOPK, CAP]),
                       top[:, t, :].unsqueeze(2).to_broadcast([P, TOPK, CAP]), ALU.is_equal)
                    tt(at_e[:, t], cst[:, C_EB:C_EB + E].unsqueeze(1).to_broadcast([P, TOPK, E]),
                       top_e[:, t, :].unsqueeze(2).to_broadcast([P, TOPK, E]), ALU.is_equal).then_inc(hot, 1)
                dve.wait_ge(listed, TILES)
                link(dve.tensor_scalar(ide[:], id_ps[:], 0.0, cst[:, C_PAD:C_PAD + 1], ALU.is_equal, ALU.mult))
                link(dve.scalar_tensor_tensor(idv[:], id_ps[:], -1.0, ide[:], ALU.add, ALU.add))
                link(dve.tensor_copy(idT[:], idv[:]))


def experts(nc, ident, xg_dram, acc_dram, idT, wg, wu, wd, weights, load_expert):
    ROUNDS = E // XB
    with ExitStack() as ctx:
        m = Mem(nc, ctx, "e")
        xg = [m.sb(f"xg{b}", [P, XW]) for b in range(XB)]
        ys = [m.sb(f"ys{b}", [P, D]) for b in range(NY)]
        xT = [m.sb(f"xT{u}", [P, 2, P]) for u in range(2)]
        sg = [m.sb(f"sg{u}", [I1, P]) for u in range(2)]
        ha = [m.sb(f"ha{u}", [I1, P]) for u in range(2)]
        hb = [m.sb(f"hb{u}", [I1, P]) for u in range(2)]
        xT_ps = [m.ps(f"xT_ps{u}", [P, 2, P]) for u in range(2)]
        gu_ps = [m.ps(f"gu_ps{u}", [I1, 2, P]) for u in range(2)]
        y_ps = [m.ps(f"y_ps{u}", [P, D]) for u in range(2)]

        gathered = [m.sem(f"gathered{b}") for b in range(XB)]
        summed = [m.sem(f"summed{u}") for u in range(2)]
        xT_done = m.sem("xT_done")
        xT_copied = m.sem("xT_copied")
        gu_done = m.sem("gu_done")
        sig = m.sem("sig")
        hid = m.sem("hid")
        y_done = m.sem("y_done")
        y_out = m.sem("y_out")

        def over_experts(eng, step):
            for b in range(XB):
                step(b, 0, b)
            with eng.Fori(1, ROUNDS - 1) as r:
                for b in range(XB):
                    step(XB * r + b, r, b)
            for b in range(XB):
                step(E - XB + b, ROUNDS - 1, b)

        with nc.Block() as block:
            @block.gpsimd
            def _(pool):
                for n in range(E + LEAD):
                    if n < E:
                        wait(pool, y_out, n - XB + 1)
                        pool.indirect_dma_start(out=xg[n % XB][:], out_offset=None, in_=xg_dram,
                                                in_offset=bass.IndirectOffsetOnAxis(ap=idT[:, n:n + 1], axis=0),
                                                bounds_check=ROWS - 1, oob_is_err=True).then_inc(gathered[n % XB], 16)
                    if n >= LEAD:
                        e = n - LEAD
                        pool.wait_ge(y_out, e + 1)
                        wait(pool, summed[e % 2], 16 * (e // 2))
                        pool.indirect_dma_start(out=acc_dram[e % 2],
                                                out_offset=bass.IndirectOffsetOnAxis(ap=idT[:, e:e + 1], axis=0),
                                                in_=ys[e % NY][:], in_offset=None, bounds_check=ROWS - 1, oob_is_err=True,
                                                compute_op=ALU.add).then_inc(summed[e % 2], 16)
                for u in range(2):
                    pool.wait_ge(summed[u], 16 * E // 2)

            @block.sync
            def _(sp):
                def step(e, r, b):
                    if not isinstance(e, int) or e + XB < E:
                        sp.wait_ge(y_done, e + 1)
                        load_expert(sp, e + XB, b)
                over_experts(sp, step)

            @block.scalar
            def _(act):
                def step(e, r, b):
                    u = b % 2
                    act.wait_ge(xT_done, e + 1)
                    wait(act, gu_done, e - 1)
                    act.copy(xT[u][:], xT_ps[u][:]).then_inc(xT_copied, 1)
                    act.wait_ge(gu_done, e + 1)
                    wait(act, hid, 2 * e - 2)
                    act.activation(sg[u][:], gu_ps[u][:, 0, :], ACT.Sigmoid).then_inc(sig, 1)
                over_experts(act, step)

            @block.vector
            def _(dve):
                def leave(e, r, b):
                    dve.wait_ge(y_done, e + 1)
                    wait(dve, summed[b % 2], 8 * (e - b % 2) - 8 * NY + 16)
                    dve.tensor_scalar(ys[b % NY][:], y_ps[b % 2][:], xg[b][:, bass.ds(D + e, 1)], None, ALU.mult).then_inc(y_out, 1)

                def step(e, r, b):
                    u = b % 2
                    dve.wait_ge(sig, e + 1)
                    wait(dve, hid, 2 * e - 2)
                    dve.tensor_tensor(ha[u][:], sg[u][:], gu_ps[u][:, 0, :], ALU.mult).then_inc(hid, 1)
                    dve.wait_ge(hid, 2 * e + 1)
                    wait(dve, y_done, e - 1)
                    dve.tensor_tensor(hb[u][:], ha[u][:], gu_ps[u][:, 1, :], ALU.mult).then_inc(hid, 1)
                    if b:
                        leave(e - 1, r, b - 1)
                    elif not isinstance(e, int) or e > 0:
                        leave(e - 1, r - 1, XB - 1)
                over_experts(dve, step)
                leave(E - 1, ROUNDS - 1, XB - 1)

            @block.tensor
            def _(pe):
                def rows(e, r, b):
                    pe.wait_ge(gathered[b], 16 * (r + 1))
                    wait(pe, xT_copied, e - 1)
                    for k in range(2):
                        last = pe.transpose(xT_ps[b % 2][:, k, :], xg[b][:, P * k:P * k + P], ident)
                    last.then_inc(xT_done, 1)

                def down(e, b):
                    pe.wait_ge(hid, 2 * e + 2)
                    wait(pe, y_out, e - 1)
                    pe.matmul(y_ps[b % 2][:], hb[b % 2][:], wd[b][:], start=True, stop=True).then_inc(y_done, 1)

                def step(e, r, b):
                    u = b % 2
                    if b + 1 < XB:
                        rows(e + 1, r, b + 1)
                    elif not isinstance(e, int) or e + 1 < E:
                        rows(e + 1, r + 1, 0)
                    pe.wait_ge(xT_copied, e + 1)
                    pe.wait_ge(weights[b], 48 * (r + 1))
                    wait(pe, hid, 2 * e - 2)
                    for n, w in enumerate((wg, wu)):
                        for k in range(2):
                            last = pe.matmul(gu_ps[u][:, n, :], w[b][:, k, :], xT[u][:, k, :], start=(k == 0), stop=(k == 1))
                    last.then_inc(gu_done, 1)
                    if not isinstance(e, int) or e > 0:
                        down(e - 1, (b - 1) % XB)
                rows(0, 0, 0)
                over_experts(pe, step)
                down(E - 1, XB - 1)


def total(nc, out, acc_dram):
    with ExitStack() as ctx:
        m = Mem(nc, ctx, "f")
        part = [m.sb(f"part{u}", [P, TILES, D]) for u in range(2)]
        loaded = [m.sem(f"loaded{c}") for c in range(CHUNKS)]
        summed = m.sem("summed")
        stored = m.sem("stored")
        rows = out.rearrange("b s d -> (b s) d").rearrange("(n p) d -> p n d", p=P)
        with nc.Block() as block:
            def load(eng, u):
                for c in range(CHUNKS):
                    n = slice(QT * c, QT * c + QT)
                    eng.dma_start(part[u][:, n], acc_dram[u][0:TOK].rearrange("(n p) d -> p n d", p=P)[:, n]).then_inc(loaded[c], 16)

            @block.sync
            def _(sp):
                load(sp, 0)
                for c in range(CHUNKS):
                    n = slice(QT * c, QT * c + QT)
                    sp.wait_ge(summed, c + 1)
                    sp.dma_start(rows[:, n], part[0][:, n]).then_inc(stored, 16)
                sp.wait_ge(stored, 16 * CHUNKS)

            @block.scalar
            def _(act):
                load(act, 1)

            @block.vector
            def _(dve):
                for c in range(CHUNKS):
                    n = slice(QT * c, QT * c + QT)
                    dve.wait_ge(loaded[c], 32)
                    dve.tensor_tensor(part[0][:, n], part[0][:, n], part[1][:, n], ALU.add).then_inc(summed, 1)


_INS = ['x', 'ctx_512', 'g_xattn', 'g_ffn', 'L0_ffn_W_up', 'L0_ffn_W_gate', 'L0_ffn_W_down', 'L1_xattn_Wq', 'L1_xattn_w_kc_q',
        'L1_xattn_w_kc_kv', 'L1_xattn_W_qr', 'L1_xattn_W_kr', 'L1_xattn_Wo', 'L1_ffn_router_weight', 'L1_ffn_e_bias',
        'L1_ffn_w_gate', 'L1_ffn_w_up', 'L1_ffn_w_down', 'L1_ffn_sh_gate', 'L1_ffn_sh_up', 'L1_ffn_sh_down']


def kernel(**inputs):
    import concourse.bacc as bacc
    from concourse.bass_utils import run_bass_kernel_spmd as run

    nc = bacc.Bacc("TRN2", target_bir_lowering=False, num_devices=1)
    arrays = {f"in_{name}": np.ascontiguousarray(inputs[name]) for name in _INS}
    arrays["in_consts"] = constants()
    a = {name[3:]: nc.dram_tensor(name, v.shape, mybir.dt.from_np(v.dtype), kind="ExternalInput").ap() for name, v in arrays.items()}
    out = nc.dram_tensor("out_0", (B, S, D), F32, kind="ExternalOutput").ap()
    xg_dram = nc.dram_tensor("xg_dram", (ROWS, XW), F32, kind="Internal").ap()
    acc_dram = [nc.dram_tensor(f"acc{u}_dram", (ROWS, D), F32, kind="Internal").ap() for u in range(2)]
    program(nc, a, out, xg_dram, acc_dram)
    r = run(nc, [arrays], core_ids=[0])
    return r.results[0]["out_0"]
```

```python
import numpy as np

import concourse.bass as bass
from concourse import mybir
from contextlib import ExitStack

F32 = mybir.dt.float32
F16 = mybir.dt.float16
F32R = mybir.dt.float32r
U32 = mybir.dt.uint32
ALU = mybir.AluOpType
ACT = mybir.ActivationFunctionType
AX = mybir.AxisListType

P = 128
B, S, D = 32, 64, 256
TOK = B * S
TILES = TOK // P
T = 64
DC = 64
EPS_LN = 1e-5
KVH, G, HD = 8, 4, 8
DE = 1024
ME = DE // P
CH = 512
CHUNKS = TOK // CH
QT = CH // P
XS = 2048.0
H1, HK, DCQ = 16, 128, 192
HP = H1 // 2
QR = 2 * DCQ // P
E, I1, NG, TOPG, TOPK, CAP = 64, 88, 8, 4, 8, 128
RSCALE = 2.5
XB = 8
NY = 4
LEAD = 5
XW = D + E
ROWS = TOK + CAP

C_ID, C_ONES, C_TRI, C_KM, C_CQ, C_SQ, C_CK, C_SK, C_GT, C_TOK, C_EB, C_POS, C_PAD = np.cumsum(
    [0, 128, 128, 128, 8, 192, 192, 64, 64, 64, 16, 64, 128]).tolist()
C_ALL = C_PAD + 1


def constants():
    def rope(length, dim):
        inv = (np.float32(1.0) / np.float32(10000.0) ** (np.arange(0, dim, 2, dtype=np.float32) / np.float32(dim))).astype(np.float32)
        f = np.arange(length, dtype=np.float32)[:, None] * inv[None, :]
        return np.repeat(np.sin(f), 2, axis=-1).astype(np.float32), np.repeat(np.cos(f), 2, axis=-1).astype(np.float32)
    c = np.zeros((P, C_ALL), np.float32)
    p = np.arange(P)
    c[:, C_ID:C_ID + P] = np.eye(P)
    c[:, C_ONES:C_ONES + P] = 1.0
    c[:, C_TRI:C_TRI + P] = p[:, None] < p[None, :]
    c[:, C_KM:C_KM + 8] = (p[:, None] % 64 // 8) == np.arange(8)[None, :]
    sin, cos = rope(S, DCQ)
    half = DCQ // 2
    low = np.where(p < half, p, p - half)
    for r, q in enumerate((low, low + half, np.where(p < 64, p + 32, p + 64))):
        c[:, C_CQ + r * 64:C_CQ + r * 64 + 64] = cos[:, q].T
        c[:, C_SQ + r * 64:C_SQ + r * 64 + 64] = np.where(q < half, -sin[:, q], sin[:, q]).T
    sin, cos = rope(T, DC)
    sin[:, :DC // 2] *= -1.0
    c[:, C_CK:C_CK + 64] = cos[p % 64]
    c[:, C_SK:C_SK + 64] = sin[p % 64]
    g = np.arange(NG)
    c[:, C_GT:C_GT + 64] = (g[None, :] < g[:, None]).astype(np.float32).reshape(1, 64)
    c[:, C_TOK:C_TOK + TILES] = p[:, None] + P * np.arange(TILES)[None, :] + 1.0
    c[:, C_EB:C_EB + E] = np.arange(1, E + 1)[None, :] * CAP
    c[:, C_POS:C_POS + CAP] = np.arange(CAP)[None, :]
    c[:, C_PAD] = TOK + p + 1.0
    return c


def key_ones():
    ones = np.zeros((2, KVH, 2, KVH, T), np.float32)
    for j in range(KVH):
        ones[:, j, :, j, :] = 1.0
    return ones.reshape(2 * KVH, 2 * KVH * T)


def wait(eng, sem, value):
    if not isinstance(value, int) or value > 0:
        eng.wait_ge(sem, value)


def over_tiles(eng, step, alone=2):
    for t in range(alone):
        step(t, t % 2)
    with eng.Fori(alone // 2, TILES // 2 - 1) as it:
        step(2 * it, 0)
        step(2 * it + 1, 1)
    for t in (TILES - 2, TILES - 1):
        step(t, t % 2)


def within(t, n=TILES):
    return not isinstance(t, int) or t < n


class Mem:

    def __init__(self, nc, ctx, stage):
        self.nc, self.ctx, self.stage = nc, ctx, stage

    def sb(self, name, shape, dt=F32):
        return self.ctx.enter_context(self.nc.sbuf_tensor(f"{self.stage}_{name}", shape, dt))

    def ps(self, name, shape, dt=F32):
        return self.ctx.enter_context(self.nc.psum_tensor(f"{self.stage}_{name}", shape, dt))

    def sem(self, name):
        return self.nc.alloc_semaphore(f"{self.stage}_{name}")


def program(nc, a, out, xg_dram, acc_dram):
    ctx = ExitStack()
    with ctx:
        g = Mem(nc, ctx, "g")
        cst = g.sb("cst", [P, C_ALL])
        x = g.sb("x", [P, TILES, D])
        gat = g.sb("gat", [P, 4])
        ln_mv = g.sb("ln_mv", [P, TILES, 2])
        ln_rs = g.sb("ln_rs", [P, TILES])
        ident = cst[:, C_ID:C_ID + P]
        sh = {name: g.sb(name, shape) for name, shape in (
            ("rw", [E, D]), ("bias", [P, E]), ("swg", [P, 2, I1]), ("swu", [P, 2, I1]), ("swd", [I1, D]))}
        sh_in = g.sem("sh_in")
        with ExitStack() as both:
            w = Mem(nc, both, "b")
            kvr = w.sb("kvr", [P, B, DC])
            raw = {name: w.sb(name, shape) for name, shape in (
                ("wqr", [P, H1, 2, 64]), ("wkr", [P, H1, 64]), ("wq", [P, H1, D]), ("wcq", [P, H1, DCQ]),
                ("wo", [P, 2, H1 * HK]), ("wck", [P, H1, DC]))}
            raw_in = {name: w.sem(f"{name}_in") for name in raw}
            with ExitStack() as layer:
                w = Mem(nc, layer, "l0")
                ctxK = w.sb("ctxK", [P, TILES, P], F32R)
                ctxd = w.sb("ctxd", [P, B, DC])
                ones = w.sb("ones", [80, 2 * KVH * T])
                k_up = w.sb("k_up", [P, 2, DE], F16)
                k_gate = w.sb("k_gate", [P, 2, DE], F16)
                k_down = w.sb("k_down", [P, ME, D], F16)
                tern = w.sb("tern", [P, 3, 3])
                fsc = w.sb("fsc", [P, 4])
                prep(nc, a, 0, raw, raw_in, cst, x, gat, ident, ctxK, ctxd, ones, k_up, k_gate, k_down, tern, fsc, None, None, None, kvr, ln_mv, ln_rs)
                attention0(nc, a, cst, x, ln_mv, ln_rs, gat, ident, ctxK, ctxd, ones, raw, raw_in, sh, sh_in)
                ffn0(nc, x, ln_mv, ln_rs, ident, k_up, k_gate, k_down, fsc)
            with ExitStack() as layer:
                w = Mem(nc, layer, "l1")
                Cw = [w.sb(f"Cw{n}", [P, 2, HP, 2 * DCQ], F32R) for n in range(2)]
                NB = w.sb("NB", [P, HP, QR, P])
                VT = [w.sb(f"VT{n}", [P, HP, D], F32R) for n in range(2)]
                prep(nc, a, 1, raw, raw_in, cst, x, gat, ident, None, None, None, None, None, None, None, None, Cw, NB, VT, kvr, ln_mv, ln_rs)
                attention1(nc, cst, x, ln_mv, ln_rs, gat, ident, Cw, NB, VT, kvr, raw)
        moe(nc, a, cst, x, ln_mv, ln_rs, gat, ident, out, xg_dram, acc_dram, sh, sh_in)


def by_pair(h, dst, src):
    src = src.rearrange("p u (s q) -> p u s q", s=2)
    first = dst[:, :, 0:2 * P].rearrange("p u (s q) -> p u s q", s=2)
    if h == 0:
        return [(first[:, :, :, 0:96], src)]
    return [(first[:, :, :, 96:P], src[:, :, :, 0:32]),
            (dst[:, :, 2 * P:3 * P].rearrange("p u (s q) -> p u s q", s=2), src[:, :, :, 32:96])]


def prep(nc, a, phase, raw, raw_in, cst, x, gat, ident, ctxK, ctxd, ones, k_up, k_gate, k_down, tern, fsc, Cw, NB, VT, kvr, ln_mv, ln_rs):
    with ExitStack() as ctx:
        m = Mem(nc, ctx, f"p{phase}")
        if phase == 0:
            ctx_tok = m.sb("ctx_tok", [P, TILES, DC])
            w3 = [m.sb(n, [P, 2048]) for n in ("w_up", "w_gate", "w_down")]
            pos = m.sb("pos", [P, 2048], F16)
            q3 = [m.sb(n, [P, 2048], F16) for n in ("q_up", "q_gate", "q_down")]
            identh = m.sb("identh", [P, P], F16)
            rot = m.sb("rot", [P, B, DC])
            part = m.sb("part", [P, 3])
            stats = m.sb("stats", [P, TILES, 6])
            graw = m.sb("graw", [P, 4])
        else:
            wq, wcq, wck, wqr, wkr, wo = (raw[name] for name in ("wq", "wcq", "wck", "wqr", "wkr", "wo"))
            qrT = m.sb("qrT", [P, HP, 2 * DCQ])
            krT = m.sb("krT", [P, HP, P])
            std = InverseStd(m)
            woT = wq
        banks = [m.ps(f"bank{n}", [P, 512]) for n in range(8)]

        loaded = raw_in if phase == 1 else {n: m.sem(f"ld_{n}") for n in ("cst", "ones", "ctx", "ctxd", "w0", "w1", "w2", "g", "x")}
        done = m.sem("done")
        act_out = m.sem("act_out")
        dve_out = m.sem("dve_out")
        zeroed = m.sem("zeroed")
        if phase == 0:
            absum = m.sem("absum")
            summed = m.sem("summed")
            quant = m.sem("quant")
            chain = m.sem("dve_chain")
            pchain = m.sem("pool_chain")
            gats = m.sem("gats")

        if phase == 0:
            jobs = [(kind, n) for n in range(4) for kind in ("ctx", "ctxl")] + [("up", 0), ("up", 1), ("gate", 0), ("gate", 1), ("down", 0), ("down", 1)]
        else:
            jobs = [(kind, n) for n in range(H1) for kind in ("C", "Cl")] + [("qr", n) for n in range(HP)] + [("kr", 0)]
            jobs += [("wo", n) for n in range(HP)] + [("N", n) for n in range(HP - 1)]
            jobs += [(kind, n) for n in range(HP) for kind in ("V", "Vl")] + [("N", HP - 1)]
        at = {j: n for n, j in enumerate(jobs)}

        def copied_out(eng, n):
            wait(eng, act_out, n // 2 + 1)
            wait(eng, dve_out, (n + 1) // 2)

        def copy_out(copy, job, bank, sem):
            kind, n = job
            if kind == "ctx":
                copy(ctxK[0:64, 4 * n:4 * n + 4, :], bank[0:64, :]).then_inc(sem, 1)
            elif kind == "qr":
                for h in range(2):
                    rows = slice(64 * h, 64 * h + 64)
                    for dst, src in by_pair(h, qrT[rows, n, :].unsqueeze(1), bank[0:64, 192 * h:192 * h + 192].unsqueeze(1)):
                        last = copy(dst, src)
                last.then_inc(sem, 1)
            elif kind == "kr":
                for h in range(2):
                    rows = slice(64 * h, 64 * h + 64)
                    last = copy(krT[rows, :, 64 * h:64 * h + 64], bank[rows, :].rearrange("p (n c) -> p n c", n=HP))
                last.then_inc(sem, 1)
            elif kind == "C":
                for dst, src in by_pair(n % 2, Cw[0][:, :, n // 2, :], bank[:, 0:2 * DCQ].rearrange("p (u q) -> p u q", u=2)):
                    last = copy(dst, src)
                last.then_inc(sem, 1)
            elif kind == "wo":
                copy(woT[:, 2 * n:2 * n + 2, :], bank[:]).then_inc(sem, 1)
            elif kind == "N":
                copy(NB[:, n, :, :], bank[:, 0:QR * P]).then_inc(sem, 1)
            elif kind == "V":
                copy(VT[0][:, n, :], bank[:, 0:D]).then_inc(sem, 1)
            elif kind in ("up", "gate"):
                copy((k_up if kind == "up" else k_gate)[:, n, :], bank[:].bitcast(F16)).then_inc(sem, 1)
            elif kind == "down":
                copy(k_down[:, :, P * n:P * n + P], bank[:].bitcast(F16).rearrange("p (m i) -> p m i", m=ME)).then_inc(sem, 1)

        with nc.Block() as block:
            @block.sync
            def _(sp):
                def load(dst, src, name):
                    sp.dma_start(dst, src).then_inc(loaded[name], 16)
                if phase == 0:
                    load(cst[:], a["consts"], "cst")
                    load(ctx_tok[:], a["ctx_512"].rearrange("(n b) t d -> (b t) n d", b=2), "ctx")
                    load(ones[64:80], a["key_ones"], "ones")
                    for h in range(2):
                        load(ctxd[64 * h:64 * h + 64], a["ctx_512"].rearrange("b t d -> t b d"), "ctxd")

            @block.scalar
            def _(act):
                if phase == 0:
                    for k, name in enumerate(("L0_ffn_W_up", "L0_ffn_W_gate", "L0_ffn_W_down")):
                        act.dma_start(w3[k][:], a[name].rearrange("(u p) d -> p u d", p=P)).then_inc(loaded[f"w{k}"], 16)
                    act.dma_start(graw[:, 0:2], a["g_xattn"].rearrange("(o g) -> o g", o=1).to_broadcast([P, 2])).then_inc(loaded["g"], 16)
                    act.dma_start(graw[:, 2:4], a["g_ffn"].rearrange("(o g) -> o g", o=1).to_broadcast([P, 2])).then_inc(loaded["g"], 16)
                    act.dma_start(x[:], a["x"].rearrange("b s d -> (b s) d").rearrange("(n p) d -> p n d", p=P)).then_inc(loaded["x"], 16)
                    act.wait_ge(loaded["g"], 32)
                    act.activation(gat[:], graw[:], ACT.Tanh).then_inc(gats, 1)
                if phase == 1:
                    std.scalar(act)
                for n in range(0, len(jobs), 2):
                    if jobs[n] == ("qr", 0):
                        act.wait_ge(zeroed, 2)
                    act.wait_ge(done, n + 1)
                    copy_out(act.copy, jobs[n], banks[n % 8], act_out)

            @block.gpsimd
            def _(pool):
                if phase == 1:
                    for w in (qrT, krT):
                        pool.memset(w[:], 0.0).then_inc(zeroed, 1)
                    return
                pool.wait_ge(loaded["cst"], 16)
                pool.tensor_copy(identh[:], ident).then_inc(zeroed, 1)
                pool.wait_ge(loaded["ctxd"], 32)
                pool.wait_ge(loaded["ones"], 16)
                half = DC // 2
                sin = cst[:, C_SK:C_SK + DC].unsqueeze(1)
                pool.tensor_tensor(rot[:, :, 0:half], ctxd[:, :, half:DC], sin[:, :, 0:half].to_broadcast([P, B, half]), ALU.mult)
                pool.tensor_tensor(rot[:, :, half:DC], ctxd[:, :, 0:half], sin[:, :, half:DC].to_broadcast([P, B, half]), ALU.mult)
                pool.tensor_tensor(kvr[:], ctxd[:], cst[:, C_CK:C_CK + DC].unsqueeze(1).to_broadcast([P, B, DC]), ALU.mult).then_inc(pchain, 1)
                pool.wait_ge(pchain, 1)
                pool.tensor_tensor(kvr[:], kvr[:], rot[:], ALU.add).then_inc(pchain, 1)
                pool.wait_ge(pchain, 2)
                pool.wait_ge(loaded["x"], 16)

            @block.vector
            def _(dve):
                n_chain = [0]

                def link(ins):
                    n_chain[0] += 1
                    ins.then_inc(chain, 1)
                    dve.wait_ge(chain, n_chain[0])

                if phase == 1:
                    std.vector(dve, ln_mv, ln_rs)
                    for n in range(1, len(jobs), 2):
                        kind, k = jobs[n]
                        if jobs[n] == ("qr", 1):
                            dve.wait_ge(zeroed, 2)
                        if kind == "Cl":
                            dve.wait_ge(act_out, n // 2 + 1)
                            high = Cw[0][:, :, k // 2, :].bitcast(F32)
                            prod = banks[(n - 1) % 8][:, 0:2 * DCQ].rearrange("p (u q) -> p u q", u=2)
                            for (dst, src), (lead, _) in zip(by_pair(k % 2, Cw[1][:, :, k // 2, :], prod), by_pair(k % 2, high, prod)):
                                last = dve.tensor_tensor(dst, src, lead, ALU.subtract)
                            last.then_inc(dve_out, 1)
                        elif kind == "Vl":
                            dve.wait_ge(act_out, n // 2 + 1)
                            dve.tensor_tensor(VT[1][:, k, :], banks[(n - 1) % 8][:, 0:D], VT[0][:, k, :].bitcast(F32), ALU.subtract).then_inc(dve_out, 1)
                        else:
                            dve.wait_ge(done, n + 1)
                            copy_out(dve.tensor_copy, jobs[n], banks[n % 8], dve_out)
                    return
                for k in range(3):
                    dve.wait_ge(loaded[f"w{k}"], 16)
                    dve.tensor_reduce(part[:, k:k + 1], w3[k][:], AX.X, ALU.add, apply_absolute_value=True).then_inc(absum, 1)
                    dve.wait_ge(summed, k + 1)
                    link(dve.tensor_scalar(tern[:, k, 0:1], banks[2 * k + 1][:, 0:1], 1.0 / (DE * D), 1e-8, ALU.mult, ALU.add))
                    dve.tensor_scalar(tern[:, k, 1:2], tern[:, k, 0:1], 0.5, None, ALU.mult)
                    link(dve.tensor_scalar(tern[:, k, 2:3], tern[:, k, 0:1], -0.5, None, ALU.mult))
                    wait(dve, quant, k)
                    link(dve.tensor_scalar(pos[:], w3[k][:], tern[:, k, 2:3], None, ALU.is_lt))
                    dve.scalar_tensor_tensor(q3[k][:], w3[k][:], tern[:, k, 1:2], pos[:], ALU.is_gt, ALU.subtract).then_inc(quant, 1)
                dve.wait_ge(gats, 1)
                dve.tensor_scalar(fsc[:, 0:1], tern[:, 0, 0:1], 1.0 / XS, None, ALU.mult)
                link(dve.tensor_scalar(fsc[:, 3:4], tern[:, 0, 0:1], 4.0 * XS, None, ALU.mult))
                link(dve.reciprocal(fsc[:, 1:2], fsc[:, 3:4]))
                link(dve.tensor_tensor(fsc[:, 2:3], tern[:, 0, 0:1], tern[:, 1, 0:1], ALU.mult))
                link(dve.tensor_tensor(fsc[:, 3:4], tern[:, 2, 0:1], gat[:, 2:3], ALU.mult))
                link(dve.tensor_tensor(fsc[:, 2:3], fsc[:, 2:3], fsc[:, 3:4], ALU.mult))
                link(dve.tensor_scalar(fsc[:, 2:3], fsc[:, 2:3], 4.0, None, ALU.mult))
                for n in range(1, len(jobs), 2):
                    kind, k = jobs[n]
                    if kind == "ctxl":
                        dve.wait_ge(act_out, n // 2 + 1)
                        four = slice(4 * k, 4 * k + 4)
                        dve.tensor_tensor(ctxK[64:P, four, :], banks[(n - 1) % 8][0:64, :].rearrange("p (n c) -> p n c", n=4),
                                          ctxK[0:64, four, :].bitcast(F32), ALU.subtract).then_inc(dve_out, 1)
                    else:
                        dve.wait_ge(done, n + 1)
                        copy_out(dve.tensor_copy, jobs[n], banks[n % 8], dve_out)
                dve.wait_ge(loaded["x"], 16)
                for t in range(TILES):
                    dve.bn_stats(stats[:, t, :], x[:, t, :]).then_inc(chain, 1)
                n_chain[0] += TILES
                dve.wait_ge(chain, n_chain[0])
                for t in range(TILES):
                    dve.bn_aggr(ln_mv[:, t, :], stats[:, t, :])

            @block.tensor
            def _(pe):
                if phase == 0:
                    pe.wait_ge(loaded["cst"], 16)
                    for k in range(3):
                        pe.wait_ge(absum, k + 1)
                        pe.matmul(banks[2 * k + 1][:, 0:1], cst[:, C_ONES:C_ONES + P], part[:, k:k + 1], start=True, stop=True).then_inc(summed, 1)
                if phase == 0:
                    pe.wait_ge(zeroed, 1)
                for n, (kind, k) in enumerate(jobs):
                    bank = banks[n % 8]
                    if kind in ("Cl", "ctxl", "Vl"):
                        continue
                    if n >= 8:
                        copied_out(pe, n - 7)
                    if kind == "ctx":
                        pe.wait_ge(loaded["ctx"], 16)
                        for q in range(4):
                            last = pe.transpose(bank[0:64, P * q:P * q + P], ctx_tok[:, 4 * k + q, :], ident)
                    elif kind == "qr":
                        pe.wait_ge(loaded["wqr"], 16)
                        for h in range(2):
                            for u in range(2):
                                c = 192 * h + 96 * u
                                last = pe.transpose(bank[0:64, c:c + 96], wqr[0:96, 2 * k + h, u, :], ident[0:96, 0:96])
                    elif kind == "kr":
                        pe.wait_ge(loaded["wkr"], 16)
                        for hp in range(HP):
                            last = pe.transpose(bank[:, 64 * hp:64 * hp + 64],
                                                wkr[0:64, 2 * hp:2 * hp + 2, :].rearrange("c h r -> c (h r)"), ident[0:64, 0:64])
                    elif kind == "C":
                        pe.wait_ge(loaded["wq"], 16)
                        pe.wait_ge(loaded["wcq"], 16)
                        for u in range(2):
                            last = pe.matmul(bank[:, DCQ * u:DCQ * u + DCQ], wq[:, k, P * u:P * u + P], wcq[:, k, :], start=True, stop=True)
                    elif kind == "wo":
                        pe.wait_ge(loaded["wo"], 16)
                        for h in range(2):
                            for u in range(2):
                                c = D * h + P * u
                                last = pe.transpose(bank[:, c:c + P], wo[:, u, P * (2 * k + h):P * (2 * k + h) + P], ident)
                    elif kind == "N":
                        copied_out(pe, max(at["qr", k], at["kr", 0]))
                        for r in range(QR):
                            last = pe.matmul(bank[:, P * r:P * r + P], qrT[:, k, P * r:P * r + P], krT[:, k, :], start=True, stop=True)
                    elif kind == "V":
                        copied_out(pe, at["wo", k])
                        pe.wait_ge(loaded["wck"], 16)
                        for h in range(2):
                            last = pe.matmul(bank[64 * h:64 * h + 64, 0:D], wck[:, 2 * k + h, :], woT[:, 2 * k + h, :], start=True, stop=True)
                    elif kind in ("up", "gate"):
                        pe.wait_ge(quant, {"up": 1, "gate": 2}[kind])
                        src = q3[{"up": 0, "gate": 1}[kind]][:].rearrange("p (u d) -> p u d", u=ME)
                        for u in range(ME):
                            last = pe.transpose(bank[:].bitcast(F16)[:, P * u:P * u + P], src[:, u, P * k:P * k + P], identh[:])
                    elif kind == "down":
                        pe.wait_ge(quant, 3)
                        for u in range(ME):
                            last = pe.transpose(bank[:].bitcast(F16)[:, P * u:P * u + P],
                                                q3[2][:, DE * k + P * u:DE * k + P * u + P], identh[:])
                    last.then_inc(done, 2 if kind in ("C", "ctx", "V") else 1)


class InverseStd:

    def __init__(self, m):
        self.ve = m.sb("ve", [P, TILES])
        self.root = m.sb("root", [P, TILES])
        self.tmp = m.sb("tmp", [P, TILES])
        self.ve_ready = m.sem("ve_ready")
        self.rooted = m.sem("rooted")
        self.newton = m.sem("newton")

    def scalar(self, act):
        act.wait_ge(self.ve_ready, 1)
        act.activation(self.root[:], self.ve[:], ACT.Sqrt).then_inc(self.rooted, 1)

    def vector(self, dve, ln_mv, ln_rs):
        ve, tmp, newton = self.ve, self.tmp, self.newton
        dve.tensor_scalar(ve[:], ln_mv[:, :, 1], EPS_LN, None, ALU.add).then_inc(self.ve_ready, 1)
        dve.wait_ge(self.rooted, 1)
        dve.reciprocal(ln_rs[:], self.root[:]).then_inc(newton, 1)
        dve.wait_ge(newton, 1)
        dve.tensor_tensor(tmp[:], ln_rs[:], ln_rs[:], ALU.mult).then_inc(newton, 1)
        dve.wait_ge(newton, 2)
        dve.tensor_tensor(tmp[:], tmp[:], ve[:], ALU.mult).then_inc(newton, 1)
        dve.wait_ge(newton, 3)
        dve.tensor_scalar(tmp[:], tmp[:], -0.5, 1.5, ALU.mult, ALU.add).then_inc(newton, 1)
        dve.wait_ge(newton, 4)
        dve.tensor_tensor(ln_rs[:], ln_rs[:], tmp[:], ALU.mult).then_inc(newton, 1)
        dve.wait_ge(newton, 5)


def add_part(part, dve, t, y, scale, x, xt, st, mv, ln_mv, added):
    wait(dve, added, 4 * t + part)
    if part == 0:
        dve.scalar_tensor_tensor(xt[:], y, scale, x[:, t, :], ALU.mult, ALU.add).then_inc(added, 1)
    elif part == 1:
        dve.bn_stats(st[:], xt[:]).then_inc(added, 1)
    elif part == 2:
        dve.tensor_scalar(x[:, t, :], xt[:], 1.0, None, ALU.mult)
        dve.bn_aggr(mv[:], st[:]).then_inc(added, 1)
    else:
        dve.tensor_scalar(ln_mv[:, t, :], mv[:], 1.0, None, ALU.mult).then_inc(added, 1)


def add_and_count(dve, t, y, scale, x, xt, st, mv, ln_mv, added):
    for part in range(4):
        add_part(part, dve, t, y, scale, x, xt, st, mv, ln_mv, added)


def attention0(nc, a, cst, x, ln_mv, ln_rs, gat, ident, ctxK, ctxd, ones, raw, raw_in, sh, sh_in):
    with ExitStack() as ctx:
        m = Mem(nc, ctx, "a")
        std = InverseStd(m)
        xn = [m.sb(f"xn{u}", [P, G, 2, 64]) for u in range(2)]
        st = m.sb("st", [P, 6])
        mv = m.sb("mv", [P, 2])
        xt = m.sb("xt", [P, D])
        q1 = [m.sb(f"q1_{u}", [P, 2, G, S], F32R) for u in range(2)]
        q2 = [m.sb(f"q2_{u}", [80, 2, G, S], F32R) for u in range(2)]
        k1 = [m.sb(f"k1_{u}", [P, 2, KVH, T], F32R) for u in range(2)]
        k2 = [m.sb(f"k2_{u}", [80, 2, KVH, T], F32R) for u in range(2)]
        vB = [m.sb(f"vB{u}", [P, 2, 4, 2, 16]) for u in range(2)]
        pr = [m.sb(f"pr{u}", [P, 2, 4, G, S]) for u in range(2)]
        mx = m.sb("mx", [P, 4, KVH])
        ms = m.sb("ms", [P, 4, 2 * KVH], F32R)
        oT = m.sb("oT", [P, G, 2, S])
        rden = m.sb("rden", [P, G, KVH])
        att = m.sb("att", [P, D])
        q_ps = m.ps("q_ps", [P, G, P])
        m_ps = [m.ps(f"m_ps{n}", [P, 512]) for n in range(2)]
        mT_ps = m.ps("mT_ps", [2 * KVH, 4, P])
        s_ps = [m.ps(f"s_ps{n}", [P, 512]) for n in range(2)]
        oT_ps = m.ps("oT_ps", [P, 2, G * S])
        o_ps = m.ps("o_ps", [P, G, KVH, 16])
        SC = float(HD) ** -0.5

        xn_ready = m.sem("xn_ready")
        q_done = m.sem("q_done")
        q_lead = m.sem("q_lead")
        q_rest = m.sem("q_rest")
        k_ready = m.sem("k_ready")
        k_copied = m.sem("k_copied")
        v_ready = m.sem("v_ready")
        scored = m.sem("scored")
        maxed = m.sem("maxed")
        split = m.sem("split")
        mT_done = m.sem("mT_done")
        mT_copied = m.sem("mT_copied")
        sT_done = m.sem("sT_done")
        exped = m.sem("exped")
        pv_done = m.sem("pv_done")
        oT_copied = m.sem("oT_copied")
        o_done = m.sem("o_done")
        nrm = m.sem("nrm")
        added = m.sem("added")
        init = m.sem("init")

        with nc.Block() as block:
            @block.sync
            def _(sp):
                for name, dst, src in (
                        ("wqr", raw["wqr"][0:96], a["L1_xattn_W_qr"].rearrange("h (u q) r -> q h u r", u=2)),
                        ("wkr", raw["wkr"][0:64], a["L1_xattn_W_kr"].rearrange("h c r -> c h r")),
                        ("wq", raw["wq"][:], a["L1_xattn_Wq"].rearrange("(h k) d -> k h d", h=H1)),
                        ("wcq", raw["wcq"][:], a["L1_xattn_w_kc_q"].rearrange("h k q -> k h q")),
                        ("wo", raw["wo"][:], a["L1_xattn_Wo"].rearrange("(u i) k -> i u k", u=2)),
                        ("wck", raw["wck"][:], a["L1_xattn_w_kc_kv"].rearrange("h k c -> k h c"))):
                    sp.dma_start(dst, src).then_inc(raw_in[name], 16)
                for dst, src in (("rw", a["L1_ffn_router_weight"]), ("bias", a["L1_ffn_e_bias"].rearrange("(o e) -> o e", o=1).to_broadcast([P, E])),
                                 ("swg", a["L1_ffn_sh_gate"].rearrange("(k d) i -> d k i", k=2)),
                                 ("swu", a["L1_ffn_sh_up"].rearrange("(k d) i -> d k i", k=2)), ("swd", a["L1_ffn_sh_down"])):
                    sp.dma_start(sh[dst][:], src).then_inc(sh_in, 16)

            @block.gpsimd
            def _(pool):
                for u in range(2):
                    pool.memset(vB[u][:], 0.0).then_inc(init, 1)
                pool.wait_ge(init, 2)
                for u in range(2):
                    for h in range(2):
                        pool.memset(vB[u][64 * h:64 * h + 64, :, :, h, HD:HD + 1], 1.0).then_inc(init, 1)
                    pool.tensor_copy(k2[u][64:80], ones[64:80]).then_inc(init, 1)
                pool.wait_ge(init, 8)

                def keys(t, u):
                    for b in range(2):
                        wait(pool, sT_done, 4 * t - 6 + 2 * b)
                        wait(pool, k_copied, 2 * t - 3 + b)
                        src = ctxK[:, t, T * b:T * b + T].bitcast(F32).unsqueeze(1).to_broadcast([P, KVH, T])
                        mask = cst[:, C_KM:C_KM + 8].unsqueeze(2).to_broadcast([P, KVH, T])
                        pool.tensor_tensor(k1[u][:, b], src, mask, ALU.mult).then_inc(k_ready, 1)

                def values(t, u):
                    wait(pool, pv_done, t - 1)
                    for h in range(2):
                        rows = slice(64 * h, 64 * h + 64)
                        for b in range(2):
                            src = ctxd[rows, 2 * t + b, :].rearrange("p (n h d) -> p n h d", n=4, h=2)[:, :, h, :]
                            last = pool.tensor_copy(vB[u][rows, b, :, h, 0:HD], src)
                    last.then_inc(v_ready, 1)

                def step(t, u):
                    if within(t + 2):
                        pool.wait_ge(v_ready, t + 1)
                        keys(t + 2, u)
                    if within(t + 1):
                        pool.wait_ge(k_ready, 2 * t + 6 if within(t + 2) else 2 * TILES)
                        values(t + 1, 1 - u)
                keys(0, 0)
                keys(1, 1)
                pool.wait_ge(k_ready, 4)
                values(0, 0)
                over_tiles(pool, step, 4)

            @block.vector
            def _(dve):
                std.vector(dve, ln_mv, ln_rs)

                def norm(t, u):
                    wait(dve, q_done, t - 1)
                    for k in range(2):
                        last = dve.tensor_scalar(xn[u][:, :, k, :].rearrange("p g (j d) -> p j g d", j=KVH), x[:, t, :].rearrange("p (j g d) -> p j g d", j=KVH, g=G),
                                                 ln_mv[:, t, 0:1], ln_rs[:, bass.ds(t, 1)], ALU.subtract, ALU.mult)
                    last.then_inc(xn_ready, 1)

                def rest(t, u):
                    dve.wait_ge(q_lead, t + 1)
                    wait(dve, sT_done, 4 * t - 4)
                    dve.tensor_tensor(q2[u][0:64].rearrange("p b g s -> p g b s"), q_ps[0:64].rearrange("p g (b s) -> p g b s", b=2),
                                      q1[u][0:64].bitcast(F32).rearrange("p b g s -> p g b s"), ALU.subtract).then_inc(q_rest, 1)

                def maxima(t, u):
                    wait(dve, split, 2 * t)
                    for n in range(4):
                        dve.wait_ge(scored, 4 * t + n + 1)
                        dve.tensor_reduce(mx[:, n, :], m_ps[n % 2][:].rearrange("p (j t) -> p j t", j=KVH), AX.X, ALU.max).then_inc(maxed, 1)
                        if not isinstance(t, int) or t > 3:
                            add(t - 4, n)
                        if n == 1 and (not isinstance(t, int) or 0 < t < TILES - 1):
                            norm(t + 1, 1 - u)
                    dve.wait_ge(maxed, 4 * t + 4)
                    wait(dve, mT_done, 1 * t)
                    dve.tensor_scalar(ms[:, :, 0:KVH], mx[:], -1.0, None, ALU.mult).then_inc(split, 1)
                    dve.wait_ge(split, 2 * t + 1)
                    dve.scalar_tensor_tensor(ms[:, :, KVH:2 * KVH], mx[:], -1.0, ms[:, :, 0:KVH].bitcast(F32), ALU.mult, ALU.subtract).then_inc(split, 1)

                def output(t):
                    wait(dve, added, 4 * t)
                    dve.wait_ge(o_done, t + 1)
                    dve.reciprocal(rden[:], o_ps[:, :, :, HD]).then_inc(nrm, 1)
                    dve.wait_ge(nrm, 2 * t + 1)
                    dve.tensor_tensor(att[:].rearrange("p (j g d) -> p g j d", j=KVH, g=G), o_ps[:, :, :, 0:HD],
                                      rden[:].unsqueeze(3).to_broadcast([P, G, KVH, HD]), ALU.mult).then_inc(nrm, 1)

                def add(t, part):
                    if part == 0:
                        dve.wait_ge(nrm, 2 * t + 2)
                    add_part(part, dve, t, att[:], gat[:, 0:1], x, xt, st, mv, ln_mv, added)

                def step(t, u):
                    if within(t + 1):
                        maxima(t + 1, 1 - u)
                    if within(t + 2):
                        rest(t + 2, u)
                    if not isinstance(t, int) or 1 < t < TILES - 1:
                        output(t - 2)
                norm(0, 0)
                norm(1, 1)
                rest(0, 0)
                rest(1, 1)
                maxima(0, 0)
                over_tiles(dve, step, 4)
                for t in range(TILES - 4, TILES):
                    if t > TILES - 4:
                        output(t)
                    for part in range(4):
                        add(t, part)

            @block.scalar
            def _(act):
                std.scalar(act)

                def lead(t, u):
                    act.wait_ge(q_done, t + 1)
                    wait(act, sT_done, 4 * t - 4)
                    act.copy(q1[u][:].rearrange("p b g s -> p g b s"), q_ps[:].rearrange("p g (b s) -> p g b s", b=2)).then_inc(q_lead, 1)

                def keys(t, u, b):
                    act.wait_ge(k_ready, 2 * t + b + 1)
                    wait(act, sT_done, 4 * t - 6 + 2 * b)
                    act.copy(k2[u][0:64, b], k1[u][0:64, b].bitcast(F32)).then_inc(k_copied, 1)

                def maximum(t, u):
                    act.wait_ge(mT_done, t + 1)
                    wait(act, sT_done, 4 * t - 4)
                    act.copy(q2[u][64:80], mT_ps[:]).then_inc(mT_copied, 1)

                def output(t):
                    act.wait_ge(pv_done, t + 1)
                    wait(act, o_done, 1 * t)
                    act.copy(oT[:].rearrange("p g b s -> p b g s"), oT_ps[:].rearrange("p b (g s) -> p b g s", g=G)).then_inc(oT_copied, 1)

                def step(t, u):
                    wait(act, pv_done, t - 1)
                    for n in range(4):
                        act.wait_ge(sT_done, 4 * t + n + 1)
                        act.activation(pr[u][:, n // 2, 2 * (n % 2):2 * (n % 2) + 2], s_ps[n % 2][:], ACT.Exp, scale=SC).then_inc(exped, 1)
                    if within(t + 2):
                        lead(t + 2, u)
                        keys(t + 2, u, 0)
                    if within(t + 1):
                        maximum(t + 1, 1 - u)
                    if within(t + 2):
                        keys(t + 2, u, 1)
                    if not isinstance(t, int) or t > 0:
                        output(t - 1)
                lead(0, 0)
                lead(1, 1)
                for t in range(2):
                    for b in range(2):
                        keys(t, t, b)
                maximum(0, 0)
                over_tiles(act, step, 4)
                output(TILES - 1)

            @block.tensor
            def _(pe):
                def queries(t, u):
                    pe.wait_ge(xn_ready, t + 1)
                    wait(pe, q_lead, 1 * t)
                    wait(pe, q_rest, 1 * t)
                    for g in range(G):
                        last = pe.transpose(q_ps[:, g, :], xn[u][:, g].rearrange("p c f -> p (c f)"), ident)
                    last.then_inc(q_done, 1)

                def score(t, u, n):
                    if n == 0:
                        pe.wait_ge(q_lead, t + 1)
                        pe.wait_ge(q_rest, t + 1)
                    wait(pe, maxed, 4 * t + n - 1)
                    if n % 2 == 0:
                        pe.wait_ge(k_copied, 2 * t + n // 2 + 1)
                    b, g = n // 2, slice(2 * (n % 2), 2 * (n % 2) + 2)
                    pe.matmul(m_ps[n % 2][:], q1[u][:, b, g, :], k1[u][:, b], start=True, stop=False)
                    pe.matmul(m_ps[n % 2][:], q2[u][0:64, b, g, :], k2[u][0:64, b], start=False, stop=True).then_inc(scored, 1)

                def maximum(t, u):
                    pe.wait_ge(split, 2 * t + 2)
                    wait(pe, mT_copied, 1 * t)
                    for n in range(4):
                        last = pe.transpose(mT_ps[:, n, :], ms[:, n, :].bitcast(F32), ident)
                    last.then_inc(mT_done, 1)

                def score_less_maximum(t, u, n):
                    pe.wait_ge(mT_copied, t + 1)
                    wait(pe, exped, 4 * t + n - 1)
                    b = n // 2
                    for k in range(2):
                        jp = 2 * (n % 2) + k
                        dst = s_ps[n % 2][:, 256 * k:256 * k + 256]
                        pe.matmul(dst, k1[u][:, b, 2 * jp:2 * jp + 2, :], q1[u][:, b], start=True, stop=False)
                        last = pe.matmul(dst, k2[u][:, b, 2 * jp:2 * jp + 2, :], q2[u][:, b], start=False, stop=True)
                    last.then_inc(sT_done, 1)

                def values(t, u):
                    pe.wait_ge(exped, 4 * t + 4)
                    pe.wait_ge(v_ready, t + 1)
                    wait(pe, oT_copied, 1 * t)
                    for b in range(2):
                        for jp in range(4):
                            last = pe.matmul(oT_ps[32 * jp:32 * jp + 32, b, :], vB[u][:, b, jp].rearrange("p h d -> p (h d)"), pr[u][:, b, jp], start=True, stop=True)
                    last.then_inc(pv_done, 1)

                def output(t):
                    pe.wait_ge(oT_copied, t + 1)
                    wait(pe, nrm, 2 * t)
                    for g in range(G):
                        last = pe.transpose(o_ps[:, g].rearrange("p j d -> p (j d)"), oT[:, g].rearrange("p b s -> p (b s)"), ident)
                    last.then_inc(o_done, 1)

                def step(t, u):
                    for ahead, banks in ((1, (0, 1)), (0, (0, 1)), (1, (2,)), (0, (2,)), (1, (3,)), (0, (3,))):
                        for n in banks:
                            if ahead == 0:
                                score_less_maximum(t, u, n)
                            elif within(t + 1):
                                score(t + 1, 1 - u, n)
                        if ahead == 0 and n == 1 and (not isinstance(t, int) or t > 1):
                            output(t - 2)
                    if within(t + 2):
                        queries(t + 2, u)
                    if not isinstance(t, int) or t > 0:
                        values(t - 1, 1 - u)
                    if within(t + 1):
                        maximum(t + 1, 1 - u)
                queries(0, 0)
                queries(1, 1)
                for n in range(4):
                    score(0, 0, n)
                maximum(0, 0)
                over_tiles(pe, step, 4)
                output(TILES - 2)
                values(TILES - 1, 1)
                output(TILES - 1)


def normalise_chunk(dve, c, x, ln_mv, ln_rs, xn, xn_ready):
    for q in range(QT):
        t = QT * c + q
        last = dve.tensor_scalar(xn[:, q, :], x[:, t, :], ln_mv[:, t, 0:1], ln_rs[:, bass.ds(t, 1)], ALU.subtract, ALU.mult)
    last.then_inc(xn_ready, 1)


def over_chunks(eng, step):
    step(0)
    with eng.Fori(1, CHUNKS - 1) as c:
        step(c)
    step(CHUNKS - 1)


def ffn0(nc, x, ln_mv, ln_rs, ident, k_up, k_gate, k_down, fsc):
    with ExitStack() as ctx:
        m = Mem(nc, ctx, "f")
        std = InverseStd(m)
        st = m.sb("st", [P, 6])
        mv = m.sb("mv", [P, 2])
        xt = m.sb("xt", [P, D])
        xn = m.sb("xn", [P, QT, D])
        xh = m.sb("xh", [P, 2, CH], F16)
        xl = m.sb("xl", [P, 2, CH], F16)
        sg = [m.sb(f"sg{n}", [P, CH]) for n in range(2)]
        h = [m.sb(f"h{n}", [P, CH]) for n in range(2)]
        hh = m.sb("hh", [P, ME, CH], F16)
        hl = m.sb("hl", [P, ME, CH], F16)
        xT_ps = m.ps("xT_ps", [P, 2, CH])
        u_ps = [m.ps(f"u_ps{n}", [P, CH]) for n in range(2)]
        g_ps = [m.ps(f"g_ps{n}", [P, CH]) for n in range(2)]
        d_ps = [m.ps(f"d_ps{n}", [P, D]) for n in range(2)]

        xn_ready = m.sem("xn_ready")
        xT_done = m.sem("xT_done")
        xh_done = m.sem("xh_done")
        xl_done = m.sem("xl_done")
        u_done = m.sem("u_done")
        g_done = m.sem("g_done")
        silu = m.sem("silu")
        h_done = m.sem("h_done")
        hh_done = m.sem("hh_done")
        hl_done = m.sem("hl_done")
        d_done = m.sem("d_done")
        added = m.sem("added")

        with nc.Block() as block:
            @block.vector
            def _(dve):
                std.vector(dve, ln_mv, ln_rs)

                def norm(c):
                    wait(dve, xT_done, 1 * c)
                    normalise_chunk(dve, c, x, ln_mv, ln_rs, xn, xn_ready)

                def x_low(c):
                    for k in range(2):
                        dve.wait_ge(xh_done, 2 * c + k + 1)
                        dve.scalar_tensor_tensor(xl[:, k, :], xT_ps[:, k, :], XS, xh[:, k, :], ALU.mult, ALU.subtract).then_inc(xl_done, 1)

                def product(c, n):
                    dve.wait_ge(silu, 8 * c + n + 1)
                    dve.wait_ge(g_done, 8 * c + n + 1)
                    wait(dve, hl_done, 8 * c + n - 1)
                    dve.scalar_tensor_tensor(h[n % 2][:], sg[n % 2][:], fsc[:, 1:2], g_ps[n % 2][:], ALU.mult, ALU.mult).then_inc(h_done, 1)

                def low(c, n):
                    dve.wait_ge(hh_done, 8 * c + n + 1)
                    dve.tensor_tensor(hl[:, n, :], h[n % 2][:], hh[:, n, :], ALU.subtract).then_inc(hl_done, 1)

                def step(c):
                    if within(c + 1, CHUNKS):
                        norm(c + 1)
                    product(c, 0)
                    for n in range(ME):
                        if n + 1 < ME:
                            product(c, n + 1)
                        low(c, n)
                    if within(c + 1, CHUNKS):
                        x_low(c + 1)
                    for q in range(QT):
                        dve.wait_ge(d_done, QT * c + q + 1)
                        wait(dve, added, 4 * (QT * c + q))
                        add_and_count(dve, QT * c + q, d_ps[q % 2][:], fsc[:, 2:3], x, xt, st, mv, ln_mv, added)
                norm(0)
                x_low(0)
                over_chunks(dve, step)

            @block.scalar
            def _(act):
                std.scalar(act)

                def x_high(c):
                    act.wait_ge(xT_done, c + 1)
                    for k in range(2):
                        act.mul(xh[:, k, :], xT_ps[:, k, :], XS).then_inc(xh_done, 1)

                def silus(c, n):
                    act.wait_ge(u_done, 8 * c + n + 1)
                    wait(act, h_done, 8 * c + n - 1)
                    act.activation(sg[n % 2][:], u_ps[n % 2][:], ACT.Silu, scale=fsc[:, 0:1]).then_inc(silu, 1)

                def step(c):
                    silus(c, 0)
                    for n in range(ME):
                        if n + 1 < ME:
                            silus(c, n + 1)
                        act.wait_ge(h_done, 8 * c + n + 1)
                        if n == 0:
                            wait(act, d_done, QT * c)
                        act.copy(hh[:, n, :], h[n % 2][:]).then_inc(hh_done, 1)
                    if within(c + 1, CHUNKS):
                        x_high(c + 1)
                x_high(0)
                over_chunks(act, step)

            @block.tensor
            def _(pe):
                def transposes(c):
                    pe.wait_ge(xn_ready, c + 1)
                    wait(pe, xl_done, 2 * c)
                    for k in range(2):
                        for q in range(QT):
                            last = pe.transpose(xT_ps[:, k, P * q:P * q + P], xn[:, q, P * k:P * k + P], ident)
                    last.then_inc(xT_done, 1)

                def step(c):
                    pe.wait_ge(xl_done, 2 * c + 2)
                    for n in range(ME):
                        for w, ps, sem, used in ((k_up, u_ps, u_done, silu), (k_gate, g_ps, g_done, h_done)):
                            wait(pe, used, 8 * c + n - 1)
                            for k in range(2):
                                for part in (xh, xl):
                                    last = pe.matmul(ps[n % 2][:], w[:, k, P * n:P * n + P], part[:, k, :],
                                                     start=(k == 0 and part is xh), stop=(k == 1 and part is xl))
                            last.then_inc(sem, 1)
                    if within(c + 1, CHUNKS):
                        transposes(c + 1)
                    for q in range(QT):
                        wait(pe, added, 4 * (QT * c + q) - 7)
                        for n in range(ME):
                            if q == 0:
                                pe.wait_ge(hl_done, 8 * c + n + 1)
                            for part in (hh, hl):
                                last = pe.matmul(d_ps[q % 2][:], part[:, n, P * q:P * q + P], k_down[:, n, :],
                                                 start=(n == 0 and part is hh), stop=(n == ME - 1 and part is hl))
                        last.then_inc(d_done, 1)
                transposes(0)
                over_chunks(pe, step)


def attention1(nc, cst, x, ln_mv, ln_rs, gat, ident, Cw, NB, VT, kvr, raw):
    with ExitStack() as ctx:
        m = Mem(nc, ctx, "c")
        st = m.sb("st", [P, 6])
        mv = m.sb("mv", [P, 2])
        xt = m.sb("xt", [P, D])
        xT = [m.sb(f"xT{n}", [P, 2, CH], F32R) for n in range(2)]
        vB = [m.sb(f"vB{u}", [P, 2, P]) for u in range(2)]
        kB = [m.sb(f"kB{u}", [P, 2, P]) for u in range(2)]
        mx = m.sb("mx", [P, H1])
        sm = m.sb("sm", [P, H1])
        rs = m.sb("rs", [P, H1])
        cT = [m.sb(f"cT{n}", [P, HP, P], F32R) for n in range(2)]
        EARLY = HP - 2
        qn = raw["wq"][:].rearrange("p h d -> p (h d)").rearrange("p (n t) -> p n t", n=HP)
        qe = raw["wcq"][:].rearrange("p h q -> p (h q)").rearrange("p (n t) -> p n t", n=EARLY)
        blocks8 = raw["wo"][:].rearrange("p u (n t) -> p (u n) t", t=CH)
        qr = [[blocks8[:, QR * u + r, :] for r in range(QR)] for u in range(2)]
        xn = blocks8[:, 2 * QR:2 * QR + 2, :].rearrange("p n t -> p (n t)").rearrange("p (q d) -> p q d", d=D)
        blocks4 = raw["wqr"][:].rearrange("p h u r -> p (h u r)").rearrange("p (n t) -> p n t", t=CH)
        qs = [blocks4[:, r, :] for r in range(QR)]
        sc = raw["wck"][:]
        pT = raw["wkr"][:].rearrange("p h r -> p (h r)").rearrange("p (n t) -> p n t", t=P)
        q_ps = [m.ps(f"q_ps{r}", [P, CH]) for r in range(QR)]
        n_ps = m.ps("n_ps", [P, CH])
        s_ps = [m.ps(f"s_ps{n}", [P, 512]) for n in range(2)]
        v_ps = [m.ps(f"v_ps{n}", [P, 512]) for n in range(2)]

        zeroed = m.sem("zeroed")
        xn_ready = m.sem("xn_ready")
        xT_done = m.sem("xT_done")
        xT_lead = m.sem("xT_lead")
        xT_rest = m.sem("xT_rest")
        q_done = m.sem("q_done")
        q_used = m.sem("q_used")
        roped = m.sem("roped")
        n_used = m.sem("n_used")
        n_copied = m.sem("n_copied")
        moved = m.sem("moved")
        vB_ready = m.sem("vB_ready")
        kB_done = m.sem("kB_done")
        kB_copied = m.sem("kB_copied")
        s_done = m.sem("s_done")
        maxed = m.sem("maxed")
        shifted = m.sem("shifted")
        exped = m.sem("exped")
        summed = m.sem("summed")
        pnorm = m.sem("pnorm")
        p_done = m.sem("p_done")
        p_copied = m.sem("p_copied")
        v_done = m.sem("v_done")
        v_lead = m.sem("v_lead")
        v_rest = m.sem("v_rest")
        o_done = m.sem("o_done")
        added = m.sem("added")

        def from_round(c, n):
            return not isinstance(c, int) or c >= n

        def projects(c):
            return not isinstance(c, int) or c < CHUNKS

        def over_rounds(eng, step):
            step(0)
            step(1)
            with eng.Fori(2, CHUNKS) as c:
                step(c)
        FINAL = range(TILES - QT, TILES)

        with nc.Block() as block:
            @block.gpsimd
            def _(pool):
                for u in range(2):
                    pool.memset(vB[u][:], 0.0).then_inc(zeroed, 1)
                pool.wait_ge(zeroed, 2)

                def blocks(t, u):
                    wait(pool, v_done, t - 1)
                    for h in range(2):
                        rows = slice(64 * h, 64 * h + 64)
                        last = pool.tensor_copy(vB[u][rows, :, 64 * h:64 * h + 64], kvr[rows, bass.ds(2 * t, 2), :])
                    last.then_inc(vB_ready, 1)

                def rotate(c, i):
                    n = HP * c + i
                    for r in range(QR):
                        pool.wait_ge(q_used, QR * n + max(r, 1) + 1)
                        pool.tensor_tensor(qr[i % 2][r], qr[i % 2][r], qs[r], ALU.add).then_inc(roped, 1)

                def step(c):
                    for i in range(HP):
                        if from_round(c, 1) and i % 2 == 0:
                            t = QT * c - QT + i // 2
                            pool.wait_ge(roped, QR * HP * c + QR * i)
                            blocks(t, i // 2 % 2)
                            pool.wait_ge(vB_ready, t + 1)
                        rotate(c, i)
                over_rounds(pool, step)
                pool.wait_ge(roped, QR * HP * CHUNKS)
                for t in FINAL:
                    blocks(t, t % 2)

            @block.vector
            def _(dve):
                cos = cst[:, C_CQ:C_CQ + QR * S].rearrange("p (r s) -> p r s", r=QR)
                sin = cst[:, C_SQ:C_SQ + QR * S].rearrange("p (r s) -> p r s", r=QR)

                def times(dst, q, tab, to=slice(0, P), of=slice(0, P)):
                    rows = to.stop - to.start
                    return dve.tensor_tensor(dst[to].rearrange("p (b s) -> p b s", s=S), q[of].rearrange("p (b s) -> p b s", s=S),
                                             tab[to].unsqueeze(1).to_broadcast([rows, CH // S, S]), ALU.mult)

                def rotate(c, i, between):
                    n = HP * c + i
                    wait(dve, roped, QR * n)
                    wait(dve, n_used, n - 1)
                    qc = qr[i % 2]
                    for r in range(2):
                        dve.wait_ge(q_done, QR * n + r + 1)
                        times(qc[r], q_ps[r], cos[:, r, :])
                        times(qs[1 - r], q_ps[r], sin[:, 1 - r, :]).then_inc(q_used, 1)
                    between()
                    dve.wait_ge(q_done, QR * n + 3)
                    times(qc[2], q_ps[2], cos[:, 2, :])
                    low, high = slice(0, 64), slice(64, P)
                    times(qs[2], q_ps[2], sin[:, 2, :], to=low, of=high)
                    times(qs[2], q_ps[2], sin[:, 2, :], to=high, of=low).then_inc(q_used, 1)

                def maximum(t):
                    dve.wait_ge(s_done, t + 1)
                    for k in range(2):
                        dve.tensor_reduce(mx[:, 8 * k:8 * k + 8], s_ps[k][:].rearrange("p (h t) -> p h t", t=T), AX.X, ALU.max).then_inc(maxed, 1)

                def shift(t):
                    dve.wait_ge(maxed, 2 * t + 2)
                    wait(dve, p_done, 2 * t)
                    for k in range(2):
                        last = dve.tensor_tensor(sc[:, 8 * k:8 * k + 8, :], s_ps[k][:].rearrange("p (h t) -> p h t", t=T),
                                                 mx[:, 8 * k:8 * k + 8].unsqueeze(2).to_broadcast([P, 8, T]), ALU.subtract)
                    last.then_inc(shifted, 1)

                def normalise(t):
                    dve.wait_ge(exped, t + 1)
                    dve.tensor_reduce(sm[:], sc, AX.X, ALU.add).then_inc(summed, 1)
                    dve.wait_ge(summed, 2 * t + 1)
                    dve.reciprocal(rs[:], sm[:]).then_inc(summed, 1)
                    dve.wait_ge(summed, 2 * t + 2)
                    dve.tensor_tensor(sc, sc, rs[:].unsqueeze(2).to_broadcast([P, H1, T]), ALU.mult).then_inc(pnorm, 1)

                def rest(t):
                    dve.wait_ge(v_lead, t + 1)
                    for b in range(2):
                        last = dve.tensor_tensor(cT[1][:, :, S * b:S * b + S], v_ps[b][:].rearrange("p (h s) -> p h s", s=S),
                                                 cT[0][:, :, S * b:S * b + S].bitcast(F32), ALU.subtract)
                    last.then_inc(v_rest, 1)

                def output(t, src):
                    wait(dve, added, 4 * t)
                    dve.wait_ge(o_done, t + 1)
                    add_and_count(dve, t, src[:, 0:D], gat[:, 1:2], x, xt, st, mv, ln_mv, added)

                def step(c):
                    normalise_chunk(dve, c, x, ln_mv, ln_rs, xn, xn_ready)
                    dve.wait_ge(xT_lead, c + 1)
                    for k in range(2):
                        last = dve.tensor_tensor(xT[1][:, k, :], s_ps[k][:], xT[0][:, k, :].bitcast(F32), ALU.subtract)
                    last.then_inc(xT_rest, 1)
                    for i in range(HP):
                        t = QT * c - QT + i // 2
                        attends = from_round(c, 1)
                        def between():
                            if attends and i % 2 == 1:
                                normalise(t)
                                if i > 1 or from_round(c, 2):
                                    output(t - 1, v_ps[0])
                        rotate(c, i, between)
                        if attends and i % 2 == 0:
                            if i or from_round(c, 2):
                                rest(t - 1)
                            maximum(t)
                            shift(t)
                over_rounds(dve, step)
                rest(FINAL[0] - 1)
                maximum(FINAL[0])
                shift(FINAL[0])
                normalise(FINAL[0])
                maximum(FINAL[1])
                for t in FINAL:
                    if within(t + 1):
                        shift(t + 1)
                        normalise(t + 1)
                    rest(t)
                    output(t - 1, n_ps)
                    if within(t + 2):
                        maximum(t + 2)
                output(TILES - 1, n_ps)

            @block.scalar
            def _(act):
                def values(t):
                    act.wait_ge(v_done, t + 1)
                    wait(act, o_done, t)
                    for b in range(2):
                        last = act.copy(cT[0][:, :, S * b:S * b + S], v_ps[b][:].rearrange("p (h s) -> p h s", s=S))
                    last.then_inc(v_lead, 1)

                def queries(c, i):
                    n = HP * c + i - 1
                    hp = (i - 1) % HP
                    act.wait_ge(n_used, n + 1)
                    if hp < EARLY:
                        wait(act, moved, 1 * c)
                        dst = qe
                    else:
                        dst = qn
                        wait(act, s_done, QT * (c - 1) if i == 0 else QT * c)
                    act.copy(dst[:, hp, :], n_ps[:]).then_inc(n_copied, 1)

                def keys(t, u):
                    act.wait_ge(kB_done, t + 1)
                    wait(act, s_done, t - 1)
                    act.copy(kB[u][:], s_ps[0][:, 0:2 * P]).then_inc(kB_copied, 1)

                def exps(t):
                    act.wait_ge(shifted, t + 1)
                    act.activation(sc, sc, ACT.Exp).then_inc(exped, 1)

                def probs(t, src):
                    for k in range(2):
                        act.wait_ge(p_done, 2 * t + k + 1)
                        if k == 0:
                            wait(act, v_done, t)
                        act.copy(pT[:, 4 * k:4 * k + 4, :], src[k][:]).then_inc(p_copied, 1)

                def step(c):
                    for i in range(HP):
                        t = QT * c - QT + i // 2
                        attends = from_round(c, 1)
                        if attends and i % 2 == 0 and (i or from_round(c, 2)):
                            values(t - 1)
                        if i == 0:
                            act.wait_ge(xT_done, c + 1)
                            for k in range(2):
                                last = act.copy(xT[0][:, k, :], s_ps[k][:])
                            last.then_inc(xT_lead, 1)
                        if i == 0 and attends:
                            queries(c, i)
                        if attends and i % 2 == 0:
                            keys(t, i // 2 % 2)
                        if i:
                            queries(c, i)
                        if attends and i % 2 == 0:
                            exps(t)
                        if attends and i % 2 == 1:
                            probs(t, v_ps)
                    wait(act, s_done, QT * c)
                    act.wait_ge(n_copied, HP * c + EARLY)
                    act.copy(qn[:, 0:EARLY, :], qe).then_inc(moved, 1)
                over_rounds(act, step)
                values(FINAL[0] - 1)
                queries(CHUNKS, 0)
                keys(FINAL[0], FINAL[0] % 2)
                exps(FINAL[0])
                keys(FINAL[1], FINAL[1] % 2)
                for t in FINAL:
                    probs(t, q_ps)
                    if within(t + 1):
                        exps(t + 1)
                    values(t)
                    if within(t + 2):
                        keys(t + 2, t % 2)

            @block.tensor
            def _(pe):
                def transpose_chunk(c):
                    pe.wait_ge(xn_ready, c + 1)
                    wait(pe, shifted, QT * (c - 1))
                    for k in range(2):
                        for q in range(QT):
                            last = pe.transpose(s_ps[k][:, P * q:P * q + P], xn[:, q, P * k:P * k + P], ident)
                    last.then_inc(xT_done, 1)

                def project(c, i):
                    n = HP * c + i
                    if i == 0:
                        pe.wait_ge(xT_lead, c + 1)
                        pe.wait_ge(xT_rest, c + 1)
                    for r in range(QR):
                        wait(pe, q_used, QR * n - QR + min(r + 1, 3))
                        parts = [(k, w, v) for k in range(2) for w, v in ((0, 0), (0, 1), (1, 0))]
                        for j, (k, w, v) in enumerate(parts):
                            last = pe.matmul(q_ps[r][:], Cw[w][:, k, i, P * r:P * r + P], xT[v][:, k, :], start=(j == 0), stop=(j == 5))
                        last.then_inc(q_done, 1)

                def combine(c, i):
                    n = HP * c + i - 1
                    wait(pe, n_copied, n)
                    for r in range(QR):
                        pe.wait_ge(roped, QR * n + r + 1)
                        last = pe.matmul(n_ps[:], NB[:, (i - 1) % HP, r, :], qr[(i - 1) % 2][r], start=(r == 0), stop=(r == QR - 1))
                    last.then_inc(n_used, 1)

                def keys(c, t, q):
                    pe.wait_ge(vB_ready, t + 1)
                    if q == 0 and projects(c):
                        pe.wait_ge(xT_lead, c + 1)
                        pe.wait_ge(xT_rest, c + 1)
                    wait(pe, shifted, t)
                    for b in range(2):
                        last = pe.transpose(s_ps[0][:, P * b:P * b + P], vB[q % 2][:, b, :], ident)
                    last.then_inc(kB_done, 1)

                def scores(c, t, q):
                    pe.wait_ge(kB_copied, t + 1)
                    pe.wait_ge(n_copied, HP * c)
                    pe.wait_ge(moved, 1 * c)
                    for b in range(2):
                        for hp in range(HP):
                            cols = slice(P * (hp % 4), P * (hp % 4) + P)
                            last = pe.matmul(s_ps[hp // 4][64 * b:64 * b + 64, cols], qn[:, hp, P * q + S * b:P * q + S * b + S],
                                             kB[q % 2][:, b, :], start=True, stop=True)
                    last.then_inc(s_done, 1)

                def transpose_probs(t, dst):
                    pe.wait_ge(pnorm, t + 1)
                    if dst is v_ps:
                        wait(pe, added, 4 * t - 3)
                        wait(pe, v_lead, t)
                        wait(pe, v_rest, t)
                    else:
                        pe.wait_ge(q_used, QR * HP * CHUNKS)
                        pe.wait_ge(p_copied, 2 * t)
                    for k in range(2):
                        for n in range(4):
                            hp = 4 * k + n
                            last = pe.transpose(dst[k][:, P * n:P * n + P], sc[:, 2 * hp:2 * hp + 2, :].rearrange("p h t -> p (h t)"), ident)
                        last.then_inc(p_done, 1)

                def values(t, u):
                    pe.wait_ge(p_copied, 2 * t + 2)
                    wait(pe, v_lead, t)
                    wait(pe, v_rest, t)
                    for b in range(2):
                        last = pe.matmul(v_ps[b][:].rearrange("p (h s) -> p h s", s=S), vB[u][:, b, :], pT[:, :, S * b:S * b + S],
                                         start=True, stop=True)
                    last.then_inc(v_done, 1)

                def output(t, dst):
                    if dst is n_ps and t in FINAL:
                        pe.wait_ge(added, 4 * t - 3)
                    pe.wait_ge(v_lead, t + 1)
                    pe.wait_ge(v_rest, t + 1)
                    parts = [(hp, u, v) for hp in range(HP) for u, v in ((0, 0), (0, 1), (1, 0))]
                    for j, (hp, u, v) in enumerate(parts):
                        last = pe.matmul(dst[:, 0:D], cT[u][:, hp, :], VT[v][:, hp, :], start=(j == 0), stop=(j == len(parts) - 1))
                    last.then_inc(o_done, 1)

                def step(c):
                    attends = from_round(c, 1)
                    for i in range(HP):
                        q = i // 2
                        t = QT * c - QT + q
                        before = i > 1 or from_round(c, 2)
                        if i:
                            project(c, i)
                        if attends and i % 2 == 0 and before:
                            values(t - 1, (q - 1) % 2)
                        if i == 0:
                            transpose_chunk(c)
                        if attends and i % 2 == 0 and i:
                            keys(c, t, q)
                        if attends and i % 2 == 1 and before:
                            output(t - 1, v_ps[0])
                        if i or attends:
                            combine(c, i)
                        if i == 0 and attends:
                            keys(c, t, q)
                        if i == 0:
                            project(c, 0)
                        if attends and i % 2 == 0:
                            scores(c, t, q)
                        if attends and i % 2 == 1:
                            transpose_probs(t, v_ps)
                over_rounds(pe, step)
                values(FINAL[0] - 1, 1)
                combine(CHUNKS, 0)
                for q in range(2):
                    keys(CHUNKS, FINAL[q], q)
                    scores(CHUNKS, FINAL[q], q)
                for q, t in enumerate(FINAL):
                    transpose_probs(t, q_ps)
                    output(t - 1, n_ps)
                    values(t, t % 2)
                    if within(t + 2):
                        keys(CHUNKS, t + 2, q + 2)
                        scores(CHUNKS, t + 2, q + 2)
                output(TILES - 1, n_ps)


def moe(nc, a, cst, x, ln_mv, ln_rs, gat, ident, out, xg_dram, acc_dram, sh, sh_in):
    with ExitStack() as ctx:
        m = Mem(nc, ctx, "m")
        idT = m.sb("idT", [CAP, E], U32)
        wg = [m.sb(f"wg{b}", [P, 2, I1]) for b in range(XB)]
        wu = [m.sb(f"wu{b}", [P, 2, I1]) for b in range(XB)]
        wd = [m.sb(f"wd{b}", [I1, D]) for b in range(XB)]
        weights = [m.sem(f"weights{b}") for b in range(XB)]

        def load_expert(sp, e, b):
            sp.dma_start(wg[b][:], a["L1_ffn_w_gate"][bass.ds(e, 1)].rearrange("o (k d) i -> d (o k) i", k=2)).then_inc(weights[b], 16)
            sp.dma_start(wu[b][:], a["L1_ffn_w_up"][bass.ds(e, 1)].rearrange("o (k d) i -> d (o k) i", k=2)).then_inc(weights[b], 16)
            sp.dma_start(wd[b][:], a["L1_ffn_w_down"][bass.ds(e, 1)].rearrange("o i d -> (o i) d")).then_inc(weights[b], 16)
        route_and_share(nc, a, cst, x, ln_mv, ln_rs, gat, ident, xg_dram, acc_dram, idT, load_expert, sh, sh_in)
        experts(nc, ident, xg_dram, acc_dram, idT, wg, wu, wd, weights, load_expert)
        total(nc, out, acc_dram)


def route_and_share(nc, a, cst, x, ln_mv, ln_rs, gat, ident, xg_dram, acc_dram, idT, load_expert, sh, sh_in):
    with ExitStack() as ctx:
        m = Mem(nc, ctx, "t")
        std = InverseStd(m)
        rw, bias, swg, swu, swd = (sh[name] for name in ("rw", "bias", "swg", "swu", "swd"))
        rwT = m.sb("rwT", [P, 2, E])
        zero = m.sb("zero", [P, XW])
        xn = m.sb("xn", [P, TILES, D])
        xT = m.sb("xT", [P, 2, TOK])
        gl = [m.sb(f"gl{u}", [I1, CH]) for u in range(2)]
        ul = [m.sb(f"ul{u}", [I1, CH]) for u in range(2)]
        hl = [m.sb(f"hl{u}", [I1, CH]) for u in range(2)]
        ol = [m.sb(f"ol{u}", [P, D]) for u in range(2)]
        scores = m.sb("scores", [P, TILES, E])
        biased = m.sb("biased", [P, TILES, E])
        hi = m.sb("hi", [P, TILES * NG, 4])
        lo = m.sb("lo", [P, TILES * NG, 4])
        hi2 = m.sb("hi2", [P, TILES * NG, 2])
        mi2 = m.sb("mi2", [P, TILES * NG, 2])
        lo2 = m.sb("lo2", [P, TILES * NG, 2])
        gs = m.sb("gs", [P, TILES, NG])
        g2 = m.sb("g2", [P, TILES, NG])
        w1 = m.sb("w1", [P, TILES, E])
        w2 = m.sb("w2", [P, TILES, E])
        sel = m.sb("sel", [P, TILES, E])
        prev = m.sb("prev", [P, TILES, E])
        top = m.sb("top", [P, TILES, TOPK])
        top_e = m.sb("top_e", [P, TILES, TOPK])
        toph = m.sb("toph", [P, 2, TILES, TOPK], F16)
        posh = m.sb("posh", [P, CAP], F16)
        eh = m.sb("eh", [P, E], F16)
        at_pos = m.sb("at_pos", [P, TILES, TOPK, CAP], F16)
        at_e = m.sb("at_e", [P, TILES, TOPK, E], F16)
        tok_e = [m.sb(f"tok_e{u}", [P, TOPK, E], F16) for u in range(2)]
        idv = m.sb("idv", [CAP, E])
        ide = m.sb("ide", [CAP, E])
        s16 = m.sb("s16", [P, TILES])
        id_ps = m.ps("id_ps", [CAP, E])
        xT_ps = [m.ps(f"xT_ps{k}", [P, CH]) for k in range(2)]
        pos_ps = xT_ps
        r_ps = m.ps("r_ps", [P, QT, E])
        g_ps = m.ps("g_ps", [I1, CH])
        u_ps = m.ps("u_ps", [I1, CH])
        o_ps = [m.ps(f"o_ps{u}", [P, 512]) for u in range(2)]
        chain = m.sem("chain")
        selected = m.sem("selected")
        gated = m.sem("gated")
        counted = m.sem("counted")
        stored = m.sem("stored")
        zeroed = m.sem("zeroed")
        rw_done = m.sem("rw_done")
        rw_copied = m.sem("rw_copied")
        xn_ready = m.sem("xn_ready")
        xT_done = m.sem("xT_done")
        xT_copied = m.sem("xT_copied")
        r_done = m.sem("r_done")
        sig = m.sem("sig")
        g_done = m.sem("g_done")
        g_silu = m.sem("g_silu")
        u_done = m.sem("u_done")
        u_copied = m.sem("u_copied")
        hid = m.sem("hid")
        o_done = m.sem("o_done")
        o_copied = m.sem("o_copied")
        x_added = m.sem("x_added")
        hot = m.sem("hot")
        tok_ready = m.sem("tok_ready")
        listed = m.sem("listed")

        with nc.Block() as block:
            @block.sync
            def _(sp):
                sp.wait_ge(zeroed, 1)
                sp.dma_start(acc_dram[1].rearrange("(n p) d -> p n d", p=P), zero[:, 0:D].unsqueeze(1).to_broadcast([P, ROWS // P, D])).then_inc(stored, 16)
                sp.dma_start(acc_dram[0][TOK:ROWS], zero[0:CAP, 0:D]).then_inc(stored, 16)
                sp.dma_start(xg_dram[TOK:ROWS], zero[0:CAP, :]).then_inc(stored, 16)
                rows = xg_dram[0:TOK].rearrange("(n p) w -> p n w", p=P)
                for c in range(CHUNKS):
                    sp.wait_ge(xn_ready, c + 1)
                    sp.dma_start(rows[:, QT * c:QT * c + QT, 0:D], xn[:, QT * c:QT * c + QT, :]).then_inc(stored, 16)
                for b in range(XB):
                    load_expert(sp, b, b)
                sp.wait_ge(x_added, TILES)
                sp.dma_start(acc_dram[0][0:TOK].rearrange("(n p) d -> p n d", p=P), x[:]).then_inc(stored, 16)
                sp.wait_ge(gated, 1)
                sp.dma_start(rows[:, :, D:XW], w2[:]).then_inc(stored, 16)
                sp.wait_ge(stored, 16 * (5 + CHUNKS))

            @block.gpsimd
            def _(pool):
                pool.memset(zero[:], 0.0).then_inc(zeroed, 1)

                def hidden(c):
                    pool.wait_ge(g_silu, c + 1)
                    pool.wait_ge(u_copied, c + 1)
                    wait(pool, o_done, QT * (c - 1))
                    pool.tensor_tensor(hl[c % 2][:], gl[c % 2][:], ul[c % 2][:], ALU.mult).then_inc(hid, 1)

                pool.wait_ge(xn_ready, CHUNKS)
                hidden(0)
                for c in range(CHUNKS):
                    if c + 1 < CHUNKS:
                        hidden(c + 1)
                    for t in range(QT * c, QT * c + QT):
                        pool.wait_ge(o_copied, t + 1)
                        pool.tensor_tensor(x[:, t, :], x[:, t, :], ol[t % 2][:], ALU.add).then_inc(x_added, 1)

            @block.scalar
            def _(act):
                std.scalar(act)

                def activations(c):
                    act.wait_ge(xT_done, c + 1)
                    for k in range(2):
                        last = act.copy(xT[:, k, CH * c:CH * c + CH], xT_ps[k][:])
                    last.then_inc(xT_copied, 1)

                def shared(c):
                    act.wait_ge(g_done, c + 1)
                    wait(act, hid, c - 1)
                    act.activation(gl[c % 2][:], g_ps[:], ACT.Silu).then_inc(g_silu, 1)
                    act.wait_ge(u_done, c + 1)
                    act.copy(ul[c % 2][:], u_ps[:]).then_inc(u_copied, 1)
                act.wait_ge(rw_done, 1)
                act.copy(rwT[:], r_ps[:, 0:2, :]).then_inc(rw_copied, 1)
                activations(0)
                for c in range(CHUNKS):
                    if c + 1 < CHUNKS:
                        activations(c + 1)
                    act.wait_ge(r_done, c + 1)
                    act.activation(scores[:, QT * c:QT * c + QT, :], r_ps[:], ACT.Sigmoid).then_inc(sig, 1)
                shared(0)
                for c in range(CHUNKS):
                    if c + 1 < CHUNKS:
                        shared(c + 1)
                    for t in range(QT * c, QT * c + QT):
                        act.wait_ge(o_done, t + 1)
                        wait(act, x_added, t - 1)
                        act.activation(ol[t % 2][:], o_ps[t % 2][:, 0:D], ACT.Copy, scale=gat[:, 3:4]).then_inc(o_copied, 1)
                for t in range(TILES):
                    act.wait_ge(hot, t + 1)
                    wait(act, listed, t - 1)
                    act.activation(tok_e[t % 2][:], at_e[:, t], ACT.Copy, scale=cst[:, C_TOK + t:C_TOK + t + 1]).then_inc(tok_ready, 1)

            @block.tensor
            def _(pe):
                def transposes(c):
                    pe.wait_ge(xn_ready, c + 1)
                    wait(pe, xT_copied, c)
                    for k in range(2):
                        for q in range(QT):
                            last = pe.transpose(xT_ps[k][:, P * q:P * q + P], xn[:, QT * c + q, P * k:P * k + P], ident)
                    last.then_inc(xT_done, 1)

                def logits(c):
                    pe.wait_ge(xT_copied, c + 1)
                    wait(pe, sig, c)
                    for q in range(QT):
                        col = CH * c + P * q
                        for k in range(2):
                            last = pe.matmul(r_ps[:, q, :], xT[:, k, col:col + P], rwT[:, k, :], start=(k == 0), stop=(k == 1))
                    last.then_inc(r_done, 1)

                def gate_up(c):
                    for w, ps, used, done in ((swg, g_ps, g_silu, g_done), (swu, u_ps, u_copied, u_done)):
                        wait(pe, used, c)
                        for k in range(2):
                            last = pe.matmul(ps[:], w[:, k, :], xT[:, k, CH * c:CH * c + CH], start=(k == 0), stop=(k == 1))
                        last.then_inc(done, 1)

                pe.wait_ge(sh_in, 80)
                for k in range(2):
                    last = pe.transpose(r_ps[:, k, :], rw[:, P * k:P * k + P], ident[0:E, 0:E])
                last.then_inc(rw_done, 1)
                transposes(0)
                pe.wait_ge(rw_copied, 1)
                for c in range(CHUNKS):
                    if c + 1 < CHUNKS:
                        transposes(c + 1)
                    logits(c)
                gate_up(0)
                for c in range(CHUNKS):
                    if c + 1 < CHUNKS:
                        gate_up(c + 1)
                    pe.wait_ge(hid, c + 1)
                    for q in range(QT):
                        t = QT * c + q
                        wait(pe, o_copied, t - 1)
                        pe.matmul(o_ps[t % 2][:, 0:D], hl[c % 2][:, P * q:P * q + P], swd[:], start=True, stop=True).then_inc(o_done, 1)
                pe.wait_ge(selected, 1)
                for k in range(2):
                    pe.matmul(pos_ps[k][:], cst[:, C_TRI:C_TRI + P], sel[:, 8 * k:8 * k + 8, :], start=True, stop=False)
                    last = pe.matmul(pos_ps[k][:], cst[:, C_ONES:C_ONES + P], prev[:, 8 * k:8 * k + 8, :], start=False, stop=True)
                last.then_inc(counted, 1)
                for t in range(TILES):
                    pe.wait_ge(tok_ready, t + 1)
                    for k in range(TOPK):
                        last = pe.matmul(id_ps[:], at_pos[:, t, k, :], tok_e[t % 2][:, k, :],
                                         start=(t == 0 and k == 0), stop=(t == TILES - 1 and k == TOPK - 1))
                    last.then_inc(listed, 1)

            @block.vector
            def _(dve):
                std.vector(dve, ln_mv, ln_rs)

                n_chain = [0]

                def link(ins):
                    n_chain[0] += 1
                    ins.then_inc(chain, 1)
                    dve.wait_ge(chain, n_chain[0])
                tt = dve.tensor_tensor
                for c in range(CHUNKS):
                    normalise_chunk(dve, c, x, ln_mv, ln_rs, xn[:, QT * c:QT * c + QT, :], xn_ready)
                dve.tensor_copy(posh[:], cst[:, C_POS:C_POS + CAP])
                dve.tensor_copy(eh[:], cst[:, C_EB:C_EB + E])
                dve.wait_ge(sh_in, 80)
                for c in range(CHUNKS):
                    dve.wait_ge(sig, c + 1)
                    part = slice(QT * c, QT * c + QT)
                    last = tt(biased[:, part, :], scores[:, part, :], bias[:].unsqueeze(1).to_broadcast([P, QT, E]), ALU.add)
                link(last)
                v = biased[:].rearrange("p t (g e) -> p (t g) e", g=NG)
                tt(hi[:], v[:, :, 0:4], v[:, :, 4:8], ALU.max)
                link(tt(lo[:], v[:, :, 0:4], v[:, :, 4:8], ALU.min))
                tt(hi2[:], hi[:, :, 0:2], hi[:, :, 2:4], ALU.max)
                tt(mi2[:], hi[:, :, 0:2], hi[:, :, 2:4], ALU.min)
                link(tt(lo2[:], lo[:, :, 0:2], lo[:, :, 2:4], ALU.max))
                link(tt(lo2[:], lo2[:], mi2[:], ALU.max))
                one = gs[:].rearrange("p t g -> p (t g)")
                two = g2[:].rearrange("p t g -> p (t g)")
                tt(one, hi2[:, :, 0], hi2[:, :, 1], ALU.max)
                tt(mi2[:, :, 0], hi2[:, :, 0], hi2[:, :, 1], ALU.min)
                link(tt(two, lo2[:, :, 0], lo2[:, :, 1], ALU.max))
                link(tt(two, two, mi2[:, :, 0], ALU.max))
                link(tt(one, one, two, ALU.add))
                mine = gs[:].unsqueeze(3).to_broadcast([P, TILES, NG, NG])
                other = gs[:].unsqueeze(2).to_broadcast([P, TILES, NG, NG])
                v1 = w1[:].rearrange("p t (g h) -> p t g h", g=NG)
                v2 = w2[:].rearrange("p t (g h) -> p t g h", g=NG)
                tt(v1, other, mine, ALU.is_gt)
                link(tt(v2, other, mine, ALU.is_equal))
                link(tt(w2[:], w2[:], cst[:, C_GT:C_GT + E].unsqueeze(1).to_broadcast([P, TILES, E]), ALU.mult))
                link(tt(w1[:], w1[:], w2[:], ALU.add))
                link(dve.tensor_reduce(g2[:], v1, AX.X, ALU.add))
                link(dve.tensor_scalar(g2[:], g2[:], float(TOPG), None, ALU.is_lt))
                link(tt(w1[:].rearrange("p t (g e) -> p (t g) e", g=NG), v,
                        g2[:].rearrange("p t g -> p (t g)").unsqueeze(2).to_broadcast([P, TILES * NG, E // NG]), ALU.mult))
                for t in range(TILES):
                    last = dve.max(top[:, t, :], w1[:, t, :])
                link(last)
                for t in range(TILES):
                    last = dve.match_replace(w2[:, t, :], top[:, t, :], w1[:, t, :], -3.0e38)
                link(last)
                link(tt(sel[:], w1[:], w2[:], ALU.not_equal))
                dve.memset(prev[:, 0, :], 0.0)
                link(dve.tensor_copy(prev[:, 1, :], sel[:, 0, :]))
                for t in range(2, TILES):
                    link(tt(prev[:, t, :], prev[:, t - 1, :], sel[:, t - 1, :], ALU.add))
                link(tt(w2[:], scores[:], sel[:], ALU.mult))
                dve.sem_inc(selected, 1)
                link(dve.tensor_reduce(s16[:], w2[:], AX.X, ALU.add))
                link(dve.tensor_scalar(s16[:], s16[:], 1e-20, None, ALU.add))
                link(dve.reciprocal(s16[:], s16[:]))
                link(dve.tensor_scalar(s16[:], s16[:], gat[:, 3:4], RSCALE, ALU.mult, ALU.mult))
                tt(w2[:], w2[:], s16[:].unsqueeze(2).to_broadcast([P, TILES, E]), ALU.mult).then_inc(gated, 1)
                dve.wait_ge(counted, 1)
                for k in range(2):
                    part = slice(8 * k, 8 * k + 8)
                    ps = pos_ps[k][:].rearrange("p (t e) -> p t e", e=E)
                    tt(w1[:, part, :], ps, cst[:, C_EB:C_EB + E].unsqueeze(1).to_broadcast([P, 8, E]), ALU.add)
                    link(dve.scalar_tensor_tensor(sel[:, part, :], ps, float(CAP), sel[:, part, :], ALU.is_lt, ALU.mult))
                link(tt(w1[:], w1[:], sel[:], ALU.mult))
                link(tt(sel[:], sel[:], cst[:, C_EB:C_EB + E].unsqueeze(1).to_broadcast([P, TILES, E]), ALU.mult))
                for t in range(TILES):
                    dve.max(top[:, t, :], w1[:, t, :])
                    last = dve.max(top_e[:, t, :], sel[:, t, :])
                link(last)
                link(tt(toph[:, 0], top[:], top_e[:], ALU.subtract))
                link(dve.tensor_copy(toph[:, 1], top_e[:]))
                for t in range(TILES):
                    tt(at_pos[:, t], posh[:].unsqueeze(1).to_broadcast([P, TOPK, CAP]),
                       toph[:, 0, t, :].unsqueeze(2).to_broadcast([P, TOPK, CAP]), ALU.is_equal)
                    tt(at_e[:, t], eh[:].unsqueeze(1).to_broadcast([P, TOPK, E]),
                       toph[:, 1, t, :].unsqueeze(2).to_broadcast([P, TOPK, E]), ALU.is_equal).then_inc(hot, 1)
                dve.wait_ge(listed, TILES)
                link(dve.tensor_scalar(ide[:], id_ps[:], 0.0, cst[:, C_PAD:C_PAD + 1], ALU.is_equal, ALU.mult))
                link(dve.scalar_tensor_tensor(idv[:], id_ps[:], -1.0, ide[:], ALU.add, ALU.add))
                link(dve.tensor_copy(idT[:], idv[:]))


def experts(nc, ident, xg_dram, acc_dram, idT, wg, wu, wd, weights, load_expert):
    ROUNDS = E // XB
    with ExitStack() as ctx:
        m = Mem(nc, ctx, "e")
        xg = [m.sb(f"xg{b}", [P, XW]) for b in range(XB)]
        ys = [m.sb(f"ys{b}", [P, D]) for b in range(NY)]
        xT = [m.sb(f"xT{u}", [P, 2, P]) for u in range(2)]
        sg = [m.sb(f"sg{u}", [I1, P]) for u in range(2)]
        ha = [m.sb(f"ha{u}", [I1, P]) for u in range(2)]
        hb = [m.sb(f"hb{u}", [I1, P]) for u in range(2)]
        xT_ps = [m.ps(f"xT_ps{u}", [P, 2, P]) for u in range(2)]
        gu_ps = [m.ps(f"gu_ps{u}", [I1, 2, P]) for u in range(2)]
        y_ps = [m.ps(f"y_ps{u}", [P, D]) for u in range(2)]

        gathered = [m.sem(f"gathered{b}") for b in range(XB)]
        summed = [m.sem(f"summed{u}") for u in range(2)]
        xT_done = m.sem("xT_done")
        xT_copied = m.sem("xT_copied")
        gu_done = m.sem("gu_done")
        sig = m.sem("sig")
        hid = m.sem("hid")
        y_done = m.sem("y_done")
        y_out = m.sem("y_out")

        def over_experts(eng, step):
            for b in range(XB):
                step(b, 0, b)
            with eng.Fori(1, ROUNDS - 1) as r:
                for b in range(XB):
                    step(XB * r + b, r, b)
            for b in range(XB):
                step(E - XB + b, ROUNDS - 1, b)

        with nc.Block() as block:
            @block.gpsimd
            def _(pool):
                for n in range(E + LEAD):
                    if n < E:
                        wait(pool, y_out, n - XB + 1)
                        pool.indirect_dma_start(out=xg[n % XB][:], out_offset=None, in_=xg_dram,
                                                in_offset=bass.IndirectOffsetOnAxis(ap=idT[:, n:n + 1], axis=0),
                                                bounds_check=ROWS - 1, oob_is_err=True).then_inc(gathered[n % XB], 16)
                    if n >= LEAD:
                        e = n - LEAD
                        pool.wait_ge(y_out, e + 1)
                        wait(pool, summed[e % 2], 16 * (e // 2))
                        pool.indirect_dma_start(out=acc_dram[e % 2],
                                                out_offset=bass.IndirectOffsetOnAxis(ap=idT[:, e:e + 1], axis=0),
                                                in_=ys[e % NY][:], in_offset=None, bounds_check=ROWS - 1, oob_is_err=True,
                                                compute_op=ALU.add).then_inc(summed[e % 2], 16)
                for u in range(2):
                    pool.wait_ge(summed[u], 16 * E // 2)

            @block.sync
            def _(sp):
                def step(e, r, b):
                    if not isinstance(e, int) or e + XB < E:
                        sp.wait_ge(y_done, e + 1)
                        load_expert(sp, e + XB, b)
                over_experts(sp, step)

            @block.scalar
            def _(act):
                def step(e, r, b):
                    u = b % 2
                    act.wait_ge(xT_done, e + 1)
                    wait(act, gu_done, e - 1)
                    act.copy(xT[u][:], xT_ps[u][:]).then_inc(xT_copied, 1)
                    act.wait_ge(gu_done, e + 1)
                    wait(act, hid, 2 * e - 2)
                    act.activation(sg[u][:], gu_ps[u][:, 0, :], ACT.Sigmoid).then_inc(sig, 1)
                over_experts(act, step)

            @block.vector
            def _(dve):
                def leave(e, r, b):
                    dve.wait_ge(y_done, e + 1)
                    wait(dve, summed[b % 2], 8 * (e - b % 2) - 8 * NY + 16)
                    dve.tensor_scalar(ys[b % NY][:], y_ps[b % 2][:], xg[b][:, bass.ds(D + e, 1)], None, ALU.mult).then_inc(y_out, 1)

                def step(e, r, b):
                    u = b % 2
                    dve.wait_ge(sig, e + 1)
                    wait(dve, hid, 2 * e - 2)
                    dve.tensor_tensor(ha[u][:], sg[u][:], gu_ps[u][:, 0, :], ALU.mult).then_inc(hid, 1)
                    dve.wait_ge(hid, 2 * e + 1)
                    wait(dve, y_done, e - 1)
                    dve.tensor_tensor(hb[u][:], ha[u][:], gu_ps[u][:, 1, :], ALU.mult).then_inc(hid, 1)
                    if b:
                        leave(e - 1, r, b - 1)
                    elif not isinstance(e, int) or e > 0:
                        leave(e - 1, r - 1, XB - 1)
                over_experts(dve, step)
                leave(E - 1, ROUNDS - 1, XB - 1)

            @block.tensor
            def _(pe):
                def rows(e, r, b):
                    pe.wait_ge(gathered[b], 16 * (r + 1))
                    wait(pe, xT_copied, e - 1)
                    for k in range(2):
                        last = pe.transpose(xT_ps[b % 2][:, k, :], xg[b][:, P * k:P * k + P], ident)
                    last.then_inc(xT_done, 1)

                def down(e, b):
                    pe.wait_ge(hid, 2 * e + 2)
                    wait(pe, y_out, e - 1)
                    pe.matmul(y_ps[b % 2][:], hb[b % 2][:], wd[b][:], start=True, stop=True).then_inc(y_done, 1)

                def step(e, r, b):
                    u = b % 2
                    if b + 1 < XB:
                        rows(e + 1, r, b + 1)
                    elif not isinstance(e, int) or e + 1 < E:
                        rows(e + 1, r + 1, 0)
                    pe.wait_ge(xT_copied, e + 1)
                    pe.wait_ge(weights[b], 48 * (r + 1))
                    wait(pe, hid, 2 * e - 2)
                    for n, w in enumerate((wg, wu)):
                        for k in range(2):
                            last = pe.matmul(gu_ps[u][:, n, :], w[b][:, k, :], xT[u][:, k, :], start=(k == 0), stop=(k == 1))
                    last.then_inc(gu_done, 1)
                    if not isinstance(e, int) or e > 0:
                        down(e - 1, (b - 1) % XB)
                rows(0, 0, 0)
                over_experts(pe, step)
                down(E - 1, XB - 1)


def total(nc, out, acc_dram):
    with ExitStack() as ctx:
        m = Mem(nc, ctx, "f")
        part = [m.sb(f"part{u}", [P, TILES, D]) for u in range(2)]
        loaded = [m.sem(f"loaded{c}") for c in range(CHUNKS)]
        summed = m.sem("summed")
        stored = m.sem("stored")
        rows = out.rearrange("b s d -> (b s) d").rearrange("(n p) d -> p n d", p=P)
        with nc.Block() as block:
            def load(eng, u):
                for c in range(CHUNKS):
                    n = slice(QT * c, QT * c + QT)
                    eng.dma_start(part[u][:, n], acc_dram[u][0:TOK].rearrange("(n p) d -> p n d", p=P)[:, n]).then_inc(loaded[c], 16)

            @block.sync
            def _(sp):
                load(sp, 0)
                for c in range(CHUNKS):
                    n = slice(QT * c, QT * c + QT)
                    sp.wait_ge(summed, c + 1)
                    sp.dma_start(rows[:, n], part[0][:, n]).then_inc(stored, 16)
                sp.wait_ge(stored, 16 * CHUNKS)

            @block.scalar
            def _(act):
                load(act, 1)

            @block.vector
            def _(dve):
                for c in range(CHUNKS):
                    n = slice(QT * c, QT * c + QT)
                    dve.wait_ge(loaded[c], 32)
                    dve.tensor_tensor(part[0][:, n], part[0][:, n], part[1][:, n], ALU.add).then_inc(summed, 1)


_INS = ['x', 'ctx_512', 'g_xattn', 'g_ffn', 'L0_ffn_W_up', 'L0_ffn_W_gate', 'L0_ffn_W_down', 'L1_xattn_Wq', 'L1_xattn_w_kc_q',
        'L1_xattn_w_kc_kv', 'L1_xattn_W_qr', 'L1_xattn_W_kr', 'L1_xattn_Wo', 'L1_ffn_router_weight', 'L1_ffn_e_bias',
        'L1_ffn_w_gate', 'L1_ffn_w_up', 'L1_ffn_w_down', 'L1_ffn_sh_gate', 'L1_ffn_sh_up', 'L1_ffn_sh_down']


def kernel(**inputs):
    import concourse.bacc as bacc
    from concourse.bass_utils import run_bass_kernel_spmd as run

    nc = bacc.Bacc("TRN2", target_bir_lowering=False, num_devices=1)
    arrays = {f"in_{name}": np.ascontiguousarray(inputs[name]) for name in _INS}
    arrays["in_consts"] = constants()
    arrays["in_key_ones"] = key_ones()
    a = {name[3:]: nc.dram_tensor(name, v.shape, mybir.dt.from_np(v.dtype), kind="ExternalInput").ap() for name, v in arrays.items()}
    out = nc.dram_tensor("out_0", (B, S, D), F32, kind="ExternalOutput").ap()
    xg_dram = nc.dram_tensor("xg_dram", (ROWS, XW), F32, kind="Internal").ap()
    acc_dram = [nc.dram_tensor(f"acc{u}_dram", (ROWS, D), F32, kind="Internal").ap() for u in range(2)]
    program(nc, a, out, xg_dram, acc_dram)
    r = run(nc, [arrays], core_ids=[0])
    return r.results[0]["out_0"]
```
